# Optimizing a Trainium2 kernel written in Bass

```python
import numpy as np
import jax
import jax.numpy as jnp

def _softmax(x, axis=-1):
    return jax.nn.softmax(x, axis=axis)

def _gelu(x):
    return jax.nn.gelu(x, approximate=True)

def _silu(x):
    return jax.nn.silu(x)

def _sigmoid(x):
    return jax.nn.sigmoid(x)

def _layernorm(x, axis=-1, eps=1e-05):
    m = jnp.mean(x, axis=axis, keepdims=True)
    v = jnp.var(x, axis=axis, keepdims=True)
    return (x - m) / jnp.sqrt(v + eps)

def _scatter_add(tgt, idx, src, axis=0):
    return tgt.at[idx].add(src)

def _segment_sum(src, seg, n):
    return jax.ops.segment_sum(src, seg, n)
kernel_name = 'mk_conv_attn_hybrid_d4_conv_nchw512_r4_017889'

def setup_inputs(seed: int=0):
    np.random.seed(seed)
    _w = jnp.asarray

    def _rec_inputs():
        import jax
        import jax.numpy as jnp
        _gk = jax.random.key(seed)
        x = -0.0003929 + 0.9999 * jax.random.normal(jax.random.fold_in(_gk, 1), (8, 128, 16, 16), jnp.float32)
        return x
    x = _rec_inputs()

    def _L0_conv_setup():
        import jax, jax.numpy as jnp
        import numpy as np
        B, C, H, W = (8, 128, 16, 16)
        KD, VD, OD = (16, 128, 128)
        BN_EPS = 1e-05
        key = jax.random.key(seed)
        ks = jax.random.split(key, 10)
        s = lambda fan_in: 1.0 / np.sqrt(fan_in)
        return {'x': jax.random.normal(ks[0], (B, C, H, W), jnp.float32), 'Wq': jax.random.normal(ks[1], (KD, C), jnp.float32) * s(C), 'bq': jnp.zeros((KD,), jnp.float32), 'Wk': jax.random.normal(ks[2], (KD, C), jnp.float32) * s(C), 'bk': jnp.zeros((KD,), jnp.float32), 'Wv': jax.random.normal(ks[3], (VD, C), jnp.float32) * s(C), 'bv': jnp.zeros((VD,), jnp.float32), 'gamma': jnp.zeros((1,), jnp.float32), 'Wf': jax.random.normal(ks[4], (OD, VD), jnp.float32) * s(VD), 'bn_w': jnp.ones((OD,), jnp.float32), 'bn_b': jnp.zeros((OD,), jnp.float32), 'bn_mean': jnp.zeros((OD,), jnp.float32), 'bn_var': jnp.ones((OD,), jnp.float32)}
    _L0_conv_all = _L0_conv_setup()
    _L0_conv_in = {k: v for k, v in _L0_conv_all.items() if k in ('Wq', 'bq', 'Wk', 'bk', 'Wv', 'bv', 'gamma', 'Wf', 'bn_w', 'bn_b', 'bn_mean', 'bn_var')}
    del _L0_conv_all

    def _L1_conv_setup():
        import jax, jax.numpy as jnp
        import numpy as np
        C_IN = 128
        OUT_CH = 64
        DIM = 16
        key = jax.random.key(seed)
        ks = jax.random.split(key, 11)
        b, c, h, w = (16, C_IN, 16, 16)

        def winit(k, o, i):
            s = 1.0 / np.sqrt(i)
            return jax.random.uniform(k, (o, i), jnp.float32, -s, s)
        return {'x': jax.random.normal(ks[0], (b, c, h, w), jnp.float32), 'Wq': winit(ks[1], OUT_CH, C_IN), 'bq': winit(ks[2], OUT_CH, C_IN)[:, 0], 'Wk': winit(ks[3], OUT_CH, C_IN), 'bk': winit(ks[4], OUT_CH, C_IN)[:, 0], 'Wv': winit(ks[5], C_IN, C_IN), 'bv': winit(ks[6], C_IN, C_IN)[:, 0], 'Ws': winit(ks[7], DIM, C_IN), 'bs': winit(ks[8], DIM, C_IN)[:, 0], 'We': winit(ks[9], DIM, C_IN), 'be': winit(ks[10], DIM, C_IN)[:, 0]}
    _L1_conv_all = _L1_conv_setup()
    _L1_conv_in = {k: v for k, v in _L1_conv_all.items() if k in ('Wq', 'bq', 'Wk', 'bk', 'Wv', 'bv', 'Ws', 'bs', 'We', 'be')}
    del _L1_conv_all

    def _L2_attn_setup():
        import jax, jax.numpy as jnp
        import numpy as np
        T, B, E, H = (512, 4, 128, 8)
        HD = E // H

        def _rotate_half(x):
            x1, x2 = jnp.split(x, 2, axis=-1)
            return jnp.concatenate([-x2, x1], axis=-1)
        key = jax.random.key(seed)
        ks = jax.random.split(key, 9)
        s = 0.05
        return {'query': jax.random.normal(ks[0], (T, B, E), jnp.float32), 'Wq': jax.random.normal(ks[1], (E, E), jnp.float32) * s, 'bq': jax.random.normal(ks[2], (E,), jnp.float32) * s, 'Wk': jax.random.normal(ks[3], (E, E), jnp.float32) * s, 'bk': jax.random.normal(ks[4], (E,), jnp.float32) * s, 'Wv': jax.random.normal(ks[5], (E, E), jnp.float32) * s, 'bv': jax.random.normal(ks[6], (E,), jnp.float32) * s, 'Wo': jax.random.normal(ks[7], (E, E), jnp.float32) * s, 'bo': jax.random.normal(ks[8], (E,), jnp.float32) * s}
    _L2_attn_all = _L2_attn_setup()
    _L2_attn_in = {k: v for k, v in _L2_attn_all.items() if k in ('Wq', 'bq', 'Wk', 'bk', 'Wv', 'bv', 'Wo', 'bo')}
    del _L2_attn_all

    def _L2_ffn_setup():
        import jax, jax.numpy as jnp
        import numpy as np
        TOP_K = 2
        key = jax.random.key(seed)
        ks = jax.random.split(key, 4)
        B, S, D, H, E = (2, 1024, 128, 512, 8)
        scale_in = 1.0 / np.sqrt(D)
        scale_h = 1.0 / np.sqrt(H)
        return {'x': jax.random.normal(ks[0], (B, S, D), dtype=jnp.float32), 'gate_w': jax.random.normal(ks[1], (D, E), dtype=jnp.float32) * scale_in, 'gate_b': jnp.zeros((E,), dtype=jnp.float32), 'w1': jax.random.normal(ks[2], (E, D, H), dtype=jnp.float32) * scale_in, 'b1': jnp.zeros((E, H), dtype=jnp.float32), 'w2': jax.random.normal(ks[3], (E, H, D), dtype=jnp.float32) * scale_h, 'b2': jnp.zeros((E, D), dtype=jnp.float32)}
    _L2_ffn_all = _L2_ffn_setup()
    _L2_ffn_in = {k: v for k, v in _L2_ffn_all.items() if k in ('gate_w', 'gate_b', 'w1', 'b1', 'w2', 'b2')}
    del _L2_ffn_all

    def _L3_attn_setup():
        import jax, jax.numpy as jnp
        import numpy as np
        HEADS = 8
        DIM_HEAD = 16
        key = jax.random.key(seed)
        ks = jax.random.split(key, 4)
        B, S, D = (4, 512, 128)
        inner = HEADS * DIM_HEAD
        hidden_states = jax.random.normal(ks[0], (B, S, D), dtype=jnp.float32)
        Wq = jax.random.normal(ks[1], (D, inner), dtype=jnp.float32) / np.sqrt(D)
        Wkv = jax.random.normal(ks[2], (D, 2 * inner), dtype=jnp.float32) / np.sqrt(D)
        Wo = jax.random.normal(ks[3], (inner, D), dtype=jnp.float32) / np.sqrt(inner)
        bo = jnp.zeros((D,), dtype=jnp.float32)
        return {'hidden_states': hidden_states, 'Wq': Wq, 'Wkv': Wkv, 'Wo': Wo, 'bo': bo}
    _L3_attn_all = _L3_attn_setup()
    _L3_attn_in = {k: v for k, v in _L3_attn_all.items() if k in ('Wq', 'Wkv', 'Wo', 'bo')}
    del _L3_attn_all

    def _L3_ffn_setup():
        import jax, jax.numpy as jnp
        import numpy as np
        TOP_K = 2
        key = jax.random.key(seed)
        k0, k1, k2, k3, k4 = jax.random.split(key, 5)
        B, S, D, F, E = (1, 512, 128, 256, 8)
        scale = 0.02
        hidden_states = jax.random.normal(k0, (B, S, D), dtype=jnp.float32)
        router_w = jax.random.normal(k1, (D, E), dtype=jnp.float32) * scale
        w1 = jax.random.normal(k2, (E, D, F), dtype=jnp.float32) * scale
        w2 = jax.random.normal(k3, (E, F, D), dtype=jnp.float32) * scale
        w3 = jax.random.normal(k4, (E, D, F), dtype=jnp.float32) * scale
        return {'hidden_states': hidden_states, 'router_w': router_w, 'w1': w1, 'w2': w2, 'w3': w3}
    _L3_ffn_all = _L3_ffn_setup()
    _L3_ffn_in = {k: v for k, v in _L3_ffn_all.items() if k in ('router_w', 'w1', 'w2', 'w3')}
    del _L3_ffn_all
    return {'x': x, 'L0_conv_Wq': _L0_conv_in['Wq'], 'L0_conv_bq': _L0_conv_in['bq'], 'L0_conv_Wk': _L0_conv_in['Wk'], 'L0_conv_bk': _L0_conv_in['bk'], 'L0_conv_Wv': _L0_conv_in['Wv'], 'L0_conv_bv': _L0_conv_in['bv'], 'L0_conv_gamma': _L0_conv_in['gamma'], 'L0_conv_Wf': _L0_conv_in['Wf'], 'L0_conv_bn_w': _L0_conv_in['bn_w'], 'L0_conv_bn_b': _L0_conv_in['bn_b'], 'L0_conv_bn_mean': _L0_conv_in['bn_mean'], 'L0_conv_bn_var': _L0_conv_in['bn_var'], 'L1_conv_Wq': _L1_conv_in['Wq'], 'L1_conv_bq': _L1_conv_in['bq'], 'L1_conv_Wk': _L1_conv_in['Wk'], 'L1_conv_bk': _L1_conv_in['bk'], 'L1_conv_Wv': _L1_conv_in['Wv'], 'L1_conv_bv': _L1_conv_in['bv'], 'L1_conv_Ws': _L1_conv_in['Ws'], 'L1_conv_bs': _L1_conv_in['bs'], 'L1_conv_We': _L1_conv_in['We'], 'L1_conv_be': _L1_conv_in['be'], 'L2_attn_Wq': _L2_attn_in['Wq'], 'L2_attn_bq': _L2_attn_in['bq'], 'L2_attn_Wk': _L2_attn_in['Wk'], 'L2_attn_bk': _L2_attn_in['bk'], 'L2_attn_Wv': _L2_attn_in['Wv'], 'L2_attn_bv': _L2_attn_in['bv'], 'L2_attn_Wo': _L2_attn_in['Wo'], 'L2_attn_bo': _L2_attn_in['bo'], 'L2_ffn_gate_w': _L2_ffn_in['gate_w'], 'L2_ffn_gate_b': _L2_ffn_in['gate_b'], 'L2_ffn_w1': _L2_ffn_in['w1'], 'L2_ffn_b1': _L2_ffn_in['b1'], 'L2_ffn_w2': _L2_ffn_in['w2'], 'L2_ffn_b2': _L2_ffn_in['b2'], 'L3_attn_Wq': _L3_attn_in['Wq'], 'L3_attn_Wkv': _L3_attn_in['Wkv'], 'L3_attn_Wo': _L3_attn_in['Wo'], 'L3_attn_bo': _L3_attn_in['bo'], 'L3_ffn_router_w': _L3_ffn_in['router_w'], 'L3_ffn_w1': _L3_ffn_in['w1'], 'L3_ffn_w2': _L3_ffn_in['w2'], 'L3_ffn_w3': _L3_ffn_in['w3']}

def reference(x, L0_conv_Wq, L0_conv_bq, L0_conv_Wk, L0_conv_bk, L0_conv_Wv, L0_conv_bv, L0_conv_gamma, L0_conv_Wf, L0_conv_bn_w, L0_conv_bn_b, L0_conv_bn_mean, L0_conv_bn_var, L1_conv_Wq, L1_conv_bq, L1_conv_Wk, L1_conv_bk, L1_conv_Wv, L1_conv_bv, L1_conv_Ws, L1_conv_bs, L1_conv_We, L1_conv_be, L2_attn_Wq, L2_attn_bq, L2_attn_Wk, L2_attn_bk, L2_attn_Wv, L2_attn_bv, L2_attn_Wo, L2_attn_bo, L2_ffn_gate_w, L2_ffn_gate_b, L2_ffn_w1, L2_ffn_b1, L2_ffn_w2, L2_ffn_b2, L3_attn_Wq, L3_attn_Wkv, L3_attn_Wo, L3_attn_bo, L3_ffn_router_w, L3_ffn_w1, L3_ffn_w2, L3_ffn_w3):
    import jax
    import jax.numpy as jnp

    def _L0_conv_ref(x, Wq, bq, Wk, bk, Wv, bv, gamma, Wf, bn_w, bn_b, bn_mean, bn_var):
        import jax, jax.numpy as jnp
        import numpy as np
        B, C, H, W = (8, 128, 16, 16)
        KD, VD, OD = (16, 128, 128)
        BN_EPS = 1e-05
        b, c, h, w = x.shape
        n = h * w
        q = jnp.einsum('bchw,kc->bkhw', x, Wq) + bq[None, :, None, None]
        k = jnp.einsum('bchw,kc->bkhw', x, Wk) + bk[None, :, None, None]
        v = jnp.einsum('bchw,vc->bvhw', x, Wv) + bv[None, :, None, None]
        q = q.reshape(b, -1, n)
        k = k.reshape(b, -1, n)
        v = v.reshape(b, -1, n)
        energy = jnp.einsum('bki,bkj->bij', q, k)
        attention = jax.nn.softmax(energy, axis=-1)
        out = jnp.einsum('bvj,bij->bvi', v, attention)
        out = out.reshape(b, c, h, w)
        out = gamma * out + x
        fused = jnp.einsum('bchw,oc->bohw', out, Wf)
        inv = jax.lax.rsqrt(bn_var + BN_EPS)
        fused = (fused - bn_mean[None, :, None, None]) * (bn_w * inv)[None, :, None, None] + bn_b[None, :, None, None]
        return jax.nn.relu(fused)

    def _L1_conv_ref(x, Wq, bq, Wk, bk, Wv, bv, Ws, bs, We, be):
        import jax, jax.numpy as jnp
        import numpy as np
        C_IN = 128
        OUT_CH = 64
        DIM = 16
        b, c, h, w = x.shape
        n = h * w
        xf = x.reshape(b, c, n)
        Q = jnp.einsum('oc,bcn->bon', Wq, xf) + bq[:, None]
        K = jnp.einsum('oc,bcn->bon', Wk, xf) + bk[:, None]
        gate = jax.nn.sigmoid(jnp.mean(Q * K, axis=1, keepdims=True))
        V = jnp.einsum('oc,bcn->bon', Wv, xf) + bv[:, None]
        V_dw = V * gate
        Qs = jnp.einsum('oc,bcn->bon', Ws, xf) + bs[:, None]
        Ke = jnp.einsum('oc,bcn->bon', We, xf) + be[:, None]
        energy = jnp.einsum('bcn,bdn->bcd', V_dw, Qs)
        attention = jax.nn.softmax(energy, axis=-1)
        Vout = jnp.einsum('bcd,bdn->bcn', attention, Ke)
        return x + Vout.reshape(b, c, h, w)

    def _L2_attn_ref(query, Wq, bq, Wk, bk, Wv, bv, Wo, bo):
        import jax, jax.numpy as jnp
        import numpy as np
        T, B, E, H = (512, 4, 128, 8)
        HD = E // H

        def _rotate_half(x):
            x1, x2 = jnp.split(x, 2, axis=-1)
            return jnp.concatenate([-x2, x1], axis=-1)
        t_len, bsz, e = query.shape
        scaling = HD ** (-0.5)
        q = (query @ Wq.T + bq) * scaling
        k = query @ Wk.T + bk
        v = query @ Wv.T + bv
        split = lambda x: x.reshape(t_len, bsz * H, HD).transpose(1, 0, 2)
        q, k, v = (split(q), split(k), split(v))
        inv_freq = 1.0 / 10000.0 ** (jnp.arange(0, HD, 2, dtype=jnp.float32) / HD)
        t = jnp.arange(t_len, dtype=jnp.float32)
        freqs = t[:, None] * inv_freq[None, :]
        emb = jnp.concatenate([freqs, freqs], axis=-1)
        cos, sin = (jnp.cos(emb)[None], jnp.sin(emb)[None])
        q = q * cos + _rotate_half(q) * sin
        k = k * cos + _rotate_half(k) * sin
        scores = jnp.einsum('bqd,bkd->bqk', q, k)
        w = jax.nn.softmax(scores.astype(jnp.float32), axis=-1).astype(query.dtype)
        attn = jnp.einsum('bqk,bkd->bqd', w, v)
        attn = attn.transpose(1, 0, 2).reshape(t_len, bsz, e)
        return attn @ Wo.T + bo

    def _L2_ffn_ref(x, gate_w, gate_b, w1, b1, w2, b2):
        import jax, jax.numpy as jnp
        import numpy as np
        TOP_K = 2
        B, S, D = x.shape
        E = gate_w.shape[1]
        flat_x = x.reshape(-1, D)
        gate_logits = flat_x @ gate_w + gate_b
        raw_weights = jax.nn.softmax(gate_logits, axis=-1)
        top_w, top_idx = jax.lax.top_k(raw_weights, TOP_K)
        one_hot = jax.nn.one_hot(top_idx, E, dtype=flat_x.dtype)
        gate_output = (one_hot * top_w[..., None]).sum(axis=-2)
        h = jax.nn.gelu(jnp.einsum('td,edh->teh', flat_x, w1) + b1, approximate=False)
        expert_out = jnp.einsum('teh,ehd->ted', h, w2) + b2
        combined = jnp.einsum('ted,te->td', expert_out, gate_output)
        return combined.reshape(B, S, -1)

    def _L3_attn_ref(hidden_states, Wq, Wkv, Wo, bo):
        import jax, jax.numpy as jnp
        import numpy as np
        HEADS = 8
        DIM_HEAD = 16
        B, S, D = hidden_states.shape
        H, dh = (HEADS, DIM_HEAD)
        q = hidden_states @ Wq
        kv = hidden_states @ Wkv
        k, v = jnp.split(kv, 2, axis=-1)
        q = q.reshape(B, S, H, dh)
        k = k.reshape(B, S, H, dh)
        v = v.reshape(B, S, H, dh)
        scale = (1.0 / jnp.sqrt(jnp.float32(dh))).astype(jnp.bfloat16).astype(jnp.float32)
        scores = jnp.einsum('bqhd,bkhd->bhqk', q * scale, k).astype(jnp.bfloat16)
        probs = jax.nn.softmax(scores, axis=-1)
        out = jnp.einsum('bhqk,bkhd->bqhd', probs.astype(jnp.float32), v)
        out = out.astype(jnp.bfloat16)
        out = out.reshape(B, S, H * dh).astype(jnp.float32)
        return out @ Wo + bo

    def _L3_ffn_ref(hidden_states, router_w, w1, w2, w3):
        import jax, jax.numpy as jnp
        import numpy as np
        TOP_K = 2
        B, S, D = hidden_states.shape
        E = router_w.shape[1]
        x = hidden_states.reshape(-1, D)
        T = x.shape[0]
        router_logits = x @ router_w
        probs = jax.nn.softmax(router_logits.astype(jnp.float32), axis=-1)
        routing_weights, selected_experts = jax.lax.top_k(probs, TOP_K)
        routing_weights = routing_weights / routing_weights.sum(axis=-1, keepdims=True)
        routing_weights = routing_weights.astype(x.dtype)
        combine = jnp.zeros((T, E), dtype=x.dtype).at[jnp.arange(T)[:, None], selected_experts].add(routing_weights)
        gate = jax.nn.silu(jnp.einsum('td,edf->tef', x, w1))
        up = jnp.einsum('td,edf->tef', x, w3)
        h = gate * up * combine[:, :, None]
        out = jnp.einsum('tef,efd->td', h, w2)
        return out.reshape(B, S, D)

    def _gn(v, G=32, eps=1e-05):
        B_, C_, H_, W_ = v.shape
        g = v.reshape(B_, G, C_ // G, H_, W_)
        m = jnp.mean(g, axis=(2, 3, 4), keepdims=True)
        s = jnp.var(g, axis=(2, 3, 4), keepdims=True)
        return ((g - m) / jnp.sqrt(s + eps)).reshape(v.shape)

    def _ln_c(v, eps=1e-06):
        m = jnp.mean(v, axis=1, keepdims=True)
        s = jnp.var(v, axis=1, keepdims=True)
        return (v - m) / jnp.sqrt(s + eps)

    def _ln_t(v, eps=1e-05):
        m = jnp.mean(v, axis=-1, keepdims=True)
        s = jnp.var(v, axis=-1, keepdims=True)
        return (v - m) / jnp.sqrt(s + eps)

    def _to_tokens(v):
        B_, C_, H_, W_ = v.shape
        return v.reshape(B_, C_, H_ * W_).transpose(0, 2, 1)

    def _from_tokens(t, like):
        B_, C_, H_, W_ = like.shape
        return t.transpose(0, 2, 1).reshape(B_, C_, H_, W_)
    x = _L0_conv_ref(x, L0_conv_Wq, L0_conv_bq, L0_conv_Wk, L0_conv_bk, L0_conv_Wv, L0_conv_bv, L0_conv_gamma, L0_conv_Wf, L0_conv_bn_w, L0_conv_bn_b, L0_conv_bn_mean, L0_conv_bn_var)
    x = _L1_conv_ref(x, L1_conv_Wq, L1_conv_bq, L1_conv_Wk, L1_conv_bk, L1_conv_Wv, L1_conv_bv, L1_conv_Ws, L1_conv_bs, L1_conv_We, L1_conv_be)
    t = _to_tokens(x)
    t = t + _L2_attn_ref(_ln_t(t), L2_attn_Wq, L2_attn_bq, L2_attn_Wk, L2_attn_bk, L2_attn_Wv, L2_attn_bv, L2_attn_Wo, L2_attn_bo)
    t = t + _L2_ffn_ref(_ln_t(t), L2_ffn_gate_w, L2_ffn_gate_b, L2_ffn_w1, L2_ffn_b1, L2_ffn_w2, L2_ffn_b2)
    t = t + _L3_attn_ref(_ln_t(t), L3_attn_Wq, L3_attn_Wkv, L3_attn_Wo, L3_attn_bo)
    t = t + _L3_ffn_ref(_ln_t(t), L3_ffn_router_w, L3_ffn_w1, L3_ffn_w2, L3_ffn_w3)
    x = _from_tokens(t, x)
    return x

_drawn_inputs = setup_inputs


def setup_inputs(seed=0):
    import zlib

    import numpy as np

    out = dict(_drawn_inputs(seed))
    spreads = {'L0_conv_bq': (0.0, 0.1),
     'L0_conv_bk': (0.0, 0.1),
     'L0_conv_bv': (0.0, 0.1),
     'L0_conv_bn_w': (1.0, 0.2),
     'L0_conv_bn_b': (0.0, 0.1),
     'L0_conv_bn_mean': (0.0, 0.1),
     'L0_conv_bn_var': (1.0, 0.2),
     'L2_ffn_gate_b': (0.0, 0.1),
     'L2_ffn_b1': (0.0, 0.1),
     'L2_ffn_b2': (0.0, 0.1),
     'L3_attn_bo': (0.0, 0.1)}
    factors = {'L1_conv_Wq': 4.607,
     'L1_conv_bq': 8.0,
     'L1_conv_Wk': 4.347,
     'L1_conv_bk': 8.0,
     'L2_attn_bq': 4.619,
     'L2_attn_bk': 7.159,
     'L3_ffn_router_w': 8.0,
     'L3_ffn_w1': 8.0,
     'L3_ffn_w2': 8.0,
     'L3_ffn_w3': 8.0}
    for name, (base, spread) in spreads.items():
        noise = np.random.default_rng([zlib.crc32(name.encode()), seed]).standard_normal(out[name].shape)
        drawn = base * np.exp(spread * noise) if base else spread * noise
        out[name] = jnp.asarray(drawn.astype(out[name].dtype))
    for name, factor in factors.items():
        out[name] = (out[name] * factor).astype(out[name].dtype)
    return out
```

```python
from contextlib import ExitStack

import numpy as np

import concourse.bass as bass
from concourse import mybir

F32 = mybir.dt.float32
F32R = mybir.dt.float32r
BF16 = mybir.dt.bfloat16
ALU = mybir.AluOpType
ACT = mybir.ActivationFunctionType
AX = mybir.AxisListType

P = 128
B = 8
N = 256
S = N // P
T = B * N
H, DH = 8, 16
KD = 16
QK1 = 64
E = 8
TOPK = 2
F2 = 512
F3 = 256
CH = 512
NCH = T // CH
BLK = B * P
FREE_W = 2
FREE_ACC = 2
FREE_H = 3
FREE_Y = NCH + 1
BN_EPS = 1e-5
LN_EPS = 1e-5

PACK = [
    ("Wq0", KD), ("Wk0", KD), ("Wv0", P), ("Wf0", P), ("W1", 2 * QK1 + P + KD), ("We1", KD),
    ("Wqkv2", 3 * P), ("Wqk2r", 2 * P), ("Wo2", P), ("gate2", E),
    ("Wq3", 2 * P), ("Wk3", 2 * P), ("Wv3", P), ("Wo3", P), ("router3", E),
    ("ident", P), ("bv0", 1), ("bn_w", 1), ("bn_b", 1), ("bn_mean", 1), ("bn_var", 1),
    ("bq0", 1), ("bk0", 1), ("be1", 1), ("gamma", 1), ("kmask", 1),
    ("bias1", 2 * QK1 + P + KD), ("bqkv2", 3 * P), ("bqk2r", 2 * P), ("bo2", P), ("gateb2", E),
    ("bo3", P), ("cosq", B * DH), ("sinq", B * DH), ("cosk", B * DH), ("sink", B * DH),
    ("earlier", E * E),
]
AT = {}
_at = 0
for _name, _w in PACK:
    AT[_name] = (_at, _at + _w)
    _at += _w
NPACK = _at


class Chain:

    def __init__(self, engine, sem):
        self.engine, self.sem, self.base, self.n, self.total = engine, sem, None, 0, 0

    def done(self, ins):
        ins.then_inc(self.sem, 1)
        self.n += 1
        return ins

    def wait(self):
        if self.base is None:
            self.engine.wait_ge(self.sem, self.total + self.n)
        else:
            self.engine.wait_ge(self.sem, self.base + self.n)

    def loop(self, i, per):
        self.total += self.n
        self.base, self.n, self.per = i * per + self.total, 0, per

    def end(self, times):
        assert self.n == self.per, (self.n, self.per)
        self.total += times * self.per
        self.base, self.n = None, 0


def build(nc, a, out):
    ctx = ExitStack()
    with ctx:
        def sb(name, shape, dt=F32):
            return ctx.enter_context(nc.sbuf_tensor(name, shape, dt))

        def sem(name):
            return ctx.enter_context(nc.semaphore(name))

        ps = ctx.enter_context(nc.psum_tensor("ps", [P, 8, CH], F32))

        def psb(bank):
            return ps[:, bank, :].bitcast(BF16)

        w = sb("w", [P, NPACK])

        def wc(name, lo=0, hi=None, rows=P):
            x, y = AT[name]
            return w[0:rows, x + lo:(y if hi is None else x + hi)]

        ident = wc("ident")
        identb = sb("identb", [P, P], BF16)
        t = sb("t", [P, S, B, P])
        halfs = sb("halfs", [P, B])
        mu = sb("mu", [P, B])
        var = sb("var", [P, B])
        rstd = sb("rstd", [P, B])
        xc = sb("xc", [P, B, P])
        sq = sb("sq", [P, B, P])
        lnT = sb("lnT", [P, BLK])
        xH = sb("xH", [P, T], F32R)
        xL = sb("xL", [P, T], F32R)
        acc = sb("acc", [P, T])
        gd = nc.dram_tensor("gates_scratch", [2, E, T], F32, kind="Internal").ap()
        wb2 = sb("wb2", [P, B, 3 * P])
        bb2 = sb("bb2", [P, B, 3 * P])
        rtmp = sb("rtmp", [P, B, P])

        room = ExitStack()

        def own(name, shape, dt=F32):
            return room.enter_context(nc.sbuf_tensor(name, shape, dt))

        s_w, s_id = sem("packed_loaded"), sem("identb_ready")
        s_set_pe, s_set_v, s_set_p = sem("setup_pe"), sem("setup_dve"), sem("setup_pool")
        s_rot = sem("rotated_ready")
        dve_s, pool_s = sem("dve_steps"), sem("pool_steps")

        xs = own("xs", [P, CH])
        gM = own("gM", [P, P])
        bn_inv, bn_s, bn_t = (own(n, [P, 1]) for n in ("bn_inv", "bn_s", "bn_t"))
        q0 = own("q0", [KD, CH])
        k0 = own("k0", [KD, CH])
        vT0 = own("vT0", [P, 4, P])
        nm0 = own("nm0", [P, 4])
        sm0 = own("sm0", [P, 4])
        A0 = own("A0", [P, 4, N])
        AT0 = own("AT0", [P, 4, N])
        x1 = own("x1", [P, CH])
        pr1 = own("pr1", [P, 4, 272])
        ke1 = own("ke1", [KD, CH])
        qk1 = own("qk1", [P, 4, QK1])
        g1 = own("g1", [P, 4])
        vd1 = own("vd1", [P, 4, P])
        nm1 = own("nm1", [P, 2])
        sm1 = own("sm1", [P, 2])
        a1 = own("a1", [P, 2, KD])
        aT1 = own("aT1", [KD, 2, P])
        names = ("xs qkp qk0 vtp vt0 ep nm ex an atp at0a at0v fp x1 prp pr kep ke z ez vd e1p nm1 ex1 a1 "
                 "a1p aT1 tp tdone").split()
        m = {n: sem("l01_" + n) for n in names}
        block = room.enter_context(nc.Block())
        chv, chp = Chain(None, dve_s), Chain(None, pool_s)

        @block.sync
        def _(sp):
            sp.dma_start(w[:], a["pack"]).then_inc(s_w, 16)
            with sp.Fori(0, 4) as j:
                sp.wait_ge(m["fp"], j + 1)
                sp.dma_start(xs[:].rearrange("c (b n) -> c b n", b=2),
                             a["x"][bass.ds(2 * j, 2)].rearrange("b c n -> c b n")).then_inc(m["xs"], 16)

        @block.gpsimd
        def _(pool):
            chp.engine = pool
            chp.done(pool.memset(halfs[:], -0.5))
            pool.wait_ge(s_w, 16)
            chp.done(pool.tensor_scalar(bn_s[:], wc("bn_var"), BN_EPS, None, ALU.add))
            chp.wait()
            chp.done(pool.tensor_tensor(bn_inv[:], bn_s[:], halfs[:, 0:1], ALU.pow))
            chp.wait()
            pool.tensor_tensor(bn_s[:], wc("bn_w"), bn_inv[:], ALU.mult).then_inc(s_set_p, 1)
            for dst, plain, turned in ((wb2, "Wqkv2", "Wqk2r"), (bb2, "bqkv2", "bqk2r")):
                for i, (c_, s_) in enumerate((("cosq", "sinq"), ("cosk", "sink"))):
                    def heads(name):
                        return wc(name, i * P, (i + 1) * P).rearrange("p (h d) -> p h d", h=H)[:, None].to_broadcast([P, B, H, DH])

                    def angle(name):
                        return wc(name).rearrange("p (b d) -> p b d", b=B)[:, :, None].to_broadcast([P, B, H, DH])
                    o = dst[:, :, i * P:(i + 1) * P].rearrange("p b (h d) -> p b h d", h=H)
                    r = rtmp[:].rearrange("p b (h d) -> p b h d", h=H)
                    chp.done(pool.tensor_tensor(o, heads(plain), angle(c_), ALU.mult))
                    chp.done(pool.tensor_tensor(r, heads(turned), angle(s_), ALU.mult))
                    chp.wait()
                    chp.done(pool.tensor_tensor(o, o, r, ALU.add))
                    chp.wait()
                chp.done(pool.tensor_copy(dst[:, :, 2 * P:], wc(plain, 2 * P, 3 * P)[:, None].to_broadcast([P, B, P])))
            chp.wait()
            pool.memset(acc[:], 0.0).then_inc(s_rot, 1)

        @block.tensor
        def _(pe):
            pe.wait_ge(s_w, 16)
            pe.matmul(ps[:, 0, 0:P], wc("Wv0"), wc("Wf0"), start=True, stop=True)
            pe.matmul(ps[:, 0, P:P + 1], wc("Wf0"), wc("bv0"), start=True, stop=True).then_inc(s_set_pe, 1)
            pe.wait_ge(s_set_v, 2)
            pe.sem_inc(m["fp"], 1)
            with pe.Fori(0, 4) as j:
                pe.wait_ge(m["xs"], 16 * j + 16)
                pe.matmul(ps[0:KD, 0, :], wc("Wq0"), xs[:], start=True, stop=True)
                pe.matmul(ps[0:KD, 1, :], wc("Wk0"), xs[:], start=True, stop=True).then_inc(m["qkp"], 1)
                for i in range(4):
                    vt = pe.matmul(ps[:, 2, i * P:(i + 1) * P], xs[:, i * P:(i + 1) * P], gM[:], start=True, stop=True)
                vt.then_inc(m["vtp"], 1)
                pe.wait_ge(m["qk0"], 2 * j + 2)
                for b in range(2):
                    for i in range(2):
                        e = pe.matmul(ps[:, 3 + b, i * N:(i + 1) * N], q0[:, b * N + i * P:b * N + (i + 1) * P],
                                      k0[:, b * N:(b + 1) * N], start=True, stop=True)
                e.then_inc(m["ep"], 1)
                pe.wait_ge(m["an"], j + 1)
                for b in range(2):
                    for jt in range(2):
                        for i in range(2):
                            e = pe.transpose(ps[:, 5 + b, jt * N + i * P:jt * N + (i + 1) * P],
                                             A0[:, 2 * b + i, jt * P:(jt + 1) * P], ident)
                    e.then_inc(m["atp"], 1)
                pe.wait_ge(m["vt0"], j + 1)
                pe.wait_ge(m["at0a"], j + 1)
                pe.wait_ge(m["at0v"], j + 1)
                for b in range(2):
                    o = ps[:, 0, b * N:(b + 1) * N]
                    pe.matmul(o, wc("Wf0"), xs[:, b * N:(b + 1) * N], start=True, stop=False)
                    pe.matmul(o, vT0[:, 2 * b, :], AT0[:, 2 * b, :], start=False, stop=False)
                    f = pe.matmul(o, vT0[:, 2 * b + 1, :], AT0[:, 2 * b + 1, :], start=False, stop=True)
                f.then_inc(m["fp"], 1)
                pe.wait_ge(m["x1"], j + 1)
                for i in range(4):
                    f = pe.matmul(ps[:, 1 + i, 0:272], x1[:, i * P:(i + 1) * P], wc("W1"), start=True, stop=True)
                f.then_inc(m["prp"], 1)
                pe.matmul(ps[0:KD, 5, :], wc("We1"), x1[:], start=True, stop=True).then_inc(m["kep"], 1)
                pe.wait_ge(m["vd"], j + 1)
                for b in range(2):
                    for i in range(2):
                        f = pe.matmul(ps[:, 6, b * KD:(b + 1) * KD], vd1[:, 2 * b + i, :], pr1[:, 2 * b + i, 256:272],
                                      start=i == 0, stop=i == 1)
                f.then_inc(m["e1p"], 1)
                pe.wait_ge(m["a1"], j + 1)
                for b in range(2):
                    f = pe.transpose(ps[0:KD, 7, b * P:(b + 1) * P], a1[:, b, :], ident)
                f.then_inc(m["a1p"], 1)
                pe.wait_ge(m["aT1"], j + 1)
                pe.wait_ge(m["ke"], j + 1)
                for i in range(4):
                    o = ps[:, 0, i * P:(i + 1) * P]
                    pe.matmul(o, x1[:, i * P:(i + 1) * P], ident, start=True, stop=False)
                    f = pe.matmul(o, ke1[:, i * P:(i + 1) * P], aT1[:, i // 2, :], start=False, stop=True)
                f.then_inc(m["tp"], 1)
                pe.wait_ge(m["tdone"], j + 1)

        @block.scalar
        def _(act):
            act.wait_ge(s_set_v, 3)
            act.preload_act_table(ACT.Exp)
            with act.Fori(0, 4) as j:
                act.wait_ge(m["vtp"], j + 1)
                act.activation(vT0[:], ps[:, 2, :].rearrange("p (a b) -> p a b", a=4), ACT.Copy).then_inc(m["vt0"], 1)
                act.wait_ge(m["nm"], j + 1)
                for i in range(4):
                    act.activation(A0[:, i, :], ps[:, 3 + i // 2, (i % 2) * N:(i % 2 + 1) * N], ACT.Exp,
                                   bias=nm0[:, i:i + 1], accum_out=sm0[:, i:i + 1]).then_inc(m["ex"], 1)
                act.wait_ge(m["atp"], 2 * j + 1)
                act.activation(AT0[:, 0:2, :], ps[:, 5, :].rearrange("p (a b) -> p a b", a=2), ACT.Copy).then_inc(m["at0a"], 1)
                act.wait_ge(m["fp"], j + 2)
                act.activation(x1[:], ps[:, 0, :], ACT.Relu, bias=bn_t[:], scale=bn_s[:]).then_inc(m["x1"], 1)
                act.wait_ge(m["kep"], j + 1)
                act.activation(ke1[:], ps[0:KD, 5, :], ACT.Identity, bias=wc("be1", rows=KD)).then_inc(m["ke"], 1)
                act.wait_ge(m["z"], j + 1)
                act.activation(g1[:], g1[:], ACT.Exp, scale=-1.0 / QK1).then_inc(m["ez"], 1)
                act.wait_ge(m["nm1"], j + 1)
                for b in range(2):
                    act.activation(a1[:, b, :], ps[:, 6, b * KD:(b + 1) * KD], ACT.Exp, bias=nm1[:, b:b + 1],
                                   accum_out=sm1[:, b:b + 1]).then_inc(m["ex1"], 1)

        @block.vector
        def _(dve):
            chv.engine = dve
            dve.wait_ge(s_w, 16)
            dve.tensor_copy(identb[:], ident).then_inc(s_id, 1)
            dve.wait_ge(s_set_pe, 1)
            dve.tensor_scalar(gM[:], ps[:, 0, 0:P], wc("gamma"), None, ALU.mult).then_inc(s_set_v, 1)
            dve.tensor_scalar(bn_t[:], ps[:, 0, P:P + 1], wc("gamma"), wc("bn_mean"), ALU.mult, ALU.subtract).then_inc(s_set_v, 1)
            dve.wait_ge(s_set_p, 1)
            dve.wait_ge(s_set_v, 2)
            dve.tensor_scalar(bn_t[:], bn_t[:], bn_s[:], wc("bn_b"), ALU.mult, ALU.add).then_inc(s_set_v, 1)
            with dve.Fori(0, 4) as j:
                chv.loop(j, 5)
                dve.wait_ge(m["qkp"], j + 1)
                dve.tensor_scalar(q0[:], ps[0:KD, 0, :], wc("bq0", rows=KD), None, ALU.add).then_inc(m["qk0"], 1)
                dve.tensor_scalar(k0[:], ps[0:KD, 1, :], wc("bk0", rows=KD), None, ALU.add).then_inc(m["qk0"], 1)
                dve.wait_ge(m["ep"], j + 1)
                dve.tensor_reduce(nm0[:], ps[:, 3:5, :].rearrange("p a (i n) -> p (a i) n", i=2), AX.X, ALU.max,
                                  negate=True).then_inc(m["nm"], 1)
                dve.wait_ge(m["ex"], 4 * j + 4)
                chv.done(dve.reciprocal(sm0[:], sm0[:]))
                chv.wait()
                dve.tensor_tensor(A0[:], A0[:], sm0[:, :, None].to_broadcast([P, 4, N]), ALU.mult).then_inc(m["an"], 1)
                dve.wait_ge(m["atp"], 2 * j + 2)
                dve.tensor_copy(AT0[:, 2:4, :], ps[:, 6, :].rearrange("p (a b) -> p a b", a=2)).then_inc(m["at0v"], 1)
                dve.wait_ge(m["prp"], j + 1)
                dve.tensor_tensor(pr1[:], ps[:, 1:5, 0:272], wc("bias1")[:, None].to_broadcast([P, 4, 272]), ALU.add).then_inc(m["pr"], 1)
                dve.wait_ge(m["pr"], j + 1)
                chv.done(dve.tensor_tensor(qk1[:], pr1[:, :, 0:QK1], pr1[:, :, QK1:2 * QK1], ALU.mult))
                chv.wait()
                dve.tensor_reduce(g1[:], qk1[:], AX.X, ALU.add).then_inc(m["z"], 1)
                dve.wait_ge(m["ez"], j + 1)
                chv.done(dve.tensor_scalar(g1[:], g1[:], 1.0, None, ALU.add))
                chv.wait()
                chv.done(dve.reciprocal(g1[:], g1[:]))
                chv.wait()
                dve.tensor_tensor(vd1[:], pr1[:, :, 2 * QK1:2 * QK1 + P], g1[:, :, None].to_broadcast([P, 4, P]), ALU.mult).then_inc(m["vd"], 1)
                dve.wait_ge(m["e1p"], j + 1)
                dve.tensor_reduce(nm1[:], ps[:, 6, 0:2 * KD].rearrange("p (b k) -> p b k", b=2), AX.X, ALU.max,
                                  negate=True).then_inc(m["nm1"], 1)
                dve.wait_ge(m["ex1"], 2 * j + 2)
                chv.done(dve.reciprocal(sm1[:], sm1[:]))
                chv.wait()
                dve.tensor_tensor(a1[:], a1[:], sm1[:, :, None].to_broadcast([P, 2, KD]), ALU.mult).then_inc(m["a1"], 1)
                dve.wait_ge(m["a1p"], j + 1)
                dve.tensor_copy(aT1[:], ps[0:KD, 7, 0:2 * P].rearrange("p (b c) -> p b c", b=2)).then_inc(m["aT1"], 1)
                dve.wait_ge(m["tp"], j + 1)
                dve.tensor_copy(t[:, :, bass.ds(2 * j, 2), :].rearrange("p s b c -> p b s c"),
                                ps[:, 0, :].rearrange("p (b s c) -> p b s c", b=2, s=2)).then_inc(m["tdone"], 1)
            chv.end(4)

        room.close()
        qkv = own("qkv", [P, B, 3 * P])
        prod = own("prod", [P, B, P])
        sc2 = own("sc2", [P, B, B, H])
        mx2 = own("mx2", [P, B, H])
        o2 = own("o2", [P, B, P])
        oT2 = own("oT2", [P, BLK])
        ln = {n: sem("ln_" + n) for n in "cen sqr var rst nrm".split()}

        def ln_vector(dve, ch, s, n):
            ts = t[:, s]
            ch.done(dve.tensor_reduce(mu[:], ts, AX.X, ALU.add))
            ch.wait()
            ch.done(dve.tensor_scalar(mu[:], mu[:], 1.0 / P, None, ALU.mult))
            ch.wait()
            dve.tensor_tensor(xc[:], ts, mu[:, :, None].to_broadcast([P, B, P]), ALU.subtract).then_inc(ln["cen"], 1)
            dve.wait_ge(ln["sqr"], n + 1)
            ch.done(dve.tensor_reduce(var[:], sq[:], AX.X, ALU.add))
            ch.wait()
            dve.tensor_scalar(var[:], var[:], 1.0 / P, LN_EPS, ALU.mult, ALU.add).then_inc(ln["var"], 1)
            dve.wait_ge(ln["rst"], n + 1)
            dve.tensor_tensor(xc[:], xc[:], rstd[:, :, None].to_broadcast([P, B, P]), ALU.mult).then_inc(ln["nrm"], 1)

        def ln_scalar(act, n):
            act.wait_ge(ln["cen"], n + 1)
            act.activation(sq[:], xc[:], ACT.Square).then_inc(ln["sqr"], 1)

        def ln_pool(pool, n):
            pool.wait_ge(ln["var"], n + 1)
            pool.tensor_tensor(rstd[:], var[:], halfs[:], ALU.pow).then_inc(ln["rst"], 1)

        m2 = {n: sem("at2_" + n) for n in "ltp lt qp qkv ep e on otp ot op done tbo".split()}
        block2 = room.enter_context(nc.Block())

        @block2.gpsimd
        def _(pool):
            chp.engine = pool
            pool.wait_ge(s_rot, 1)
            for s in range(S):
                ln_pool(pool, s)
                pool.wait_ge(ln["nrm"], s + 1)
                ts = t[:, s]
                pool.tensor_tensor(ts, ts, wc("bo2")[:, None].to_broadcast([P, B, P]), ALU.add).then_inc(m2["tbo"], 1)

        @block2.scalar
        def _(act):
            act.preload_act_table(ACT.Exp)
            for s in range(S):
                ln_scalar(act, s)
                act.wait_ge(m2["ltp"], s + 1)
                act.activation(lnT[:], ps[:, 0:2, :].rearrange("p a b -> p (a b)"), ACT.Copy).then_inc(m2["lt"], 1)
                act.wait_ge(m2["ep"], s + 1)
                act.activation(sc2[:], sc2[:], ACT.Exp).then_inc(m2["e"], 1)
                act.wait_ge(m2["otp"], s + 1)
                act.activation(oT2[:], ps[:, 0:2, :].rearrange("p a b -> p (a b)"), ACT.Copy).then_inc(m2["ot"], 1)

        @block2.tensor
        def _(pe):
            for s in range(S):
                pe.wait_ge(ln["nrm"], s + 1)
                for b in range(B):
                    e = pe.transpose(ps[:, b // 4, (b % 4) * P:(b % 4 + 1) * P], xc[:, b, :], ident)
                e.then_inc(m2["ltp"], 1)
                pe.wait_ge(m2["lt"], s + 1)
                pe.wait_ge(s_rot, 1)
                for g in range(2):
                    pe.wait_ge(m2["qkv"], 2 * s + g)
                    for b in range(4):
                        i = 4 * g + b
                        e = pe.matmul(ps[:, 4 + b, 0:3 * P], lnT[:, i * P:(i + 1) * P], wb2[:, i, :], start=True, stop=True)
                    e.then_inc(m2["qp"], 1)
                pe.wait_ge(m2["on"], s + 1)
                for b in range(B):
                    e = pe.transpose(ps[:, b // 4, (b % 4) * P:(b % 4 + 1) * P], o2[:, b, :], ident)
                e.then_inc(m2["otp"], 1)
                pe.wait_ge(m2["ot"], s + 1)
                for b in range(B):
                    e = pe.matmul(ps[:, 2 + b // 4, (b % 4) * P:(b % 4 + 1) * P], oT2[:, b * P:(b + 1) * P], wc("Wo2"),
                                  start=True, stop=True)
                e.then_inc(m2["op"], 1)
                pe.wait_ge(m2["done"], s + 1)

        @block2.vector
        def _(dve):
            chv.engine = dve
            for s in range(S):
                ln_vector(dve, chv, s, s)
                for g in range(2):
                    dve.wait_ge(m2["qp"], 2 * s + g + 1)
                    dve.tensor_tensor(qkv[:, 4 * g:4 * g + 4, :], ps[:, 4:8, 0:3 * P], bb2[:, 4 * g:4 * g + 4, :],
                                      ALU.add).then_inc(m2["qkv"], 1)
                dve.wait_ge(m2["qkv"], 2 * s + 2)
                for b in range(B):
                    chv.done(dve.tensor_tensor(prod[:], qkv[:, :, P:2 * P], qkv[:, b, 0:P][:, None].to_broadcast([P, B, P]), ALU.mult))
                    chv.wait()
                    chv.done(dve.tensor_reduce(sc2[:, b], prod[:].rearrange("p c (h d) -> p c h d", h=H), AX.X, ALU.add))
                    chv.wait()
                chv.done(dve.tensor_reduce(mx2[:], sc2[:].rearrange("p b c h -> p b h c"), AX.X, ALU.max))
                chv.wait()
                dve.tensor_tensor(sc2[:], sc2[:], mx2[:, :, None].to_broadcast([P, B, B, H]), ALU.subtract).then_inc(m2["ep"], 1)
                dve.wait_ge(m2["e"], s + 1)
                chv.done(dve.tensor_reduce(mx2[:], sc2[:].rearrange("p b c h -> p b h c"), AX.X, ALU.add))
                chv.wait()
                chv.done(dve.reciprocal(mx2[:], mx2[:]))
                for b in range(B):
                    chv.done(dve.tensor_tensor(prod[:].rearrange("p c (h d) -> p c h d", h=H),
                                               qkv[:, :, 2 * P:3 * P].rearrange("p c (h d) -> p c h d", h=H),
                                               sc2[:, b][:, :, :, None].to_broadcast([P, B, H, DH]), ALU.mult))
                    chv.wait()
                    chv.done(dve.tensor_reduce(o2[:, b], prod[:].rearrange("p c e -> p e c"), AX.X, ALU.add))
                    chv.wait()
                dve.tensor_tensor(o2[:].rearrange("p b (h d) -> p b h d", h=H), o2[:].rearrange("p b (h d) -> p b h d", h=H),
                                  mx2[:][:, :, :, None].to_broadcast([P, B, H, DH]), ALU.mult).then_inc(m2["on"], 1)
                dve.wait_ge(m2["op"], s + 1)
                dve.wait_ge(m2["tbo"], s + 1)
                ts = t[:, s]
                dve.tensor_tensor(ts, ts, ps[:, 2:4, :].rearrange("p a (b c) -> p (a b) c", c=P), ALU.add).then_inc(m2["done"], 1)

        gs = {n: sem("gate_" + n) for n in "ltp lt xh xl lgp ep e g gp gT st".split()}

        def gate_feature_major(xT, s):
            return xT[:].rearrange("p (b s n) -> p b s n", b=B, s=S)[:, :, s, :]

        def experts(layer, w_in, n_up, hid, gate_w, gate_b):
            hc = hid // P
            wcols = (n_up + 1) * hid
            n_bias = hc + 1 if layer == 0 else 0
            room.close()
            lg = own(f"lg_{layer}", [P, B, E])
            pg = own(f"pg_{layer}", [P, B, E])
            gmx = own(f"gmx_{layer}", [P, B])
            cmp = own(f"cmp_{layer}", [P, B, E, E])
            cmq = own(f"cmq_{layer}", [P, B, E, E])
            gT = own(f"gT_{layer}", [E, BLK])
            wraw = own(f"wraw_{layer}", [P, 2, wcols + n_bias])
            wH = own(f"wH_{layer}", [P, 2, wcols], F32R)
            wL = own(f"wL_{layer}", [P, 2, wcols], F32R)
            bias = own(f"bias_{layer}", [P, 2, hc + 1])
            G = own(f"G_{layer}", [P, 2, T])
            hraw = own(f"hraw_{layer}", [P, 2, hc, CH])
            hH = own(f"hH_{layer}", [P, 2, hc, CH], F32R)
            hL = own(f"hL_{layer}", [P, 2, hc, CH], F32R)
            yg = own(f"yg_{layer}", [P, 2, CH])
            def rounds(engine):
                with engine.Fori(0, E // 2 - 1) as j:
                    for k in range(2 * NCH):
                        yield j, k, False
                for k in range(2 * NCH):
                    yield E // 2 - 1, k, True

            z = {n: sem(f"ex{layer}_" + n) for n in "split wH hp act hm hH hl yp yg acc".split()}
            zw = [[sem(f"ex{layer}_w{p}"), sem(f"ex{layer}_g{p}")] for p in range(2)]
            fin = {n: sem(f"fin{layer}_" + n) for n in "tp done st".split()}
            gi = layer * S
            blk = room.enter_context(nc.Block())
            lnn = {0: 2, 1: 6}[layer]

            @blk.sync
            def _(sp):
                for s in range(S):
                    sp.wait_ge(gs["gT"], s + 1 + gi)
                    sp.dma_start(gd[layer].rearrange("e (b s n) -> e b s n", b=B, s=S)[:, :, s, :],
                                 gT[:].rearrange("e (b n) -> e b n", b=B)).then_inc(gs["st"], 16)
                    sp.wait_ge(gs["st"], 16 * (s + 1 + gi))
                with sp.Fori(0, E // 2) as j:
                    for p in range(2):
                        e = 2 * j + p
                        sp.wait_ge(z["split"], e + 1)
                        sp.dma_start(wraw[:, p, :], w_in[bass.ds(e, 1)].rearrange("e p n -> p (e n)")).then_inc(zw[p][0], 16)
                        sp.wait_ge(z["yg"], NCH * e + 1)
                        sp.dma_start(G[:, p, :], gd[layer][bass.ds(e, 1), :].to_broadcast([P, T])).then_inc(zw[p][1], 16)
                if layer == 1:
                    for c in range(NCH):
                        sp.wait_ge(fin["done"], c + 1)
                        sp.dma_start(out.rearrange("b c n -> c b n")[:, 2 * c:2 * c + 2, :],
                                     acc[:, c * CH:(c + 1) * CH].rearrange("c (b n) -> c b n", b=2)).then_inc(fin["st"], 16)
                    sp.wait_ge(fin["st"], 16 * NCH)

            @blk.gpsimd
            def _(pool):
                chp.engine = pool
                for s in range(S):
                    ln_pool(pool, s + lnn)
                if layer == 1:
                    chp.done(pool.memset(acc[:], 0.0))
                    chp.wait()
                pool.sem_inc(z["split"], FREE_W)
                pool.sem_inc(z["acc"], FREE_ACC)

                def lower(j, p):
                    pool.wait_ge(z["wH"], 2 * j + p + 1)
                    pool.tensor_tensor(wL[:, p, 0:wcols], wraw[:, p, 0:wcols], wH[:, p, 0:wcols].bitcast(F32), ALU.subtract).then_inc(z["split"], 1)

                lower(0, 0)
                for j, k, last in rounds(pool):
                    if k == 1:
                        lower(j, 1)
                    if k == NCH + 1 and not last:
                        lower(j + 1, 0)
                    c = k % NCH
                    pool.wait_ge(z["yg"], 2 * NCH * j + k + 1 + FREE_Y)
                    pool.tensor_tensor(acc[:, c * CH:(c + 1) * CH], acc[:, c * CH:(c + 1) * CH], yg[:, k % 2, :], ALU.add).then_inc(z["acc"], 1)

            @blk.scalar
            def _(act):
                act.preload_act_table(ACT.Exp)
                for s in range(S):
                    ln_scalar(act, s + lnn)
                    act.wait_ge(gs["ltp"], s + 1 + gi)
                    act.activation(lnT[:], ps[:, 0:2, :].rearrange("p a b -> p (a b)"), ACT.Copy).then_inc(gs["lt"], 1)
                    act.wait_ge(gs["ep"], s + 1 + gi)
                    act.activation(pg[:], lg[:], ACT.Exp).then_inc(gs["e"], 1)
                act.preload_act_table(ACT.Gelu if layer == 0 else ACT.Silu)
                for j, k, last in rounds(act):
                    item = 2 * NCH * j + k
                    act.wait_ge(z["hl"], 2 * (item - 1) + FREE_H)
                    for h in range(hc):
                        act.wait_ge(z["hp"], item * hc + h + 1)
                        if layer == 0:
                            act.activation(hraw[:, k % 2, h, :], ps[:, h, :], ACT.Gelu,
                                           bias=bias[:, k // NCH, h:h + 1]).then_inc(z["act"], 1)
                        else:
                            act.activation(hraw[:, k % 2, h, :], ps[:, 2 * h, :], ACT.Silu).then_inc(z["act"], 1)

            @blk.tensor
            def _(pe):
                for s in range(S):
                    pe.wait_ge(ln["nrm"], s + 1 + lnn)
                    for b in range(B):
                        x = pe.transpose(ps[:, b // 4, (b % 4) * P:(b % 4 + 1) * P], xc[:, b, :], ident)
                    x.then_inc(gs["ltp"], 1)
                    pe.wait_ge(gs["lt"], s + 1 + gi)
                    for b in range(B):
                        x = pe.matmul(ps[:, 2, b * E:(b + 1) * E], lnT[:, b * P:(b + 1) * P], wc(gate_w), start=True, stop=True)
                    x.then_inc(gs["lgp"], 1)
                    pe.wait_ge(gs["g"], s + 1 + gi)
                    for b in range(B):
                        x = pe.transpose(ps[0:E, 3 + b // 4, (b % 4) * P:(b % 4 + 1) * P], lg[:, b, :], ident)
                    x.then_inc(gs["gp"], 1)
                    pe.wait_ge(gs["gT"], s + 1 + gi)
                pe.wait_ge(gs["xl"], S * (layer + 1))
                pe.sem_inc(z["yp"], FREE_Y)

                def up(j, k):
                    item, p = 2 * NCH * j + k, k // NCH % 2
                    xa, xb = xH[:, (k % NCH) * CH:(k % NCH + 1) * CH], xL[:, (k % NCH) * CH:(k % NCH + 1) * CH]
                    if k % NCH == 0:
                        pe.wait_ge(z["split"], 2 * j + k // NCH + 1 + FREE_W)
                    for h in range(hc):
                        if not (isinstance(item, int) and item == 0):
                            pe.wait_ge(z["act"] if layer == 0 else z["hm"], (item - 1) * hc + h + 1)
                        for u in range(n_up):
                            at = u * hid + h * P
                            o = ps[:, n_up * h + u, :]
                            pe.matmul(o, wH[:, p, at:at + P], xa, start=True, stop=False)
                            pe.matmul(o, wH[:, p, at:at + P], xb, start=False, stop=False)
                            x = pe.matmul(o, wL[:, p, at:at + P], xa, start=False, stop=True)
                        x.then_inc(z["hp"], 1)

                def down(j, k):
                    item, p = 2 * NCH * j + k, k // NCH
                    pe.wait_ge(z["yg"], item - 1 + FREE_Y)
                    pe.wait_ge(z["hl"], 2 * (item + 1) + FREE_H)
                    for h in range(hc):
                        at = n_up * hid + h * P
                        o = ps[:, 4 + k % 2, :]
                        pe.matmul(o, wH[:, p, at:at + P], hH[:, k % 2, h, :], start=h == 0, stop=False)
                        pe.matmul(o, wH[:, p, at:at + P], hL[:, k % 2, h, :], start=False, stop=False)
                        x = pe.matmul(o, wL[:, p, at:at + P], hH[:, k % 2, h, :], start=False, stop=h == hc - 1)
                    x.then_inc(z["yp"], 1)

                up(0, 0)
                for j, k, last in rounds(pe):
                    if not (last and k == 2 * NCH - 1):
                        up(j, k + 1)
                    down(j, k)
                if layer == 0:
                    pe.wait_ge(z["acc"], E * NCH + FREE_ACC)
                    for s in range(S):
                        for b in range(B):
                            x = pe.transpose(ps[:, 2 * s + b // 4, (b % 4) * P:(b % 4 + 1) * P],
                                             acc[:, (b * S + s) * P:(b * S + s + 1) * P], ident)
                        x.then_inc(fin["tp"], 1)
                else:
                    pe.wait_ge(z["yg"], E * NCH + FREE_Y)
                    for c in range(NCH):
                        for i in range(4):
                            x = pe.transpose(ps[:, c, i * P:(i + 1) * P], t[:, i % 2, 2 * c + i // 2, :], ident)
                        x.then_inc(fin["tp"], 1)

            @blk.vector
            def _(dve):
                chv.engine = dve
                for s in range(S):
                    ln_vector(dve, chv, s, s + lnn)
                    dve.wait_ge(gs["lt"], s + 1 + gi)
                    lnv = lnT[:].rearrange("p (b n) -> p b n", b=B)
                    chv.done(dve.tensor_copy(gate_feature_major(xH, s), lnv))
                    chv.wait()
                    dve.tensor_tensor(gate_feature_major(xL, s), lnv, gate_feature_major(xH, s).bitcast(F32), ALU.subtract).then_inc(gs["xl"], 1)
                    dve.wait_ge(gs["lgp"], s + 1 + gi)
                    if gate_b is None:
                        chv.done(dve.tensor_copy(lg[:], ps[:, 2, 0:B * E].rearrange("p (b e) -> p b e", b=B)))
                    else:
                        chv.done(dve.tensor_tensor(lg[:], ps[:, 2, 0:B * E].rearrange("p (b e) -> p b e", b=B),
                                                   wc(gate_b)[:, None].to_broadcast([P, B, E]), ALU.add))
                    chv.wait()
                    chv.done(dve.tensor_reduce(gmx[:], lg[:], AX.X, ALU.max))
                    chv.wait()
                    dve.tensor_tensor(lg[:], lg[:], gmx[:, :, None].to_broadcast([P, B, E]), ALU.subtract).then_inc(gs["ep"], 1)
                    dve.wait_ge(gs["e"], s + 1 + gi)
                    chv.done(dve.tensor_reduce(gmx[:], pg[:], AX.X, ALU.add))
                    chv.wait()
                    chv.done(dve.reciprocal(gmx[:], gmx[:]))
                    chv.wait()
                    chv.done(dve.tensor_tensor(pg[:], pg[:], gmx[:, :, None].to_broadcast([P, B, E]), ALU.mult))
                    chv.wait()
                    pi = pg[:][:, :, :, None].to_broadcast([P, B, E, E])
                    pj = pg[:][:, :, None, :].to_broadcast([P, B, E, E])
                    chv.done(dve.tensor_tensor(cmp[:], pj, pi, ALU.is_equal))
                    chv.done(dve.tensor_tensor(cmq[:], pj, pi, ALU.is_gt))
                    chv.wait()
                    chv.done(dve.tensor_tensor(cmp[:], cmp[:], wc("earlier").rearrange("p (i j) -> p i j", i=E)[:, None].to_broadcast([P, B, E, E]), ALU.mult))
                    chv.wait()
                    chv.done(dve.tensor_tensor(cmp[:], cmp[:], cmq[:], ALU.add))
                    chv.wait()
                    chv.done(dve.tensor_reduce(lg[:], cmp[:], AX.X, ALU.add))
                    chv.wait()
                    k = dve.scalar_tensor_tensor(lg[:], lg[:], TOPK - 0.5, pg[:], ALU.is_lt, ALU.mult)
                    if layer == 0:
                        k.then_inc(gs["g"], 1)
                    else:
                        chv.done(k)
                        chv.wait()
                        chv.done(dve.tensor_reduce(gmx[:], lg[:], AX.X, ALU.add))
                        chv.wait()
                        chv.done(dve.reciprocal(gmx[:], gmx[:]))
                        chv.wait()
                        dve.tensor_tensor(lg[:], lg[:], gmx[:, :, None].to_broadcast([P, B, E]), ALU.mult).then_inc(gs["g"], 1)
                    dve.wait_ge(gs["gp"], s + 1 + gi)
                    dve.wait_ge(gs["st"], 16 * (s + gi))
                    dve.tensor_copy(gT[:].rearrange("p (a b) -> p a b", a=2), ps[0:E, 3:5, :]).then_inc(gs["gT"], 1)
                dve.sem_inc(z["hl"], FREE_H)
                dve.sem_inc(z["yg"], FREE_Y)
                half = hc // 2

                def upper(j, p):
                    dve.wait_ge(zw[p][0], 16 * (j + 1))
                    dve.wait_ge(z["yp"], NCH * (2 * j + p - 1) + FREE_Y)
                    if layer == 0:
                        dve.tensor_copy(bias[:, p, :], wraw[:, p, wcols:])
                    dve.tensor_copy(wH[:, p, 0:wcols], wraw[:, p, 0:wcols]).then_inc(z["wH"], 1)

                def gated(j, k):
                    item, p, c = 2 * NCH * j + k, k // NCH, k % NCH
                    dve.wait_ge(z["yp"], item + 1 + FREE_Y)
                    if c == 0:
                        dve.wait_ge(zw[p][1], 16 * (j + 1))
                    dve.wait_ge(z["acc"], item - 1 + FREE_ACC)
                    gsl = G[:, p, c * CH:(c + 1) * CH]
                    if layer == 0:
                        dve.scalar_tensor_tensor(yg[:, k % 2, :], ps[:, 4 + k % 2, :], bias[:, p, hc:hc + 1],
                                                 gsl, ALU.add, ALU.mult).then_inc(z["yg"], 1)
                    else:
                        dve.tensor_tensor(yg[:, k % 2, :], ps[:, 4 + k % 2, :], gsl, ALU.mult).then_inc(z["yg"], 1)

                upper(0, 0)
                for j, k, last in rounds(dve):
                    item = 2 * NCH * j + k
                    if layer == 1:
                        for h in range(hc):
                            dve.wait_ge(z["act"], item * hc + h + 1)
                            dve.tensor_tensor(hraw[:, k % 2, h, :], hraw[:, k % 2, h, :], ps[:, 2 * h + 1, :], ALU.mult).then_inc(z["hm"], 1)
                    for g in range(2):
                        dve.wait_ge(z["act"] if layer == 0 else z["hm"], item * hc + (g + 1) * half)
                        if g == 0:
                            dve.wait_ge(z["yp"], item - 1 + FREE_Y)
                        src, hi = hraw[:, k % 2, g * half:(g + 1) * half, :], hH[:, k % 2, g * half:(g + 1) * half, :]
                        dve.tensor_copy(hi, src).then_inc(z["hH"], 1)
                        dve.wait_ge(z["hH"], 2 * item + g + 1)
                        dve.tensor_tensor(hL[:, k % 2, g * half:(g + 1) * half, :], src, hi.bitcast(F32), ALU.subtract).then_inc(z["hl"], 1)
                    if k > 0:
                        gated(j, k - 1)
                    if k == 1:
                        upper(j, 1)
                    if k == NCH + 1 and not last:
                        upper(j + 1, 0)
                    if k == 2 * NCH - 1:
                        gated(j, k)
                if layer == 0:
                    for s in range(S):
                        dve.wait_ge(fin["tp"], s + 1)
                        dve.tensor_tensor(t[:, s], t[:, s], ps[:, 2 * s:2 * s + 2, :].rearrange("p a (b c) -> p (a b) c", c=P), ALU.add).then_inc(fin["done"], 1)
                    dve.wait_ge(fin["done"], S)
                else:
                    dve.wait_ge(z["acc"], E * NCH + FREE_ACC)
                    for c in range(NCH):
                        dve.wait_ge(fin["tp"], c + 1)
                        dve.tensor_tensor(acc[:, c * CH:(c + 1) * CH], acc[:, c * CH:(c + 1) * CH], ps[:, c, :], ALU.add).then_inc(fin["done"], 1)

        experts(0, a["ex2"], 1, F2, "gate2", "gateb2")

        room.close()
        wq3H, wq3L = own("wq3H", [P, 2 * P], F32R), own("wq3L", [P, 2 * P], F32R)
        wk3H, wk3L = own("wk3H", [P, 2 * P], F32R), own("wk3L", [P, 2 * P], F32R)
        wv3H, wv3L = own("wv3H", [P, P], F32R), own("wv3L", [P, P], F32R)
        wo3 = own("wo3", [P, 3, P], BF16)
        wtmp = own("wtmp", [P, P])
        xsH, xsL = own("xsH", [P, N], F32R), own("xsL", [P, N], F32R)
        q3H, q3L = own("q3H", [P, 2, N], F32R), own("q3L", [P, 2, N], F32R)
        k3H, k3S = own("k3H", [P, 2, N], F32R), own("k3S", [P, 2, N], F32R)
        v3r = own("v3r", [P, S, P])
        vp3 = own("vp3", [P, S, H, 3, DH], BF16)
        mx3 = own("mx3", [P, H // 2, 2 * S])
        sm3 = own("sm3", [P, H // 2, 2 * S])
        smb3 = own("smb3", [P, H // 2, 2 * S], BF16)
        s3 = own("s3", [P, 2, 2 * S, N], BF16)
        p3 = own("p3", [P, 2, 2 * S, N], BF16)
        pT3 = own("pT3", [P, 2, S, N], BF16)
        o3b = own("o3b", [P, S, P], BF16)
        oT3 = own("oT3", [P, N], BF16)
        m3 = {n: sem("at3_" + n) for n in
              ("wl ltp lt xl xs qp kp vp qh ql kh ks vb vr v2 v sp sb sub ex p tp pt op o otp ot fp done tbo").split()}
        block4 = room.enter_context(nc.Block())

        @block4.gpsimd
        def _(pool):
            chp.engine = pool
            for s in range(S):
                ln_pool(pool, s + 4)
                pool.wait_ge(ln["nrm"], s + 5)
                ts = t[:, s]
                pool.tensor_tensor(ts, ts, wc("bo3")[:, None].to_broadcast([P, B, P]), ALU.add).then_inc(m3["tbo"], 1)
            with pool.Fori(0, B) as b:
                pool.wait_ge(m3["v2"], b + 1)
                pool.tensor_tensor(vp3[:, :, :, 2, :], v3r[:].rearrange("p s (h d) -> p s h d", h=H), vp3[:, :, :, 1, :], ALU.subtract).then_inc(m3["v"], 1)

        @block4.sync
        def _(sp):
            sp.wait_ge(m3["xl"], S)
            with sp.Fori(0, B) as b:
                sp.wait_ge(m3["vp"], b + 1)
                sp.dma_start(xsH[:].bitcast(F32), xH[:, bass.ds(b * N, N)].bitcast(F32)).then_inc(m3["xs"], 16)
                sp.dma_start(xsL[:].bitcast(F32), xL[:, bass.ds(b * N, N)].bitcast(F32)).then_inc(m3["xs"], 16)

        def vbank():
            return ps[:, 6:8, 384:384 + P]

        @block4.scalar
        def _(act):
            act.preload_act_table(ACT.Exp)
            for s in range(S):
                ln_scalar(act, s + 4)
                act.wait_ge(m3["ltp"], s + 1)
                act.activation(lnT[:], ps[:, 0:2, :].rearrange("p a b -> p (a b)"), ACT.Copy).then_inc(m3["lt"], 1)
            act.sem_inc(m3["sb"], 1)
            with act.Fori(0, B) as b:
                act.wait_ge(m3["qp"], b + 1)
                act.activation(q3H[:], ps[:, 0, :].rearrange("p (g n) -> p g n", g=2), ACT.Copy, scale=DH ** -0.5).then_inc(m3["qh"], 1)
                act.wait_ge(m3["kp"], b + 1)
                act.activation(k3H[:], ps[:, 1, :].rearrange("p (g n) -> p g n", g=2), ACT.Copy).then_inc(m3["kh"], 1)
                act.wait_ge(m3["vp"], b + 2)
                act.activation(vp3[:, :, :, 0, :], vbank().rearrange("p s (h d) -> p s h d", h=H), ACT.Copy).then_inc(m3["vb"], 1)
                act.wait_ge(m3["vr"], b + 1)
                act.activation(vp3[:, :, :, 1, :], v3r[:].rearrange("p s (h d) -> p s h d", h=H), ACT.Copy).then_inc(m3["v2"], 1)

                def rounded(g):
                    act.wait_ge(m3["sp"], b * 4 + g + 1)
                    act.activation(s3[:, g % 2], ps[:, 2 + 2 * (g % 2):4 + 2 * (g % 2), :].rearrange("p a (s n) -> p (a s) n", s=2),
                                   ACT.Copy).then_inc(m3["sb"], 1)
                rounded(0)
                for g in range(4):
                    if g + 1 < 4:
                        rounded(g + 1)
                    act.wait_ge(m3["sub"], (b * 4 + g + 1) * 4)
                    if g >= 2:
                        act.wait_ge(m3["tp"], b * H + 2 * g - 2)
                    for i in range(4):
                        act.activation(p3[:, g % 2, i, :], s3[:, g % 2, i, :], ACT.Exp,
                                       accum_out=sm3[:, g, i:i + 1]).then_inc(m3["ex"], 1)

        @block4.tensor
        def _(pe):
            for s in range(S):
                pe.wait_ge(ln["nrm"], s + 5)
                for b in range(B):
                    x = pe.transpose(ps[:, b // 4, (b % 4) * P:(b % 4 + 1) * P], xc[:, b, :], ident)
                x.then_inc(m3["ltp"], 1)
                pe.wait_ge(m3["lt"], s + 1)
            pe.wait_ge(m3["wl"], 3)
            pe.sem_inc(m3["vp"], 1)
            with pe.Fori(0, B) as b:
                pe.wait_ge(m3["xs"], 32 * b + 32)
                pe.wait_ge(m3["done"], b + 1)
                for bank, wh, wl, what in ((0, wq3H, wq3L, "qp"), (1, wk3H, wk3L, "kp")):
                    for g in range(2):
                        o = ps[:, bank, g * N:(g + 1) * N]
                        pe.matmul(o, wh[:, g * P:(g + 1) * P], xsH[:], start=True, stop=False)
                        pe.matmul(o, wh[:, g * P:(g + 1) * P], xsL[:], start=False, stop=False)
                        x = pe.matmul(o, wl[:, g * P:(g + 1) * P], xsH[:], start=False, stop=True)
                    x.then_inc(m3[what], 1)
                for s in range(S):
                    o = ps[:, 6 + s, 384:384 + P]
                    pe.matmul(o, xsH[:, s * P:(s + 1) * P], wv3H[:], start=True, stop=False)
                    pe.matmul(o, xsL[:, s * P:(s + 1) * P], wv3H[:], start=False, stop=False)
                    x = pe.matmul(o, xsH[:, s * P:(s + 1) * P], wv3L[:], start=False, stop=True)
                x.then_inc(m3["vp"], 1)

                def scores(g):
                    pe.wait_ge(m3["sb"], b * 4 + max(g - 1, 0) + 1)
                    for h in (2 * g, 2 * g + 1):
                        r, q = 32 * (h % 4), h // 4
                        for s in range(S):
                            o = ps[:, 2 + 2 * (g % 2) + h % 2, s * N:(s + 1) * N]
                            pe.matmul(o, q3H[r:r + 32, q, s * P:(s + 1) * P], k3S[r:r + 32, q, :], start=True, stop=False)
                            x = pe.matmul(o, q3L[r:r + 32, q, s * P:(s + 1) * P], k3S[r:r + 32, q, :], start=False, stop=True)
                    x.then_inc(m3["sp"], 1)

                pe.wait_ge(m3["ql"], b + 1)
                pe.wait_ge(m3["ks"], b + 1)
                scores(0)
                scores(1)
                pe.wait_ge(m3["v"], b + 1)
                for h in range(H):
                    g = h // 2
                    if h % 2 == 0:
                        pe.wait_ge(m3["p"], (b * 4 + g + 1) * 4)
                    if h >= 2:
                        pe.wait_ge(m3["pt"], b * H + h - 1)
                    for kt in range(S):
                        for s in range(S):
                            x = pe.transpose(psb(h % 2)[:, kt * N + s * P:kt * N + (s + 1) * P],
                                             p3[:, g % 2, (h % 2) * 2 + s, kt * P:(kt + 1) * P], identb[:])
                    x.then_inc(m3["tp"], 1)
                    if h % 2 == 0 and g + 2 < 4:
                        scores(g + 2)
                    pe.wait_ge(m3["pt"], b * H + h + 1)
                    for s in range(S):
                        for kt in range(S):
                            x = pe.matmul(ps[:, 6 + s, h * 48:(h + 1) * 48], pT3[:, h % 2, kt, s * P:(s + 1) * P],
                                          vp3[:, kt, h].rearrange("p a d -> p (a d)"), start=kt == 0, stop=kt == 1)
                    x.then_inc(m3["op"], 1)
                pe.wait_ge(m3["o"], b + 1)
                for s in range(S):
                    x = pe.transpose(psb(0)[:, s * P:(s + 1) * P], o3b[:, s, :], identb[:])
                x.then_inc(m3["otp"], 1)
                pe.wait_ge(m3["ot"], b + 1)
                for s in range(S):
                    for i in range(3):
                        x = pe.matmul(ps[:, 6 + s, 384:384 + P], oT3[:, s * P:(s + 1) * P], wo3[:, i, :], start=i == 0, stop=i == 2)
                x.then_inc(m3["fp"], 1)

        @block4.vector
        def _(dve):
            chv.engine = dve
            for name, wh, wl in (("Wq3", wq3H, wq3L), ("Wk3", wk3H, wk3L), ("Wv3", wv3H, wv3L)):
                chv.done(dve.tensor_copy(wh[:], wc(name)))
                chv.wait()
                dve.tensor_tensor(wl[:], wc(name), wh[:].bitcast(F32), ALU.subtract).then_inc(m3["wl"], 1)
            chv.done(dve.tensor_copy(wo3[:, 0], wc("Wo3")))
            chv.wait()
            chv.done(dve.tensor_tensor(wtmp[:], wc("Wo3"), wo3[:, 0], ALU.subtract))
            chv.wait()
            chv.done(dve.tensor_copy(wo3[:, 1], wtmp[:]))
            chv.wait()
            chv.done(dve.tensor_tensor(wo3[:, 2], wtmp[:], wo3[:, 1], ALU.subtract))
            for s in range(S):
                ln_vector(dve, chv, s, s + 4)
                dve.wait_ge(m3["lt"], s + 1)
                lnv = lnT[:].rearrange("p (b n) -> p b n", b=B)
                chv.done(dve.tensor_copy(gate_feature_major(xH, s), lnv))
                chv.wait()
                dve.tensor_tensor(gate_feature_major(xL, s), lnv, gate_feature_major(xH, s).bitcast(F32), ALU.subtract).then_inc(m3["xl"], 1)
            dve.sem_inc(m3["done"], 1)
            with dve.Fori(0, B) as b:
                chv.loop(b, 12)
                dve.wait_ge(m3["qh"], b + 1)
                dve.scalar_tensor_tensor(q3L[:], ps[:, 0, :].rearrange("p (g n) -> p g n", g=2), DH ** -0.5,
                                         q3H[:].bitcast(F32), ALU.mult, ALU.subtract).then_inc(m3["ql"], 1)
                dve.wait_ge(m3["kh"], b + 1)
                dve.scalar_tensor_tensor(k3S[:], k3H[:].bitcast(F32), wc("kmask"), ps[:, 1, :].rearrange("p (g n) -> p g n", g=2),
                                         ALU.mult, ALU.add).then_inc(m3["ks"], 1)
                dve.wait_ge(m3["vb"], b + 1)
                dve.tensor_tensor(v3r[:].rearrange("p s (h d) -> p s h d", h=H), vbank().rearrange("p s (h d) -> p s h d", h=H),
                                  vp3[:, :, :, 0, :], ALU.subtract).then_inc(m3["vr"], 1)

                def centre(g):
                    dve.wait_ge(m3["sb"], b * 4 + g + 2)
                    chv.done(dve.tensor_reduce(mx3[:, g, :], s3[:, g % 2], AX.X, ALU.max))
                    chv.wait()
                    for i in range(4):
                        dve.tensor_scalar(s3[:, g % 2, i, :], s3[:, g % 2, i, :], mx3[:, g, i:i + 1], None,
                                          ALU.subtract).then_inc(m3["sub"], 1)

                def normalise(g):
                    dve.wait_ge(m3["ex"], (b * 4 + g + 1) * 4)
                    chv.done(dve.tensor_copy(smb3[:, g, :], sm3[:, g, :]))
                    chv.wait()
                    chv.done(dve.reciprocal(sm3[:, g, :], smb3[:, g, :]))
                    chv.wait()
                    for i in range(4):
                        dve.tensor_scalar(p3[:, g % 2, i, :], p3[:, g % 2, i, :], sm3[:, g, i:i + 1], None,
                                          ALU.mult).then_inc(m3["p"], 1)

                def evacuate(h):
                    dve.wait_ge(m3["tp"], b * H + h + 1)
                    if h >= 2:
                        dve.wait_ge(m3["op"], b * H + h - 1)
                    dve.tensor_copy(pT3[:, h % 2], psb(h % 2)[:, 0:2 * N].rearrange("p (k n) -> p k n", k=2)).then_inc(m3["pt"], 1)

                centre(0)
                for g in range(4):
                    normalise(g) if g else None
                    if g + 1 < 4:
                        centre(g + 1)
                    if g == 0:
                        normalise(0)
                    evacuate(2 * g)
                    evacuate(2 * g + 1)
                dve.wait_ge(m3["op"], b * H + H)
                with nc.allow_low_precision(reason="the reference's output here is bfloat16; the sum itself is float32"):
                    dve.tensor_reduce(o3b[:].rearrange("p s (h d) -> p s h d", h=H),
                                           ps[:, 6:8, 0:384].rearrange("p s (h a d) -> p s h d a", h=H, a=3), AX.X, ALU.add).then_inc(m3["o"], 1)
                dve.wait_ge(m3["otp"], b + 1)
                dve.tensor_copy(oT3[:], psb(0)[:, 0:N]).then_inc(m3["ot"], 1)
                dve.wait_ge(m3["fp"], b + 1)
                dve.wait_ge(m3["tbo"], S)
                tb = t[:, :, bass.ds(b, 1), :].rearrange("p s b c -> p s (b c)")
                dve.tensor_tensor(tb, tb, vbank(), ALU.add).then_inc(m3["done"], 1)
            chv.end(B)

        experts(1, a["ex3"], 2, F3, "router3", None)
        room.close()


def _layout(inp):
    def rows(v):
        return np.tile(np.asarray(v).reshape(1, -1), (P, 1))

    def col(v):
        v = np.asarray(v).reshape(-1, 1)
        return np.concatenate([v, np.zeros((P - len(v), 1), np.float32)])

    def swap(x):
        y = x.reshape(*x.shape[:-1], -1, 2, DH // 2)[..., ::-1, :]
        return y.reshape(x.shape)

    def slots(x):
        return np.repeat(x.reshape(P, H, 1, DH), 2, axis=2).reshape(P, 2 * H * DH)

    f = (np.arange(B, dtype=np.float64)[:, None] / 10000.0 ** (np.arange(0, DH, 2) / DH)[None, :]).astype(np.float32)
    cos = np.cos(np.concatenate([f, f], 1))
    sin = np.sin(np.concatenate([-f, f], 1))
    wq, wk, wv = (inp[f"L2_attn_W{n}"].T for n in "qkv")
    bq, bk, bv = (inp[f"L2_attn_b{n}"] for n in "qkv")
    parts = {
        "Wq0": inp["L0_conv_Wq"].T, "Wk0": inp["L0_conv_Wk"].T, "Wv0": inp["L0_conv_Wv"], "Wf0": inp["L0_conv_Wf"].T,
        "W1": np.concatenate([inp[f"L1_conv_W{n}"].T for n in "qkvs"], 1), "We1": inp["L1_conv_We"].T,
        "Wqkv2": np.concatenate([wq, wk, wv], 1), "Wqk2r": np.concatenate([swap(wq), swap(wk)], 1),
        "Wo2": inp["L2_attn_Wo"].T, "gate2": inp["L2_ffn_gate_w"],
        "Wq3": slots(inp["L3_attn_Wq"]), "Wk3": slots(inp["L3_attn_Wkv"][:, :P]), "Wv3": inp["L3_attn_Wkv"][:, P:],
        "Wo3": inp["L3_attn_Wo"], "router3": inp["L3_ffn_router_w"], "ident": np.eye(P),
        "bv0": col(inp["L0_conv_bv"]), "bn_w": col(inp["L0_conv_bn_w"]), "bn_b": col(inp["L0_conv_bn_b"]),
        "bn_mean": col(inp["L0_conv_bn_mean"]), "bn_var": col(inp["L0_conv_bn_var"]),
        "bq0": col(inp["L0_conv_bq"]), "bk0": col(inp["L0_conv_bk"]), "be1": col(inp["L1_conv_be"]),
        "gamma": rows(inp["L0_conv_gamma"]),
        "kmask": np.where(np.arange(P) % (2 * DH) < DH, 0.0, -1.0)[:, None],
        "bias1": rows(np.concatenate([inp[f"L1_conv_b{n}"] for n in "qkvs"])),
        "bqkv2": rows(np.concatenate([bq, bk, bv])), "bqk2r": rows(np.concatenate([swap(bq), swap(bk)])),
        "bo2": rows(inp["L2_attn_bo"]), "gateb2": rows(inp["L2_ffn_gate_b"]), "bo3": rows(inp["L3_attn_bo"]),
        "cosq": rows(cos * DH ** -0.5), "sinq": rows(sin * DH ** -0.5), "cosk": rows(cos), "sink": rows(sin),
        "earlier": rows(np.tril(np.ones((E, E)), -1)),
    }
    pack = np.concatenate([np.asarray(parts[n], np.float32) for n, _ in PACK], 1)

    def down(x, hid):
        return x.reshape(E, hid // P, P, P).transpose(0, 2, 1, 3).reshape(E, P, hid)
    ex2 = np.concatenate([inp["L2_ffn_w1"], down(inp["L2_ffn_w2"], F2), inp["L2_ffn_b1"].reshape(E, F2 // P, P).transpose(0, 2, 1),
                          inp["L2_ffn_b2"][:, :, None]], 2)
    ex3 = np.concatenate([inp["L3_ffn_w1"], inp["L3_ffn_w3"], down(inp["L3_ffn_w2"], F3)], 2)
    return {"pack": pack, "x": inp["x"].reshape(B, P, N), "ex2": ex2, "ex3": ex3}


def kernel(**inputs):
    from concourse import bacc
    from concourse.bass_utils import run_bass_kernel_spmd

    arrays = {k: np.ascontiguousarray(v) for k, v in _layout({k: np.asarray(v) for k, v in inputs.items()}).items()}
    nc = bacc.Bacc("TRN2", target_bir_lowering=False, num_devices=1)
    args = {k: nc.dram_tensor(f"in_{k}", v.shape, mybir.dt.from_np(v.dtype), kind="ExternalInput").ap() for k, v in arrays.items()}
    out = nc.dram_tensor("out", (B, P, N), F32, kind="ExternalOutput").ap()
    build(nc, args, out)
    r = run_bass_kernel_spmd(nc, [{f"in_{k}": v for k, v in arrays.items()}], core_ids=[0])
    return r.results[0]["out"].reshape(B, P, 16, 16)
```

```python
from contextlib import ExitStack

import numpy as np

import concourse.bass as bass
from concourse import mybir

F32 = mybir.dt.float32
F32R = mybir.dt.float32r
BF16 = mybir.dt.bfloat16
ALU = mybir.AluOpType
ACT = mybir.ActivationFunctionType
AX = mybir.AxisListType

P = 128
B = 8
N = 256
S = N // P
T = B * N
H, DH = 8, 16
KD = 16
QK1 = 64
E = 8
TOPK = 2
F2 = 512
F3 = 256
CH = 512
NCH = T // CH
BLK = B * P
FREE_W = 2
FREE_ACC = 2
FREE_H = 3
FREE_Y = NCH + 1
BN_EPS = 1e-5
LN_EPS = 1e-5

PACK = [
    ("Wq0", KD), ("Wk0", KD), ("Wv0", P), ("Wf0", P), ("W1", 2 * QK1 + P + KD), ("We1", KD), ("ident", P),
    ("bv0", 1), ("bn_w", 1), ("bn_b", 1), ("bn_mean", 1), ("bn_var", 1), ("bq0", 1), ("bk0", 1), ("be1", 1),
    ("gamma", 1), ("bias1", 2 * QK1 + P + KD),
    ("Wqkv2", 3 * P), ("Wqk2r", 2 * P), ("Wo2", P), ("gate2", E),
    ("Wq3", 2 * P), ("Wk3", 2 * P), ("Wv3", P), ("Wo3", P), ("router3", E), ("kmask", 1),
    ("bqkv2", 3 * P), ("bqk2r", 2 * P), ("bo2", P), ("gateb2", E),
    ("bo3", P), ("cosq", B * DH), ("sinq", B * DH), ("cosk", B * DH), ("sink", B * DH),
    ("earlier", E * E),
]
AT = {}
_at = 0
for _name, _w in PACK:
    AT[_name] = (_at, _at + _w)
    _at += _w
NPACK = _at


class Chain:

    def __init__(self, engine, sem):
        self.engine, self.sem, self.base, self.n, self.total = engine, sem, None, 0, 0

    def done(self, ins):
        ins.then_inc(self.sem, 1)
        self.n += 1
        return ins

    def wait(self):
        if self.base is None:
            self.engine.wait_ge(self.sem, self.total + self.n)
        else:
            self.engine.wait_ge(self.sem, self.base + self.n)

    def loop(self, i, per):
        self.total += self.n
        self.base, self.n, self.per = i * per + self.total, 0, per

    def end(self, times):
        assert self.n == self.per, (self.n, self.per)
        self.total += times * self.per
        self.base, self.n = None, 0


def build(nc, a, out):
    ctx = ExitStack()
    with ctx:
        def sb(name, shape, dt=F32):
            return ctx.enter_context(nc.sbuf_tensor(name, shape, dt))

        def sem(name):
            return ctx.enter_context(nc.semaphore(name))

        ps = ctx.enter_context(nc.psum_tensor("ps", [P, 8, CH], F32))

        def psb(bank):
            return ps[:, bank, :].bitcast(BF16)

        w = sb("w", [P, NPACK])

        def wc(name, lo=0, hi=None, rows=P):
            x, y = AT[name]
            return w[0:rows, x + lo:(y if hi is None else x + hi)]

        ident = wc("ident")
        identb = sb("identb", [P, P], BF16)
        t = sb("t", [P, S, B, P])
        halfs = sb("halfs", [P, B])
        stats = sb("stats", [P, S, B, 6])
        mv = sb("mv", [P, S, B, 2])
        var = sb("var", [P, S, B])
        rstd = sb("rstd", [P, S, B])
        xc = sb("xc", [P, S, B, P])
        lnT = sb("lnT", [P, S, BLK])
        xH = sb("xH", [P, T], F32R)
        xL = sb("xL", [P, T], F32R)
        acc = sb("acc", [P, T])
        gd = nc.dram_tensor("gates_scratch", [2, E, T], F32, kind="Internal").ap()
        wb2 = sb("wb2", [P, B, 2 * P])
        bb2 = sb("bb2", [P, B, 3 * P])

        room = ExitStack()

        def own(name, shape, dt=F32):
            return room.enter_context(nc.sbuf_tensor(name, shape, dt))

        s_w, s_w2, s_id = sem("packed_loaded"), sem("rest_loaded"), sem("identb_ready")
        s_set_pe, s_set_v, s_set_p = sem("setup_pe"), sem("setup_dve"), sem("setup_pool")
        s_rot = sem("rotated_ready")
        dve_s, pool_s = sem("dve_steps"), sem("pool_steps")

        xs = own("xs", [P, 2, CH])
        rtmp = own("rtmp", [P, B, P])
        gM = own("gM", [P, P])
        bn_inv, bn_s, bn_t = (own(n, [P, 1]) for n in ("bn_inv", "bn_s", "bn_t"))
        q0 = own("q0", [KD, 2, CH])
        k0 = own("k0", [KD, 2, CH])
        vT0 = own("vT0", [P, 2, 4, P])
        nm0 = own("nm0", [P, 2, 4])
        sm0 = own("sm0", [P, 2, 4])
        A0 = own("A0", [P, 2, 4, N])
        AT0 = own("AT0", [P, 2, 4, N])
        x1 = own("x1", [P, 2, CH])
        pr1 = own("pr1", [P, 2, 4, 272])
        ke1 = own("ke1", [KD, 2, CH])
        qk1 = own("qk1", [P, 2, 4, QK1])
        g1 = own("g1", [P, 2, 4])
        vd1 = own("vd1", [P, 2, 4, P])
        nm1 = own("nm1", [P, 2, 2])
        sm1 = own("sm1", [P, 2, 2])
        a1 = own("a1", [P, 2, 2, KD])
        aT1 = own("aT1", [KD, 2, 2, P])
        names = ("xs0 xs1 qkp qk0 vtp vt0 ep nm ex an atp at0a at0v fp x1 prp pr kep ke z ez vd e1p nm1 ex1 a1 "
                 "a1p aT1 tp tdone").split()
        m = {n: sem("l01_" + n) for n in names}
        block = room.enter_context(nc.Block())
        chv, chp = Chain(None, dve_s), Chain(None, pool_s)

        def in_step(steps, j):
            for step in steps:
                for p in range(2):
                    step(p, 2 * j + p)

        def bank(p, k):
            return ps[:, 4 * p + k, :]

        def banks(p, lo, hi):
            return ps[:, 4 * p + lo:4 * p + hi, :]

        @block.sync
        def _(sp):
            early = AT["bias1"][1]
            sp.dma_start(w[:, 0:early], a["pack"][:, 0:early]).then_inc(s_w, 16)

            def images_in(p, i):
                sp.dma_start(xs[:, p, :].rearrange("c (b n) -> c b n", b=2),
                             a["x"][bass.ds(2 * i, 2)].rearrange("b c n -> c b n")).then_inc(m[f"xs{p}"], 16)
            images_in(0, 0)
            images_in(1, 1)
            sp.dma_start(w[:, early:], a["pack"][:, early:]).then_inc(s_w2, 16)
            for p in range(2):
                sp.wait_ge(m["fp"], p + 1)
                images_in(p, 2 + p)

        @block.gpsimd
        def _(pool):
            chp.engine = pool
            chp.done(pool.memset(halfs[:], -0.5))
            pool.wait_ge(s_w, 16)
            chp.done(pool.tensor_scalar(bn_s[:], wc("bn_var"), BN_EPS, None, ALU.add))
            chp.wait()
            chp.done(pool.tensor_tensor(bn_inv[:], bn_s[:], halfs[:, 0:1], ALU.pow))
            chp.wait()
            pool.tensor_tensor(bn_s[:], wc("bn_w"), bn_inv[:], ALU.mult).then_inc(s_set_p, 1)
            pool.wait_ge(s_w2, 16)
            for dst, plain, swapped in ((wb2, "Wqkv2", "Wqk2r"), (bb2, "bqkv2", "bqk2r")):
                for i, (c_, s_) in enumerate((("cosq", "sinq"), ("cosk", "sink"))):
                    def heads(name):
                        return wc(name, i * P, (i + 1) * P).rearrange("p (h d) -> p h d", h=H)[:, None].to_broadcast([P, B, H, DH])

                    def angle(name):
                        return wc(name).rearrange("p (b d) -> p b d", b=B)[:, :, None].to_broadcast([P, B, H, DH])
                    o = dst[:, :, i * P:(i + 1) * P].rearrange("p b (h d) -> p b h d", h=H)
                    turned = rtmp[:].rearrange("p b (h d) -> p b h d", h=H)
                    chp.done(pool.tensor_tensor(o, heads(plain), angle(c_), ALU.mult))
                    chp.done(pool.tensor_tensor(turned, heads(swapped), angle(s_), ALU.mult))
                    chp.wait()
                    chp.done(pool.tensor_tensor(o, o, turned, ALU.add))
                    chp.wait()
            chp.done(pool.tensor_copy(bb2[:, :, 2 * P:], wc("bqkv2", 2 * P, 3 * P)[:, None].to_broadcast([P, B, P])))
            chp.wait()
            pool.memset(acc[:], 0.0).then_inc(s_rot, 1)

        @block.tensor
        def _(pe):
            pe.wait_ge(s_w, 16)
            pe.matmul(ps[:, 0, 0:P], wc("Wv0"), wc("Wf0"), start=True, stop=True)
            pe.matmul(ps[:, 0, P:P + 1], wc("Wf0"), wc("bv0"), start=True, stop=True).then_inc(s_set_pe, 1)
            pe.wait_ge(s_set_v, 2)

            def projections(p, i):
                pe.wait_ge(m[f"xs{p}"], 8 * (i - p) + 16)
                pe.matmul(bank(p, 0)[0:KD], wc("Wq0"), xs[:, p, :], start=True, stop=True)
                pe.matmul(bank(p, 1)[0:KD], wc("Wk0"), xs[:, p, :], start=True, stop=True).then_inc(m["qkp"], 1)
                for c in range(4):
                    x = pe.matmul(bank(p, 2)[:, c * P:(c + 1) * P], xs[:, p, c * P:(c + 1) * P], gM[:], start=True, stop=True)
                x.then_inc(m["vtp"], 1)

            def energies(p, i):
                pe.wait_ge(m["qk0"], 2 * i + 2)
                for b in range(2):
                    for c in range(2):
                        x = pe.matmul(bank(p, b)[:, c * N:(c + 1) * N], q0[:, p, b * N + c * P:b * N + (c + 1) * P],
                                      k0[:, p, b * N:(b + 1) * N], start=True, stop=True)
                x.then_inc(m["ep"], 1)

            def transposes(p, i):
                pe.wait_ge(m["an"], i + 1)
                pe.wait_ge(m["vt0"], i + 1)
                for b in range(2):
                    for jt in range(2):
                        for c in range(2):
                            x = pe.transpose(bank(p, 2 + b)[:, jt * N + c * P:jt * N + (c + 1) * P],
                                             A0[:, p, 2 * b + c, jt * P:(jt + 1) * P], ident)
                    x.then_inc(m["atp"], 1)

            def fused(p, i):
                pe.wait_ge(m["at0a"], i + 1)
                pe.wait_ge(m["at0v"], i + 1)
                for b in range(2):
                    o = bank(p, 0)[:, b * N:(b + 1) * N]
                    pe.matmul(o, wc("Wf0"), xs[:, p, b * N:(b + 1) * N], start=True, stop=False)
                    pe.matmul(o, vT0[:, p, 2 * b, :], AT0[:, p, 2 * b, :], start=False, stop=False)
                    x = pe.matmul(o, vT0[:, p, 2 * b + 1, :], AT0[:, p, 2 * b + 1, :], start=False, stop=True)
                x.then_inc(m["fp"], 1)

            def projections1(p, i):
                pe.wait_ge(m["x1"], i + 1)
                for c in range(4):
                    x = pe.matmul(bank(p, c)[:, 0:272], x1[:, p, c * P:(c + 1) * P], wc("W1"), start=True, stop=True)
                x.then_inc(m["prp"], 1)

            def keys1(p, i):
                pe.wait_ge(m["pr"], i + 1)
                pe.matmul(bank(p, 0)[0:KD], wc("We1"), x1[:, p, :], start=True, stop=True).then_inc(m["kep"], 1)

            def energies1(p, i):
                pe.wait_ge(m["vd"], i + 1)
                for b in range(2):
                    for c in range(2):
                        x = pe.matmul(bank(p, 1)[:, b * KD:(b + 1) * KD], vd1[:, p, 2 * b + c, :], pr1[:, p, 2 * b + c, 256:272],
                                      start=c == 0, stop=c == 1)
                x.then_inc(m["e1p"], 1)

            def transposes1(p, i):
                pe.wait_ge(m["a1"], i + 1)
                for b in range(2):
                    x = pe.transpose(bank(p, 2)[0:KD, b * P:(b + 1) * P], a1[:, p, b, :], ident)
                x.then_inc(m["a1p"], 1)

            def tokens(p, i):
                pe.wait_ge(m["aT1"], i + 1)
                pe.wait_ge(m["ke"], i + 1)
                for c in range(4):
                    o = bank(p, 3)[:, c * P:(c + 1) * P]
                    pe.matmul(o, x1[:, p, c * P:(c + 1) * P], ident, start=True, stop=False)
                    x = pe.matmul(o, ke1[:, p, c * P:(c + 1) * P], aT1[:, p, c // 2, :], start=False, stop=True)
                x.then_inc(m["tp"], 1)

            with pe.Fori(0, 2) as j:
                in_step((projections, energies, transposes, fused, projections1, keys1, energies1, transposes1, tokens), j)
                pe.wait_ge(m["tdone"], 2 * j + 2)

        @block.scalar
        def _(act):
            act.wait_ge(s_set_v, 3)
            act.preload_act_table(ACT.Exp)

            def values(p, i):
                act.wait_ge(m["vtp"], i + 1)
                act.activation(vT0[:, p], bank(p, 2).rearrange("p (a b) -> p a b", a=4), ACT.Copy).then_inc(m["vt0"], 1)

            def exponentials(p, i):
                act.wait_ge(m["nm"], i + 1)
                for c in range(4):
                    act.activation(A0[:, p, c, :], bank(p, c // 2)[:, (c % 2) * N:(c % 2 + 1) * N], ACT.Exp,
                                   bias=nm0[:, p, c:c + 1], accum_out=sm0[:, p, c:c + 1]).then_inc(m["ex"], 1)

            def copy(p, i):
                act.wait_ge(m["atp"], 2 * i + 1)
                act.activation(AT0[:, p, 0:2, :], bank(p, 2).rearrange("p (a b) -> p a b", a=2), ACT.Copy).then_inc(m["at0a"], 1)

            def norm_relu(p, i):
                act.wait_ge(m["fp"], i + 1)
                act.activation(x1[:, p, :], bank(p, 0), ACT.Relu, bias=bn_t[:], scale=bn_s[:]).then_inc(m["x1"], 1)

            def keys1(p, i):
                act.wait_ge(m["kep"], i + 1)
                act.activation(ke1[:, p, :], bank(p, 0)[0:KD], ACT.Identity, bias=wc("be1", rows=KD)).then_inc(m["ke"], 1)

            def gate_exp(p, i):
                act.wait_ge(m["z"], i + 1)
                act.activation(g1[:, p, :], g1[:, p, :], ACT.Exp, scale=-1.0 / QK1).then_inc(m["ez"], 1)

            def exponentials1(p, i):
                act.wait_ge(m["nm1"], i + 1)
                for b in range(2):
                    act.activation(a1[:, p, b, :], bank(p, 1)[:, b * KD:(b + 1) * KD], ACT.Exp, bias=nm1[:, p, b:b + 1],
                                   accum_out=sm1[:, p, b:b + 1]).then_inc(m["ex1"], 1)

            with act.Fori(0, 2) as j:
                in_step((values, exponentials, copy, norm_relu, gate_exp, keys1, exponentials1), j)

        @block.vector
        def _(dve):
            chv.engine = dve
            dve.wait_ge(s_w, 16)
            dve.tensor_copy(identb[:], ident).then_inc(s_id, 1)
            dve.wait_ge(s_set_pe, 1)
            dve.tensor_scalar(gM[:], ps[:, 0, 0:P], wc("gamma"), None, ALU.mult).then_inc(s_set_v, 1)
            dve.tensor_scalar(bn_t[:], ps[:, 0, P:P + 1], wc("gamma"), wc("bn_mean"), ALU.mult, ALU.subtract).then_inc(s_set_v, 1)
            dve.wait_ge(s_set_p, 1)
            dve.wait_ge(s_set_v, 2)
            dve.tensor_scalar(bn_t[:], bn_t[:], bn_s[:], wc("bn_b"), ALU.mult, ALU.add).then_inc(s_set_v, 1)

            def queries_keys(p, i):
                dve.wait_ge(m["qkp"], i + 1)
                dve.tensor_scalar(q0[:, p, :], bank(p, 0)[0:KD], wc("bq0", rows=KD), None, ALU.add).then_inc(m["qk0"], 1)
                dve.tensor_scalar(k0[:, p, :], bank(p, 1)[0:KD], wc("bk0", rows=KD), None, ALU.add).then_inc(m["qk0"], 1)

            def maxima(p, i):
                dve.wait_ge(m["ep"], i + 1)
                dve.tensor_reduce(nm0[:, p, :], banks(p, 0, 2).rearrange("p a (i n) -> p (a i) n", i=2), AX.X, ALU.max,
                                  negate=True).then_inc(m["nm"], 1)

            def normalise(p, i):
                dve.wait_ge(m["ex"], 4 * i + 4)
                chv.done(dve.reciprocal(sm0[:, p, :], sm0[:, p, :]))
                chv.wait()
                dve.tensor_tensor(A0[:, p], A0[:, p], sm0[:, p, :, None].to_broadcast([P, 4, N]), ALU.mult).then_inc(m["an"], 1)

            def copy(p, i):
                dve.wait_ge(m["atp"], 2 * i + 2)
                dve.tensor_copy(AT0[:, p, 2:4, :], bank(p, 3).rearrange("p (a b) -> p a b", a=2)).then_inc(m["at0v"], 1)

            def projected1(p, i):
                dve.wait_ge(m["prp"], i + 1)
                dve.tensor_tensor(pr1[:, p], banks(p, 0, 4)[:, :, 0:272], wc("bias1")[:, None].to_broadcast([P, 4, 272]), ALU.add).then_inc(m["pr"], 1)
                dve.wait_ge(m["pr"], i + 1)
                chv.done(dve.tensor_tensor(qk1[:, p], pr1[:, p, :, 0:QK1], pr1[:, p, :, QK1:2 * QK1], ALU.mult))
                chv.wait()
                dve.tensor_reduce(g1[:, p, :], qk1[:, p], AX.X, ALU.add).then_inc(m["z"], 1)

            def gate(p, i):
                dve.wait_ge(m["ez"], i + 1)
                chv.done(dve.tensor_scalar(g1[:, p, :], g1[:, p, :], 1.0, None, ALU.add))
                chv.wait()
                chv.done(dve.reciprocal(g1[:, p, :], g1[:, p, :]))
                chv.wait()
                dve.tensor_tensor(vd1[:, p], pr1[:, p, :, 2 * QK1:2 * QK1 + P], g1[:, p, :, None].to_broadcast([P, 4, P]), ALU.mult).then_inc(m["vd"], 1)

            def maxima1(p, i):
                dve.wait_ge(m["e1p"], i + 1)
                dve.tensor_reduce(nm1[:, p, :], bank(p, 1)[:, 0:2 * KD].rearrange("p (b k) -> p b k", b=2), AX.X, ALU.max,
                                  negate=True).then_inc(m["nm1"], 1)

            def normalise1(p, i):
                dve.wait_ge(m["ex1"], 2 * i + 2)
                chv.done(dve.reciprocal(sm1[:, p, :], sm1[:, p, :]))
                chv.wait()
                dve.tensor_tensor(a1[:, p], a1[:, p], sm1[:, p, :, None].to_broadcast([P, 2, KD]), ALU.mult).then_inc(m["a1"], 1)

            def copy1(p, i):
                dve.wait_ge(m["a1p"], i + 1)
                dve.tensor_copy(aT1[:, p], bank(p, 2)[0:KD, 0:2 * P].rearrange("p (b c) -> p b c", b=2)).then_inc(m["aT1"], 1)

            def tokens(p, i):
                dve.wait_ge(m["tp"], i + 1)
                dve.tensor_copy(t[:, :, bass.ds(2 * i, 2), :].rearrange("p s b c -> p b s c"),
                                bank(p, 3).rearrange("p (b s c) -> p b s c", b=2, s=2)).then_inc(m["tdone"], 1)

            with dve.Fori(0, 2) as j:
                chv.loop(j, 10)
                in_step((queries_keys, maxima, normalise, copy, projected1, gate, maxima1, normalise1, copy1, tokens), j)
            chv.end(2)

        room.close()
        qkv = own("qkv", [P, S, B, 3 * P])
        prd = own("prd", [P, B, P])
        prp = own("prp", [P, 2, B, P])
        sc2 = own("sc2", [P, S, B, B, H])
        mx2 = own("mx2", [P, S, B, H])
        o2 = own("o2", [P, S, B, P])
        oT2 = own("oT2", [P, S, BLK])
        ln = {n: sem("ln_" + n) for n in "var rst nrm".split()}

        def ln_statistics(dve, ch, n):
            for s in range(S):
                for b in range(B):
                    k = dve.bn_stats(stats[:, s, b, :], t[:, s, b, :])
                ch.done(k)
            for s in range(S):
                ch.wait()
                for b in range(B):
                    k = dve.bn_aggr(mv[:, s, b, :], stats[:, s, b, :])
                ch.done(k)
            for s in range(S):
                ch.wait()
                dve.tensor_scalar(var[:, s, :], mv[:, s, :, 1], LN_EPS, None, ALU.add).then_inc(ln["var"], 1)

        def ln_apply(dve, n):
            for s in range(S):
                dve.wait_ge(ln["rst"], S * n + s + 1)
                for b in range(B):
                    k = dve.tensor_scalar(xc[:, s, b, :], t[:, s, b, :], mv[:, s, b, 0:1], rstd[:, s, b:b + 1], ALU.subtract, ALU.mult)
                k.then_inc(ln["nrm"], 1)

        def ln_pool(pool, n):
            for s in range(S):
                pool.wait_ge(ln["var"], S * n + s + 1)
                pool.tensor_tensor(rstd[:, s, :], var[:, s, :], halfs[:], ALU.pow).then_inc(ln["rst"], 1)

        def add_bias(pool, n, name, done):
            for s in range(S):
                pool.wait_ge(ln["nrm"], S * n + s + 1)
                ts = t[:, s]
                pool.tensor_tensor(ts, ts, wc(name)[:, None].to_broadcast([P, B, P]), ALU.add).then_inc(done, 1)

        def flat(banks):
            return banks.rearrange("p a b -> p (a b)")

        def ln_transposes(pe, n, done):
            for s in range(S):
                pe.wait_ge(ln["nrm"], S * n + s + 1)
                for b in range(B):
                    x = pe.transpose(ps[:, 2 * s + b // 4, (b % 4) * P:(b % 4 + 1) * P], xc[:, s, b, :], ident)
                x.then_inc(done, 1)

        def ln_copies(act, n, transposed, done):
            for s in range(S):
                act.wait_ge(transposed, s + 1)
                act.activation(lnT[:, s, :], flat(ps[:, 2 * s:2 * s + 2, :]), ACT.Copy).then_inc(done, 1)

        m2 = {n: sem("at2_" + n) for n in "ltp lt qp qkv ep e pn pp red otp ot op done tbo".split()}
        block2 = room.enter_context(nc.Block())
        OTB2, FB2 = (0, 4), (2, 6)

        def weighted(engine, s, q, out):
            return engine.tensor_tensor(out.rearrange("p k (h d) -> p k h d", h=H),
                                        qkv[:, s, :, 2 * P:3 * P].rearrange("p k (h d) -> p k h d", h=H),
                                        sc2[:, s, q][:, :, :, None].to_broadcast([P, B, H, DH]), ALU.mult)

        def multiplied(engine, s, q, out):
            return engine.tensor_tensor(out, qkv[:, s, :, P:2 * P], qkv[:, s, q, 0:P][:, None].to_broadcast([P, B, P]), ALU.mult)

        @block2.gpsimd
        def _(pool):
            ln_pool(pool, 0)
            i = 0
            for s in range(S):
                for product, ready, count in ((multiplied, "qkv", 2), (weighted, "pn", 1)):
                    pool.wait_ge(m2[ready], count * (s + 1))
                    for q in range(1, B, 2):
                        if i >= 2:
                            pool.wait_ge(m2["red"], 2 * i - 2)
                        product(pool, s, q, prp[:, i % 2]).then_inc(m2["pp"], 1)
                        i += 1
                    if s == 0 and product is multiplied:
                        add_bias(pool, 0, "bo2", m2["tbo"])

        @block2.scalar
        def _(act):
            act.preload_act_table(ACT.Exp)
            ln_copies(act, 0, m2["ltp"], m2["lt"])
            for s in range(S):
                act.wait_ge(m2["ep"], s + 1)
                act.activation(sc2[:, s], sc2[:, s], ACT.Exp).then_inc(m2["e"], 1)
                act.wait_ge(m2["otp"], s + 1)
                act.activation(oT2[:, s, :], flat(ps[:, OTB2[s]:OTB2[s] + 2, :]), ACT.Copy).then_inc(m2["ot"], 1)

        @block2.tensor
        def _(pe):
            ln_transposes(pe, 0, m2["ltp"])
            pe.wait_ge(s_rot, 1)
            for s in range(S):
                for g in range(2):
                    if s == 0:
                        pe.wait_ge(m2["lt"], 2 if g else 1)
                    else:
                        pe.wait_ge(m2["qkv"], g + 1)
                    for b in range(4):
                        i = 4 * g + b
                        lhsT, o = lnT[:, s, i * P:(i + 1) * P], ps[:, 4 * (1 - g) + b, :]
                        pe.matmul(o[:, 0:2 * P], lhsT, wb2[:, i, :], start=True, stop=True)
                        x = pe.matmul(o[:, 2 * P:3 * P], lhsT, wc("Wqkv2", 2 * P, 3 * P), start=True, stop=True)
                    x.then_inc(m2["qp"], 1)
            pe.wait_ge(m2["qkv"], 4)
            for s in range(S):
                pe.wait_ge(m2["red"], 2 * B * (s + 1))
                for b in range(B):
                    x = pe.transpose(ps[:, OTB2[s] + b // 4, (b % 4) * P:(b % 4 + 1) * P], o2[:, s, b, :], ident)
                x.then_inc(m2["otp"], 1)
                pe.wait_ge(m2["ot"], s + 1)
                for b in range(B):
                    x = pe.matmul(ps[:, FB2[s] + b // 4, (b % 4) * P:(b % 4 + 1) * P], oT2[:, s, b * P:(b + 1) * P], wc("Wo2"),
                                  start=True, stop=True)
                x.then_inc(m2["op"], 1)

        @block2.vector
        def _(dve):
            chv.engine = dve

            def projected(s, g):
                dve.wait_ge(m2["qp"], 2 * s + g + 1)
                at = 4 * (1 - g)
                dve.tensor_tensor(qkv[:, s, 4 * g:4 * g + 4, :], ps[:, at:at + 4, 0:3 * P], bb2[:, 4 * g:4 * g + 4, :],
                                  ALU.add).then_inc(m2["qkv"], 1)

            def rounds2(n, s, product, total):
                for q in range(B):
                    i = n + q
                    if q % 2 == 0:
                        if i:
                            dve.wait_ge(m2["red"], i)
                        chv.done(product(dve, s, q, prd[:]))
                        chv.wait()
                        total(s, q, prd[:]).then_inc(m2["red"], 1)
                    else:
                        dve.wait_ge(m2["pp"], i // 2 + 1)
                        total(s, q, prp[:, i // 2 % 2]).then_inc(m2["red"], 1)

            def over_width(s, q, src):
                return dve.tensor_reduce(sc2[:, s, q], src.rearrange("p k (h d) -> p k h d", h=H), AX.X, ALU.add)

            def over_images(s, q, src):
                return dve.tensor_reduce(o2[:, s, q], src.rearrange("p k e -> p e k"), AX.X, ALU.add)

            def centre(s):
                dve.wait_ge(m2["red"], (2 * s + 1) * B)
                sc = sc2[:, s]
                chv.done(dve.tensor_reduce(mx2[:, s], sc.rearrange("p q k h -> p q h k"), AX.X, ALU.max))
                chv.wait()
                dve.tensor_tensor(sc, sc, mx2[:, s][:, :, None].to_broadcast([P, B, B, H]), ALU.subtract).then_inc(m2["ep"], 1)

            def normalise(s):
                dve.wait_ge(m2["e"], s + 1)
                chv.done(dve.tensor_reduce(mx2[:, s], sc2[:, s].rearrange("p q k h -> p q h k"), AX.X, ALU.add))
                chv.wait()
                chv.done(dve.reciprocal(mx2[:, s], mx2[:, s]))
                chv.wait()
                dve.tensor_tensor(sc2[:, s], sc2[:, s], mx2[:, s][:, :, None].to_broadcast([P, B, B, H]), ALU.mult).then_inc(m2["pn"], 1)
                dve.wait_ge(m2["pn"], s + 1)

            def add(s):
                dve.wait_ge(m2["op"], s + 1)
                dve.wait_ge(m2["tbo"], s + 1)
                ts = t[:, s]
                dve.tensor_tensor(ts, ts, ps[:, FB2[s]:FB2[s] + 2, :].rearrange("p a (b c) -> p (a b) c", c=P), ALU.add).then_inc(m2["done"], 1)

            ln_statistics(dve, chv, 0)
            ln_apply(dve, 0)
            projected(0, 0)
            projected(0, 1)
            dve.wait_ge(m2["qkv"], 2)
            rounds2(0, 0, multiplied, over_width)
            centre(0)
            projected(1, 0)
            projected(1, 1)
            normalise(0)
            rounds2(B, 0, weighted, over_images)
            rounds2(2 * B, 1, multiplied, over_width)
            centre(1)
            add(0)
            normalise(1)
            rounds2(3 * B, 1, weighted, over_images)
            add(1)

        gs = {n: sem("gate_" + n) for n in "ltp lt xl lgp ep e g gp gT st".split()}

        def gate_feature_major(xT, s):
            return xT[:].rearrange("p (b s n) -> p b s n", b=B, s=S)[:, :, s, :]

        def experts(layer, w_in, n_up, hid, gate_w, gate_b):
            hc = hid // P
            wcols = (n_up + 1) * hid
            n_bias = hc + 1 if layer == 0 else 0
            room.close()
            R = S * B
            lg = own(f"lg_{layer}", [P, R, E])
            pg = own(f"pg_{layer}", [P, R, E])
            gmx = own(f"gmx_{layer}", [P, R])
            cmp = own(f"cmp_{layer}", [P, R, E, E])
            cmq = own(f"cmq_{layer}", [P, R, E, E])
            gT = own(f"gT_{layer}", [E, S, BLK])
            wraw = own(f"wraw_{layer}", [P, 2, wcols + n_bias])
            wH = own(f"wH_{layer}", [P, 2, wcols], F32R)
            wL = own(f"wL_{layer}", [P, 2, wcols], F32R)
            bias = own(f"bias_{layer}", [P, 2, hc + 1])
            G = own(f"G_{layer}", [P, 2, T])
            hraw = own(f"hraw_{layer}", [P, 2, hc, CH])
            hH = own(f"hH_{layer}", [P, 2, hc, CH], F32R)
            hL = own(f"hL_{layer}", [P, 2, hc, CH], F32R)
            yg = own(f"yg_{layer}", [P, 2, CH])
            def rounds(engine):
                with engine.Fori(0, E // 2 - 1) as j:
                    for k in range(2 * NCH):
                        yield j, k, False
                for k in range(2 * NCH):
                    yield E // 2 - 1, k, True

            z = {n: sem(f"ex{layer}_" + n) for n in "split wH hp act hm hH hl yp yg acc".split()}
            zw = [[sem(f"ex{layer}_w{p}"), sem(f"ex{layer}_g{p}")] for p in range(2)]
            fin = {n: sem(f"fin{layer}_" + n) for n in "tp done st".split()}
            nn = 1 + 2 * layer
            blk = room.enter_context(nc.Block())

            @blk.sync
            def _(sp):
                def weights(j, p):
                    sp.wait_ge(z["split"], 2 * j + p + 1)
                    sp.dma_start(wraw[:, p, :], w_in[bass.ds(2 * j + p, 1)].rearrange("e p n -> p (e n)")).then_inc(zw[p][0], 16)

                def gates(j, p):
                    e = 2 * j + p
                    sp.wait_ge(z["yg"], NCH * e + 1)
                    sp.dma_start(G[:, p, :], gd[layer][bass.ds(e, 1), :].to_broadcast([P, T])).then_inc(zw[p][1], 16)

                weights(0, 0)
                weights(0, 1)
                for s in range(S):
                    sp.wait_ge(gs["gT"], S * layer + s + 1)
                    sp.dma_start(gd[layer].rearrange("e (b s n) -> e b s n", b=B, s=S)[:, :, s, :],
                                 gT[:, s, :].rearrange("e (b n) -> e b n", b=B)).then_inc(gs["st"], 16)
                sp.wait_ge(gs["st"], 16 * S * (layer + 1))
                gates(0, 0)
                gates(0, 1)
                with sp.Fori(1, E // 2) as j:
                    for p in range(2):
                        weights(j, p)
                        gates(j, p)
                if layer == 1:
                    for c in range(NCH):
                        sp.wait_ge(fin["done"], c + 1)
                        sp.dma_start(out.rearrange("b c n -> c b n")[:, 2 * c:2 * c + 2, :],
                                     acc[:, c * CH:(c + 1) * CH].rearrange("c (b n) -> c b n", b=2)).then_inc(fin["st"], 16)
                    sp.wait_ge(fin["st"], 16 * NCH)

            @blk.gpsimd
            def _(pool):
                pool.sem_inc(z["split"], FREE_W)
                chp.engine = pool
                ln_pool(pool, nn)
                if layer == 1:
                    chp.done(pool.memset(acc[:], 0.0))
                    chp.wait()
                pool.sem_inc(z["acc"], FREE_ACC)

                def lower(j, p):
                    pool.wait_ge(z["wH"], 2 * j + p + 1)
                    pool.tensor_tensor(wL[:, p, 0:wcols], wraw[:, p, 0:wcols], wH[:, p, 0:wcols].bitcast(F32), ALU.subtract).then_inc(z["split"], 1)

                lower(0, 0)
                for j, k, last in rounds(pool):
                    if k == 1:
                        lower(j, 1)
                    if k == NCH + 1 and not last:
                        lower(j + 1, 0)
                    c = k % NCH
                    pool.wait_ge(z["yg"], 2 * NCH * j + k + 1 + FREE_Y)
                    pool.tensor_tensor(acc[:, c * CH:(c + 1) * CH], acc[:, c * CH:(c + 1) * CH], yg[:, k % 2, :], ALU.add).then_inc(z["acc"], 1)

            @blk.scalar
            def _(act):
                act.preload_act_table(ACT.Exp)
                for s in range(S):
                    act.wait_ge(gs["ltp"], S * layer + s + 1)
                    act.activation(lnT[:, s, :], flat(ps[:, 2 * s:2 * s + 2, :]), ACT.Copy).then_inc(gs["lt"], 1)
                act.wait_ge(gs["ep"], layer + 1)
                act.activation(pg[:], lg[:], ACT.Exp).then_inc(gs["e"], 1)
                act.preload_act_table(ACT.Gelu if layer == 0 else ACT.Silu)
                for j, k, last in rounds(act):
                    item = 2 * NCH * j + k
                    act.wait_ge(z["hl"], 2 * (item - 1) + FREE_H)
                    for h in range(hc):
                        act.wait_ge(z["hp"], item * hc + h + 1)
                        if layer == 0:
                            act.activation(hraw[:, k % 2, h, :], ps[:, h, :], ACT.Gelu,
                                           bias=bias[:, k // NCH, h:h + 1]).then_inc(z["act"], 1)
                        else:
                            act.activation(hraw[:, k % 2, h, :], ps[:, 2 * h, :], ACT.Silu).then_inc(z["act"], 1)

            @blk.tensor
            def _(pe):
                ln_transposes(pe, nn, gs["ltp"])
                LGB, GTB = 6, 6
                for s in range(S):
                    pe.wait_ge(gs["lt"], S * layer + s + 1)
                    for b in range(B):
                        r = s * B + b
                        x = pe.matmul(ps[:, LGB, r * E:(r + 1) * E], lnT[:, s, b * P:(b + 1) * P], wc(gate_w), start=True, stop=True)
                x.then_inc(gs["lgp"], 1)

                def gates_transposed():
                    pe.wait_ge(gs["g"], layer + 1)
                    for s in range(S):
                        if s:
                            pe.wait_ge(gs["gT"], S * layer + s)
                        for b in range(B):
                            x = pe.transpose(ps[0:E, GTB + b // 4, (b % 4) * P:(b % 4 + 1) * P], lg[:, s * B + b, :], ident)
                        x.then_inc(gs["gp"], 1)

                pe.wait_ge(gs["xl"], S * (layer + 1))
                pe.sem_inc(z["yp"], FREE_Y)

                def up(j, k):
                    item, p = 2 * NCH * j + k, k // NCH % 2
                    xa, xb = xH[:, (k % NCH) * CH:(k % NCH + 1) * CH], xL[:, (k % NCH) * CH:(k % NCH + 1) * CH]
                    if k % NCH == 0:
                        pe.wait_ge(z["split"], 2 * j + k // NCH + 1 + FREE_W)
                    for h in range(hc):
                        if not (isinstance(item, int) and item == 0):
                            pe.wait_ge(z["act"] if layer == 0 else z["hm"], (item - 1) * hc + h + 1)
                        for u in range(n_up):
                            at = u * hid + h * P
                            o = ps[:, n_up * h + u, :]
                            pe.matmul(o, wH[:, p, at:at + P], xa, start=True, stop=False)
                            pe.matmul(o, wH[:, p, at:at + P], xb, start=False, stop=False)
                            x = pe.matmul(o, wL[:, p, at:at + P], xa, start=False, stop=True)
                        x.then_inc(z["hp"], 1)

                def down(j, k):
                    item, p = 2 * NCH * j + k, k // NCH
                    pe.wait_ge(z["yg"], item - 1 + FREE_Y)
                    pe.wait_ge(z["hl"], 2 * (item + 1) + FREE_H)
                    for h in range(hc):
                        at = n_up * hid + h * P
                        o = ps[:, 4 + k % 2, :]
                        pe.matmul(o, wH[:, p, at:at + P], hH[:, k % 2, h, :], start=h == 0, stop=False)
                        pe.matmul(o, wH[:, p, at:at + P], hL[:, k % 2, h, :], start=False, stop=False)
                        x = pe.matmul(o, wL[:, p, at:at + P], hH[:, k % 2, h, :], start=False, stop=h == hc - 1)
                    x.then_inc(z["yp"], 1)

                up(0, 0)
                gates_transposed()
                for j, k, last in rounds(pe):
                    if not (last and k == 2 * NCH - 1):
                        up(j, k + 1)
                    down(j, k)
                if layer == 0:
                    pe.wait_ge(z["acc"], E * NCH + FREE_ACC)
                    for s in range(S):
                        for b in range(B):
                            x = pe.transpose(ps[:, 2 * s + b // 4, (b % 4) * P:(b % 4 + 1) * P],
                                             acc[:, (b * S + s) * P:(b * S + s + 1) * P], ident)
                        x.then_inc(fin["tp"], 1)
                else:
                    pe.wait_ge(z["yg"], E * NCH + FREE_Y)
                    for c in range(NCH):
                        for i in range(4):
                            x = pe.transpose(ps[:, c, i * P:(i + 1) * P], t[:, i % 2, 2 * c + i // 2, :], ident)
                        x.then_inc(fin["tp"], 1)

            @blk.vector
            def _(dve):
                chv.engine = dve
                ln_statistics(dve, chv, nn)
                ln_apply(dve, nn)
                for s in range(S):
                    dve.wait_ge(gs["lt"], S * layer + s + 1)
                    lnv = lnT[:, s, :].rearrange("p (b n) -> p b n", b=B)
                    chv.done(dve.tensor_copy(gate_feature_major(xH, s), lnv))
                    chv.wait()
                    dve.tensor_tensor(gate_feature_major(xL, s), lnv, gate_feature_major(xH, s).bitcast(F32), ALU.subtract).then_inc(gs["xl"], 1)
                half = hc // 2

                def upper(j, p):
                    dve.wait_ge(zw[p][0], 16 * (j + 1))
                    if not isinstance(j, int) or j > 0:
                        dve.wait_ge(z["yp"], NCH * (2 * j + p - 1) + FREE_Y)
                    if layer == 0:
                        dve.tensor_copy(bias[:, p, :], wraw[:, p, wcols:])
                    dve.tensor_copy(wH[:, p, 0:wcols], wraw[:, p, 0:wcols]).then_inc(z["wH"], 1)

                upper(0, 0)
                dve.wait_ge(gs["lgp"], layer + 1)
                lgb = ps[:, 6, 0:R * E].rearrange("p (r e) -> p r e", r=R)
                if gate_b is None:
                    chv.done(dve.tensor_copy(lg[:], lgb))
                else:
                    chv.done(dve.tensor_tensor(lg[:], lgb, wc(gate_b)[:, None].to_broadcast([P, R, E]), ALU.add))
                chv.wait()
                chv.done(dve.tensor_reduce(gmx[:], lg[:], AX.X, ALU.max))
                chv.wait()
                dve.tensor_tensor(lg[:], lg[:], gmx[:, :, None].to_broadcast([P, R, E]), ALU.subtract).then_inc(gs["ep"], 1)
                dve.wait_ge(gs["e"], layer + 1)
                chv.done(dve.tensor_reduce(gmx[:], pg[:], AX.X, ALU.add))
                chv.wait()
                chv.done(dve.reciprocal(gmx[:], gmx[:]))
                chv.wait()
                chv.done(dve.tensor_tensor(pg[:], pg[:], gmx[:, :, None].to_broadcast([P, R, E]), ALU.mult))
                chv.wait()
                pi = pg[:][:, :, :, None].to_broadcast([P, R, E, E])
                pj = pg[:][:, :, None, :].to_broadcast([P, R, E, E])
                chv.done(dve.tensor_tensor(cmp[:], pj, pi, ALU.is_equal))
                chv.done(dve.tensor_tensor(cmq[:], pj, pi, ALU.is_gt))
                chv.wait()
                chv.done(dve.tensor_tensor(cmp[:], cmp[:], wc("earlier").rearrange("p (i j) -> p i j", i=E)[:, None].to_broadcast([P, R, E, E]), ALU.mult))
                chv.wait()
                chv.done(dve.tensor_tensor(cmp[:], cmp[:], cmq[:], ALU.add))
                chv.wait()
                chv.done(dve.tensor_reduce(lg[:], cmp[:], AX.X, ALU.add))
                chv.wait()
                k = dve.scalar_tensor_tensor(lg[:], lg[:], TOPK - 0.5, pg[:], ALU.is_lt, ALU.mult)
                if layer == 0:
                    k.then_inc(gs["g"], 1)
                else:
                    chv.done(k)
                    chv.wait()
                    chv.done(dve.tensor_reduce(gmx[:], lg[:], AX.X, ALU.add))
                    chv.wait()
                    chv.done(dve.reciprocal(gmx[:], gmx[:]))
                    chv.wait()
                    dve.tensor_tensor(lg[:], lg[:], gmx[:, :, None].to_broadcast([P, R, E]), ALU.mult).then_inc(gs["g"], 1)
                for s in range(S):
                    dve.wait_ge(gs["gp"], S * layer + s + 1)
                    dve.tensor_copy(gT[:, s, :].rearrange("p (a b) -> p a b", a=2), ps[0:E, 6:8, :]).then_inc(gs["gT"], 1)
                dve.sem_inc(z["hl"], FREE_H)
                dve.sem_inc(z["yg"], FREE_Y)
                def gated(j, k):
                    item, p, c = 2 * NCH * j + k, k // NCH, k % NCH
                    dve.wait_ge(z["yp"], item + 1 + FREE_Y)
                    if c == 0:
                        dve.wait_ge(zw[p][1], 16 * (j + 1))
                    dve.wait_ge(z["acc"], item - 1 + FREE_ACC)
                    gsl = G[:, p, c * CH:(c + 1) * CH]
                    if layer == 0:
                        dve.scalar_tensor_tensor(yg[:, k % 2, :], ps[:, 4 + k % 2, :], bias[:, p, hc:hc + 1],
                                                 gsl, ALU.add, ALU.mult).then_inc(z["yg"], 1)
                    else:
                        dve.tensor_tensor(yg[:, k % 2, :], ps[:, 4 + k % 2, :], gsl, ALU.mult).then_inc(z["yg"], 1)

                for j, k, last in rounds(dve):
                    item = 2 * NCH * j + k
                    if layer == 1:
                        for h in range(hc):
                            dve.wait_ge(z["act"], item * hc + h + 1)
                            dve.tensor_tensor(hraw[:, k % 2, h, :], hraw[:, k % 2, h, :], ps[:, 2 * h + 1, :], ALU.mult).then_inc(z["hm"], 1)
                    for g in range(2):
                        dve.wait_ge(z["act"] if layer == 0 else z["hm"], item * hc + (g + 1) * half)
                        if g == 0:
                            dve.wait_ge(z["yp"], item - 1 + FREE_Y)
                        src, hi = hraw[:, k % 2, g * half:(g + 1) * half, :], hH[:, k % 2, g * half:(g + 1) * half, :]
                        dve.tensor_copy(hi, src).then_inc(z["hH"], 1)
                        dve.wait_ge(z["hH"], 2 * item + g + 1)
                        dve.tensor_tensor(hL[:, k % 2, g * half:(g + 1) * half, :], src, hi.bitcast(F32), ALU.subtract).then_inc(z["hl"], 1)
                    if k > 0:
                        gated(j, k - 1)
                    if k == 1:
                        upper(j, 1)
                    if k == NCH + 1 and not last:
                        upper(j + 1, 0)
                    if k == 2 * NCH - 1:
                        gated(j, k)
                if layer == 0:
                    for s in range(S):
                        dve.wait_ge(fin["tp"], s + 1)
                        dve.tensor_tensor(t[:, s], t[:, s], ps[:, 2 * s:2 * s + 2, :].rearrange("p a (b c) -> p (a b) c", c=P), ALU.add).then_inc(fin["done"], 1)
                    dve.wait_ge(fin["done"], S)
                else:
                    dve.wait_ge(z["acc"], E * NCH + FREE_ACC)
                    for c in range(NCH):
                        dve.wait_ge(fin["tp"], c + 1)
                        dve.tensor_tensor(acc[:, c * CH:(c + 1) * CH], acc[:, c * CH:(c + 1) * CH], ps[:, c, :], ALU.add).then_inc(fin["done"], 1)

        experts(0, a["ex2"], 1, F2, "gate2", "gateb2")

        room.close()
        wq3H, wq3L = own("wq3H", [P, 2 * P], F32R), own("wq3L", [P, 2 * P], F32R)
        wk3H, wk3L = own("wk3H", [P, 2 * P], F32R), own("wk3L", [P, 2 * P], F32R)
        wv3H, wv3L = own("wv3H", [P, P], F32R), own("wv3L", [P, P], F32R)
        wo3 = own("wo3", [P, 3, P], BF16)
        wtmp = own("wtmp", [P, P])
        q3H, q3L = own("q3H", [P, 2, N], F32R), own("q3L", [P, 2, N], F32R)
        k3H, k3S = own("k3H", [P, 2, N], F32R), own("k3S", [P, 2, N], F32R)
        v3r = own("v3r", [P, 2, S, P])
        vp3 = own("vp3", [P, B, S, H, 3, DH], BF16)
        mx3 = own("mx3", [P, H // 2, 2 * S])
        sm3 = own("sm3", [P, H // 2, 2 * S])
        smb3 = own("smb3", [P, H // 2, 2 * S], BF16)
        s3 = own("s3", [P, 2, 2 * S, N], BF16)
        p3 = own("p3", [P, 2, 2 * S, N], BF16)
        pT3 = own("pT3", [P, 2, 2, S, N], BF16)
        o3b = own("o3b", [P, S, P], BF16)
        oT3 = own("oT3", [P, N], BF16)
        m3 = {n: sem("at3_" + n) for n in
              "wl wo ltp lt xl vp vb vr v2 v qkp kh ks sp sb sub ex p tp pt op o otp ot fp done tbo".split()}
        block4 = room.enter_context(nc.Block())
        QKB, TB, SB, OB = 0, 1, 2, 6

        def images(engine, step):
            for g in range(4):
                step(0, g, True, False)
            with engine.Fori(1, B - 1) as b:
                for g in range(4):
                    step(b, g, False, False)
            for g in range(4):
                step(B - 1, g, False, True)

        def ahead(b, g, n):
            return (b, g + n) if g + n < 4 else (b + 1, g + n - 4)

        def by_head(x):
            return x.rearrange("p s (h d) -> p s h d", h=H)

        @block4.gpsimd
        def _(pool):
            ln_pool(pool, 2)
            add_bias(pool, 2, "bo3", m3["tbo"])
            for b in range(B):
                pool.wait_ge(m3["v2"], b + 1)
                pool.tensor_tensor(vp3[:, b, :, :, 2, :], by_head(v3r[:, b % 2]), vp3[:, b, :, :, 1, :], ALU.subtract).then_inc(m3["v"], 1)

        @block4.scalar
        def _(act):
            act.preload_act_table(ACT.Exp)
            ln_copies(act, 2, m3["ltp"], m3["lt"])

            def qk(n, g):
                act.wait_ge(m3["qkp"], n + 1)
                act.activation(q3H[:, g, :], ps[:, QKB, 0:N], ACT.Copy, scale=DH ** -0.5)
                act.activation(k3H[:, g, :], ps[:, QKB, N:2 * N], ACT.Copy).then_inc(m3["kh"], 1)

            def rounded(b, g):
                i = 4 * b + g
                act.wait_ge(m3["sp"], i + 1)
                if not (isinstance(b, int) and i < 2):
                    act.wait_ge(m3["ex"], 4 * (i - 1))
                act.activation(s3[:, g % 2], ps[:, SB + 2 * (g % 2):SB + 2 * (g % 2) + 2, :].rearrange("p a (s n) -> p (a s) n", s=2), ACT.Copy).then_inc(m3["sb"], 1)

            def exponentials(b, g):
                i = 4 * b + g
                act.wait_ge(m3["sub"], 4 * i + 4)
                if not (isinstance(b, int) and i < 2):
                    act.wait_ge(m3["tp"], i - 1)
                for r in range(4):
                    act.activation(p3[:, g % 2, r, :], s3[:, g % 2, r, :], ACT.Exp, accum_out=sm3[:, g, r:r + 1]).then_inc(m3["ex"], 1)

            def evacuate(b, g):
                i = 4 * b + g
                act.wait_ge(m3["tp"], i + 1)
                if not (isinstance(b, int) and i < 2):
                    act.wait_ge(m3["op"], i - 1)
                act.activation(pT3[:, g % 2].rearrange("p h k n -> p (h k n)"), psb(TB), ACT.Copy).then_inc(m3["pt"], 1)

            qk(0, 0)
            qk(1, 1)
            for b in range(B):
                act.wait_ge(m3["vp"], b + 1)
                act.activation(vp3[:, b, :, :, 0, :], by_head(ps[:, 4 + b % 4, 0:N].rearrange("p (s c) -> p s c", s=S)),
                               ACT.Copy).then_inc(m3["vb"], 1)
            rounded(0, 0)
            rounded(0, 1)
            exponentials(0, 0)

            def step(b, g, first, last):
                if not (last and g >= 2):
                    rounded(*ahead(b, g, 2))
                if not (first and g == 0):
                    evacuate(*((b, g - 1) if g else (b - 1, 3)))
                if not (last and g == 3):
                    exponentials(*ahead(b, g, 1))
                if g % 2 == 0 and not last:
                    qk(2 * b + 2 + g // 2, g // 2)
            images(act, step)
            evacuate(B - 1, 3)

        @block4.tensor
        def _(pe):
            ln_transposes(pe, 2, m3["ltp"])
            pe.wait_ge(m3["wl"], 3)
            pe.wait_ge(m3["wo"], 1)
            pe.wait_ge(m3["xl"], S)

            def qk(b, g):
                n = 2 * b + g
                if not (isinstance(b, int) and n == 0):
                    pe.wait_ge(m3["ks"], n)
                xa, xb = xH[:, bass.ds(b * N, N)], xL[:, bass.ds(b * N, N)]
                for i, (wh, wl) in enumerate(((wq3H, wq3L), (wk3H, wk3L))):
                    o, c = ps[:, QKB, i * N:(i + 1) * N], slice(g * P, (g + 1) * P)
                    pe.matmul(o, wh[:, c], xa, start=True, stop=False)
                    pe.matmul(o, wh[:, c], xb, start=False, stop=False)
                    x = pe.matmul(o, wl[:, c], xa, start=False, stop=True)
                x.then_inc(m3["qkp"], 1)

            def scores(b, g):
                i = 4 * b + g
                if g % 2 == 0:
                    pe.wait_ge(m3["ks"], 2 * b + g // 2 + 1)
                if not (isinstance(b, int) and i < 2):
                    pe.wait_ge(m3["sb"], i - 1)
                for h in (2 * g, 2 * g + 1):
                    r, q = 32 * (h % 4), h // 4
                    for s in range(S):
                        o = ps[:, SB + 2 * (g % 2) + h % 2, s * N:(s + 1) * N]
                        pe.matmul(o, q3H[r:r + 32, q, s * P:(s + 1) * P], k3S[r:r + 32, q, :], start=True, stop=False)
                        x = pe.matmul(o, q3L[r:r + 32, q, s * P:(s + 1) * P], k3S[r:r + 32, q, :], start=False, stop=True)
                x.then_inc(m3["sp"], 1)

            def transposed(b, g):
                i = 4 * b + g
                pe.wait_ge(m3["p"], 4 * i + 4)
                if not (isinstance(b, int) and i == 0):
                    pe.wait_ge(m3["pt"], i)
                if g in (1, 2) and not (isinstance(b, int) and b == 0):
                    pe.wait_ge(m3["ot" if g == 1 else "done"], b)
                for h in range(2):
                    for kt in range(S):
                        for s in range(S):
                            x = pe.transpose(psb(TB)[:, ((h * S + kt) * S + s) * P:((h * S + kt) * S + s + 1) * P],
                                             p3[:, g % 2, h * S + s, kt * P:(kt + 1) * P], identb[:])
                x.then_inc(m3["tp"], 1)

            def values(b, g):
                i = 4 * b + g
                pe.wait_ge(m3["pt"], i + 1)
                if g == 0 and not (isinstance(b, int) and b == 0):
                    pe.wait_ge(m3["o"], b)
                for h in (2 * g, 2 * g + 1):
                    for s in range(S):
                        for kt in range(S):
                            v = vp3[:, bass.ds(b, 1), kt, h].rearrange("p b a d -> p (b a d)")
                            x = pe.matmul(ps[:, OB + s, h * 48:(h + 1) * 48], pT3[:, g % 2, h % 2, kt, s * P:(s + 1) * P], v,
                                          start=kt == 0, stop=kt == 1)
                x.then_inc(m3["op"], 1)

            def out_transposed(b):
                pe.wait_ge(m3["o"], b + 1)
                for s in range(S):
                    x = pe.transpose(psb(TB)[:, s * P:(s + 1) * P], o3b[:, s, :], identb[:])
                x.then_inc(m3["otp"], 1)

            def final(b):
                pe.wait_ge(m3["ot"], b + 1)
                for s in range(S):
                    for i in range(3):
                        x = pe.matmul(ps[:, TB, s * P:(s + 1) * P], oT3[:, s * P:(s + 1) * P], wo3[:, i, :], start=i == 0, stop=i == 2)
                x.then_inc(m3["fp"], 1)

            qk(0, 0)
            for b in range(B):
                if b >= 4:
                    pe.wait_ge(m3["vr"], b - 3)
                for s in range(S):
                    o, c = ps[:, 4 + b % 4, s * P:(s + 1) * P], slice(b * N + s * P, b * N + (s + 1) * P)
                    pe.matmul(o, xH[:, c], wv3H[:], start=True, stop=False)
                    pe.matmul(o, xL[:, c], wv3H[:], start=False, stop=False)
                    x = pe.matmul(o, xH[:, c], wv3L[:], start=False, stop=True)
                x.then_inc(m3["vp"], 1)
                if b == 0:
                    qk(0, 1)
            scores(0, 0)
            pe.wait_ge(m3["v"], B)
            scores(0, 1)
            scores(0, 2)

            def step(b, g, first, last):
                if not (last and g >= 1):
                    scores(*ahead(b, g, 3))
                if g % 2 == 0 and not last:
                    qk(b + 1, g // 2)
                if not (first and g == 0):
                    values(*((b, g - 1) if g else (b - 1, 3)))
                if g == 1 and not first:
                    out_transposed(b - 1)
                if g == 2 and not first:
                    final(b - 1)
                transposed(b, g)
            images(pe, step)
            values(B - 1, 3)
            out_transposed(B - 1)
            final(B - 1)

        @block4.vector
        def _(dve):
            chv.engine = dve
            ln_statistics(dve, chv, 2)
            for name, wh, wl in (("Wq3", wq3H, wq3L), ("Wk3", wk3H, wk3L), ("Wv3", wv3H, wv3L)):
                chv.done(dve.tensor_copy(wh[:], wc(name)))
                chv.wait()
                dve.tensor_tensor(wl[:], wc(name), wh[:].bitcast(F32), ALU.subtract).then_inc(m3["wl"], 1)
            chv.done(dve.tensor_copy(wo3[:, 0], wc("Wo3")))
            chv.wait()
            chv.done(dve.tensor_tensor(wtmp[:], wc("Wo3"), wo3[:, 0], ALU.subtract))
            chv.wait()
            chv.done(dve.tensor_copy(wo3[:, 1], wtmp[:]))
            chv.wait()
            dve.tensor_tensor(wo3[:, 2], wtmp[:], wo3[:, 1], ALU.subtract).then_inc(m3["wo"], 1)
            ln_apply(dve, 2)
            for s in range(S):
                dve.wait_ge(m3["lt"], s + 1)
                lnv = lnT[:, s, :].rearrange("p (b n) -> p b n", b=B)
                chv.done(dve.tensor_copy(gate_feature_major(xH, s), lnv))
                chv.wait()
                dve.tensor_tensor(gate_feature_major(xL, s), lnv, gate_feature_major(xH, s).bitcast(F32), ALU.subtract).then_inc(m3["xl"], 1)

            def qk(n, g):
                dve.wait_ge(m3["kh"], n + 1)
                dve.scalar_tensor_tensor(q3L[:, g, :], ps[:, QKB, 0:N], DH ** -0.5, q3H[:, g, :].bitcast(F32), ALU.mult, ALU.subtract)
                dve.scalar_tensor_tensor(k3S[:, g, :], k3H[:, g, :].bitcast(F32), wc("kmask"), ps[:, QKB, N:2 * N],
                                         ALU.mult, ALU.add).then_inc(m3["ks"], 1)

            def centre(b, g):
                dve.wait_ge(m3["sb"], 4 * b + g + 1)
                chv.done(dve.tensor_reduce(mx3[:, g, :], s3[:, g % 2], AX.X, ALU.max))
                chv.wait()
                for r in range(4):
                    dve.tensor_scalar(s3[:, g % 2, r, :], s3[:, g % 2, r, :], mx3[:, g, r:r + 1], None, ALU.subtract).then_inc(m3["sub"], 1)

            def normalise(b, g):
                dve.wait_ge(m3["ex"], 4 * (4 * b + g) + 4)
                chv.done(dve.tensor_copy(smb3[:, g, :], sm3[:, g, :]))
                chv.wait()
                chv.done(dve.reciprocal(sm3[:, g, :], smb3[:, g, :]))
                chv.wait()
                for r in range(4):
                    dve.tensor_scalar(p3[:, g % 2, r, :], p3[:, g % 2, r, :], sm3[:, g, r:r + 1], None, ALU.mult).then_inc(m3["p"], 1)

            def gather(b):
                dve.wait_ge(m3["op"], 4 * b + 4)
                if not isinstance(b, int) or b > 0:
                    dve.wait_ge(m3["otp"], b)
                with nc.allow_low_precision(reason="the reference's output here is bfloat16; the sum itself is float32"):
                    dve.tensor_reduce(by_head(o3b[:]), ps[:, OB:OB + 2, 0:384].rearrange("p s (h a d) -> p s h d a", h=H, a=3),
                                      AX.X, ALU.add).then_inc(m3["o"], 1)

            def copy_out(b):
                dve.wait_ge(m3["otp"], b + 1)
                if not isinstance(b, int) or b > 0:
                    dve.wait_ge(m3["fp"], b)
                dve.tensor_copy(oT3[:], psb(TB)[:, 0:N]).then_inc(m3["ot"], 1)

            def add(b):
                dve.wait_ge(m3["fp"], b + 1)
                tb = t[:, :, bass.ds(b, 1), :].rearrange("p s b c -> p s (b c)")
                dve.tensor_tensor(tb, tb, ps[:, TB, 0:N].rearrange("p (s c) -> p s c", s=S), ALU.add).then_inc(m3["done"], 1)

            def split_values(b):
                dve.wait_ge(m3["vb"], b + 1)
                if b >= 2:
                    dve.wait_ge(m3["v"], b - 1)
                dve.tensor_tensor(by_head(v3r[:, b % 2]), by_head(ps[:, 4 + b % 4, 0:N].rearrange("p (s c) -> p s c", s=S)),
                                  vp3[:, b, :, :, 0, :], ALU.subtract).then_inc(m3["vr"], 1)
                dve.wait_ge(m3["vr"], b + 1)
                dve.tensor_copy(vp3[:, b, :, :, 1, :], by_head(v3r[:, b % 2])).then_inc(m3["v2"], 1)

            qk(0, 0)
            qk(1, 1)
            for b in range(B):
                split_values(b)
            centre(0, 0)

            def step(b, g, first, last):
                if not (last and g == 3):
                    centre(*ahead(b, g, 1))
                normalise(b, g)
                if g == 2 and not first:
                    add(b - 1)
                if g % 2 == 0 and not last:
                    qk(2 * b + 2 + g // 2, g // 2)
                if g == 0 and not first:
                    gather(b - 1)
                if g == 1 and not first:
                    copy_out(b - 1)
            dve.wait_ge(m3["tbo"], S)
            for g in range(4):
                step(0, g, True, False)
            with dve.Fori(1, B - 1) as b:
                chv.loop(b - 1, 12)
                for g in range(4):
                    step(b, g, False, False)
            chv.end(B - 2)
            for g in range(4):
                step(B - 1, g, False, True)
            gather(B - 1)
            copy_out(B - 1)
            add(B - 1)

        experts(1, a["ex3"], 2, F3, "router3", None)
        room.close()


def _layout(inp):
    def rows(v):
        return np.tile(np.asarray(v).reshape(1, -1), (P, 1))

    def col(v):
        v = np.asarray(v).reshape(-1, 1)
        return np.concatenate([v, np.zeros((P - len(v), 1), np.float32)])

    def swap(x):
        y = x.reshape(*x.shape[:-1], -1, 2, DH // 2)[..., ::-1, :]
        return y.reshape(x.shape)

    def slots(x):
        return np.repeat(x.reshape(P, H, 1, DH), 2, axis=2).reshape(P, 2 * H * DH)

    f = (np.arange(B, dtype=np.float64)[:, None] / 10000.0 ** (np.arange(0, DH, 2) / DH)[None, :]).astype(np.float32)
    cos = np.cos(np.concatenate([f, f], 1))
    sin = np.sin(np.concatenate([-f, f], 1))
    wq, wk, wv = (inp[f"L2_attn_W{n}"].T for n in "qkv")
    bq, bk, bv = (inp[f"L2_attn_b{n}"] for n in "qkv")
    parts = {
        "Wq0": inp["L0_conv_Wq"].T, "Wk0": inp["L0_conv_Wk"].T, "Wv0": inp["L0_conv_Wv"], "Wf0": inp["L0_conv_Wf"].T,
        "W1": np.concatenate([inp[f"L1_conv_W{n}"].T for n in "qkvs"], 1), "We1": inp["L1_conv_We"].T,
        "Wqkv2": np.concatenate([wq, wk, wv], 1), "Wqk2r": np.concatenate([swap(wq), swap(wk)], 1),
        "Wo2": inp["L2_attn_Wo"].T, "gate2": inp["L2_ffn_gate_w"],
        "Wq3": slots(inp["L3_attn_Wq"]), "Wk3": slots(inp["L3_attn_Wkv"][:, :P]), "Wv3": inp["L3_attn_Wkv"][:, P:],
        "Wo3": inp["L3_attn_Wo"], "router3": inp["L3_ffn_router_w"], "ident": np.eye(P),
        "bv0": col(inp["L0_conv_bv"]), "bn_w": col(inp["L0_conv_bn_w"]), "bn_b": col(inp["L0_conv_bn_b"]),
        "bn_mean": col(inp["L0_conv_bn_mean"]), "bn_var": col(inp["L0_conv_bn_var"]),
        "bq0": col(inp["L0_conv_bq"]), "bk0": col(inp["L0_conv_bk"]), "be1": col(inp["L1_conv_be"]),
        "gamma": rows(inp["L0_conv_gamma"]),
        "kmask": np.where(np.arange(P) % (2 * DH) < DH, 0.0, -1.0)[:, None],
        "bias1": rows(np.concatenate([inp[f"L1_conv_b{n}"] for n in "qkvs"])),
        "bqkv2": rows(np.concatenate([bq, bk, bv])), "bqk2r": rows(np.concatenate([swap(bq), swap(bk)])),
        "bo2": rows(inp["L2_attn_bo"]), "gateb2": rows(inp["L2_ffn_gate_b"]), "bo3": rows(inp["L3_attn_bo"]),
        "cosq": rows(cos * DH ** -0.5), "sinq": rows(sin * DH ** -0.5), "cosk": rows(cos), "sink": rows(sin),
        "earlier": rows(np.tril(np.ones((E, E)), -1)),
    }
    pack = np.concatenate([np.asarray(parts[n], np.float32) for n, _ in PACK], 1)

    def down(x, hid):
        return x.reshape(E, hid // P, P, P).transpose(0, 2, 1, 3).reshape(E, P, hid)
    ex2 = np.concatenate([inp["L2_ffn_w1"], down(inp["L2_ffn_w2"], F2), inp["L2_ffn_b1"].reshape(E, F2 // P, P).transpose(0, 2, 1),
                          inp["L2_ffn_b2"][:, :, None]], 2)
    ex3 = np.concatenate([inp["L3_ffn_w1"], inp["L3_ffn_w3"], down(inp["L3_ffn_w2"], F3)], 2)
    return {"pack": pack, "x": inp["x"].reshape(B, P, N), "ex2": ex2, "ex3": ex3}


def kernel(**inputs):
    from concourse import bacc
    from concourse.bass_utils import run_bass_kernel_spmd

    arrays = {k: np.ascontiguousarray(v) for k, v in _layout({k: np.asarray(v) for k, v in inputs.items()}).items()}
    nc = bacc.Bacc("TRN2", target_bir_lowering=False, num_devices=1)
    args = {k: nc.dram_tensor(f"in_{k}", v.shape, mybir.dt.from_np(v.dtype), kind="ExternalInput").ap() for k, v in arrays.items()}
    out = nc.dram_tensor("out", (B, P, N), F32, kind="ExternalOutput").ap()
    build(nc, args, out)
    r = run_bass_kernel_spmd(nc, [{f"in_{k}": v for k, v in arrays.items()}], core_ids=[0])
    return r.results[0]["out"].reshape(B, P, 16, 16)
```

```python
from contextlib import ExitStack

import numpy as np

import concourse.bass as bass
from concourse import mybir

F32 = mybir.dt.float32
F32R = mybir.dt.float32r
BF16 = mybir.dt.bfloat16
ALU = mybir.AluOpType
ACT = mybir.ActivationFunctionType
AX = mybir.AxisListType

P = 128
B = 8
N = 256
S = N // P
T = B * N
H, DH = 8, 16
KD = 16
QK1 = 64
E = 8
TOPK = 2
F2 = 512
F3 = 256
CH = 512
NCH = T // CH
BLK = B * P
FREE_W = 2
FREE_ACC = 2
FREE_H = 3
FREE_Y = NCH + 1
BN_EPS = 1e-5
LN_EPS = 1e-5

PACK = [
    ("Wq0", KD), ("Wk0", KD), ("Wv0", P), ("Wf0", P), ("W1", 2 * QK1 + P + KD), ("We1", KD), ("ident", P),
    ("bv0", 1), ("bn_w", 1), ("bn_b", 1), ("bn_mean", 1), ("bn_var", 1), ("bq0", 1), ("bk0", 1), ("be1", 1),
    ("gamma", 1), ("bias1", 2 * QK1 + P + KD),
    ("Wqkv2", 3 * P), ("Wqk2r", 2 * P), ("Wo2", P), ("gate2", E),
    ("Wq3", 2 * P), ("Wk3", 2 * P), ("Wv3", P), ("Wo3", P), ("router3", E), ("kmask", 1),
    ("bqkv2", 3 * P), ("bqk2r", 2 * P), ("bo2", P), ("gateb2", E),
    ("bo3", P), ("cosq", B * DH), ("sinq", B * DH), ("cosk", B * DH), ("sink", B * DH),
]
AT = {}
_at = 0
for _name, _w in PACK:
    AT[_name] = (_at, _at + _w)
    _at += _w
NPACK = _at


class Chain:

    def __init__(self, engine, sem):
        self.engine, self.sem, self.base, self.n, self.total = engine, sem, None, 0, 0

    def done(self, ins):
        ins.then_inc(self.sem, 1)
        self.n += 1
        return ins

    def wait(self):
        if self.base is None:
            self.engine.wait_ge(self.sem, self.total + self.n)
        else:
            self.engine.wait_ge(self.sem, self.base + self.n)

    def loop(self, i, per):
        self.total += self.n
        self.base, self.n, self.per = i * per + self.total, 0, per

    def end(self, times):
        assert self.n == self.per, (self.n, self.per)
        self.total += times * self.per
        self.base, self.n = None, 0


def build(nc, a, out):
    ctx = ExitStack()
    with ctx:
        def sb(name, shape, dt=F32):
            return ctx.enter_context(nc.sbuf_tensor(name, shape, dt))

        def sem(name):
            return ctx.enter_context(nc.semaphore(name))

        ps = ctx.enter_context(nc.psum_tensor("ps", [P, 8, CH], F32))

        def psb(bank):
            return ps[:, bank, :].bitcast(BF16)

        w = sb("w", [P, NPACK])

        def wc(name, lo=0, hi=None, rows=P):
            x, y = AT[name]
            return w[0:rows, x + lo:(y if hi is None else x + hi)]

        ident = wc("ident")
        identb = sb("identb", [P, P], BF16)
        t = sb("t", [P, S, B, P])
        halfs = sb("halfs", [P, B])
        stats = sb("stats", [P, S, B, 6])
        mv = sb("mv", [P, S, B, 2])
        var = sb("var", [P, S, B])
        rstd = sb("rstd", [P, S, B])
        xc = sb("xc", [P, S, B, P])
        lnT = sb("lnT", [P, S, BLK])
        xH = sb("xH", [P, T], F32R)
        xL = sb("xL", [P, T], F32R)
        acc = sb("acc", [P, T])
        gd = nc.dram_tensor("gates_scratch", [2, E, T], F32, kind="Internal").ap()
        wb2 = sb("wb2", [P, B, 2 * P])
        bb2 = sb("bb2", [P, B, 3 * P])

        room = ExitStack()

        def own(name, shape, dt=F32):
            return room.enter_context(nc.sbuf_tensor(name, shape, dt))

        s_w, s_w2 = sem("packed_loaded"), sem("rest_loaded")
        s_set_pe, s_set_v, s_set_p = sem("setup_pe"), sem("setup_dve"), sem("setup_pool")
        s_rot = sem("rotated_ready")
        dve_s, pool_s = sem("dve_steps"), sem("pool_steps")

        xs = own("xs", [P, 2, CH])
        rtmp = own("rtmp", [P, B, P])
        gM = own("gM", [P, P])
        bn_inv, bn_s, bn_t = (own(n, [P, 1]) for n in ("bn_inv", "bn_s", "bn_t"))
        q0 = own("q0", [KD, 2, CH])
        k0 = own("k0", [KD, 2, CH])
        vT0 = own("vT0", [P, 2, 4, P])
        nm0 = own("nm0", [P, 2, 4])
        sm0 = own("sm0", [P, 2, 4])
        A0 = own("A0", [P, 2, 4, N])
        AT0 = own("AT0", [P, 2, 4, N])
        x1 = own("x1", [P, 2, CH])
        pr1 = own("pr1", [P, 2, 4, 272])
        ke1 = own("ke1", [KD, 2, CH])
        qk1 = own("qk1", [P, 2, 4, QK1])
        g1 = own("g1", [P, 2, 4])
        vd1 = own("vd1", [P, 2, 4, P])
        nm1 = own("nm1", [P, 2, 2])
        sm1 = own("sm1", [P, 2, 2])
        a1 = own("a1", [P, 2, 2, KD])
        aT1 = own("aT1", [KD, 2, 2, P])
        names = ("xs0 xs1 qkp qk0 vtp vt0 ep nm ex an atp at0a at0v fp x1 prp pr kep ke z ez vd e1p nm1 ex1 a1 "
                 "a1p aT1 tp tdone").split()
        m = {n: sem("l01_" + n) for n in names}
        block = room.enter_context(nc.Block())
        chv, chp = Chain(None, dve_s), Chain(None, pool_s)

        def in_step(steps, j):
            for step in steps:
                for p in range(2):
                    step(p, 2 * j + p)

        def bank(p, k):
            return ps[:, 4 * p + k, :]

        def banks(p, lo, hi):
            return ps[:, 4 * p + lo:4 * p + hi, :]

        @block.sync
        def _(sp):
            early = AT["bias1"][1]
            sp.dma_start(w[:, 0:early], a["pack"][:, 0:early]).then_inc(s_w, 16)

            def images_in(p, i):
                sp.dma_start(xs[:, p, :].rearrange("c (b n) -> c b n", b=2),
                             a["x"][bass.ds(2 * i, 2)].rearrange("b c n -> c b n")).then_inc(m[f"xs{p}"], 16)
            images_in(0, 0)
            images_in(1, 1)
            sp.dma_start(w[:, early:], a["pack"][:, early:]).then_inc(s_w2, 16)
            for p in range(2):
                sp.wait_ge(m["fp"], p + 1)
                images_in(p, 2 + p)

        @block.gpsimd
        def _(pool):
            chp.engine = pool
            chp.done(pool.memset(halfs[:], -0.5))
            pool.wait_ge(s_w, 16)
            chp.done(pool.tensor_scalar(bn_s[:], wc("bn_var"), BN_EPS, None, ALU.add))
            chp.wait()
            chp.done(pool.tensor_tensor(bn_inv[:], bn_s[:], halfs[:, 0:1], ALU.pow))
            chp.wait()
            pool.tensor_tensor(bn_s[:], wc("bn_w"), bn_inv[:], ALU.mult).then_inc(s_set_p, 1)
            pool.wait_ge(s_w2, 16)
            for dst, plain, swapped in ((wb2, "Wqkv2", "Wqk2r"), (bb2, "bqkv2", "bqk2r")):
                for i, (c_, s_) in enumerate((("cosq", "sinq"), ("cosk", "sink"))):
                    def heads(name):
                        return wc(name, i * P, (i + 1) * P).rearrange("p (h d) -> p h d", h=H)[:, None].to_broadcast([P, B, H, DH])

                    def angle(name):
                        return wc(name).rearrange("p (b d) -> p b d", b=B)[:, :, None].to_broadcast([P, B, H, DH])
                    o = dst[:, :, i * P:(i + 1) * P].rearrange("p b (h d) -> p b h d", h=H)
                    turned = rtmp[:].rearrange("p b (h d) -> p b h d", h=H)
                    chp.done(pool.tensor_tensor(o, heads(plain), angle(c_), ALU.mult))
                    chp.done(pool.tensor_tensor(turned, heads(swapped), angle(s_), ALU.mult))
                    chp.wait()
                    chp.done(pool.tensor_tensor(o, o, turned, ALU.add))
                    chp.wait()
            chp.done(pool.tensor_copy(bb2[:, :, 2 * P:], wc("bqkv2", 2 * P, 3 * P)[:, None].to_broadcast([P, B, P])))
            chp.wait()
            pool.memset(acc[:], 0.0).then_inc(s_rot, 1)

        @block.tensor
        def _(pe):
            pe.wait_ge(s_w, 16)
            pe.matmul(ps[:, 0, 0:P], wc("Wv0"), wc("Wf0"), start=True, stop=True)
            pe.matmul(ps[:, 0, P:P + 1], wc("Wf0"), wc("bv0"), start=True, stop=True).then_inc(s_set_pe, 1)
            pe.wait_ge(s_set_v, 2)

            def projections(p, i):
                pe.wait_ge(m[f"xs{p}"], 8 * (i - p) + 16)
                pe.matmul(bank(p, 0)[0:KD], wc("Wq0"), xs[:, p, :], start=True, stop=True)
                pe.matmul(bank(p, 1)[0:KD], wc("Wk0"), xs[:, p, :], start=True, stop=True).then_inc(m["qkp"], 1)
                for c in range(4):
                    x = pe.matmul(bank(p, 2)[:, c * P:(c + 1) * P], xs[:, p, c * P:(c + 1) * P], gM[:], start=True, stop=True)
                x.then_inc(m["vtp"], 1)

            def energies(p, i):
                pe.wait_ge(m["qk0"], 2 * i + 2)
                for b in range(2):
                    for c in range(2):
                        x = pe.matmul(bank(p, b)[:, c * N:(c + 1) * N], q0[:, p, b * N + c * P:b * N + (c + 1) * P],
                                      k0[:, p, b * N:(b + 1) * N], start=True, stop=True)
                x.then_inc(m["ep"], 1)

            def transposes(p, i):
                pe.wait_ge(m["an"], i + 1)
                pe.wait_ge(m["vt0"], i + 1)
                pe.wait_ge(m["tdone"], i + 1)
                for b in range(2):
                    for jt in range(2):
                        for c in range(2):
                            x = pe.transpose(bank(p, 2 + b)[:, jt * N + c * P:jt * N + (c + 1) * P],
                                             A0[:, p, 2 * b + c, jt * P:(jt + 1) * P], ident)
                    x.then_inc(m["atp"], 1)

            def fused(p, i):
                pe.wait_ge(m["at0a"], i + 1)
                pe.wait_ge(m["at0v"], i + 1)
                for b in range(2):
                    o = bank(p, 0)[:, b * N:(b + 1) * N]
                    pe.matmul(o, wc("Wf0"), xs[:, p, b * N:(b + 1) * N], start=True, stop=False)
                    pe.matmul(o, vT0[:, p, 2 * b, :], AT0[:, p, 2 * b, :], start=False, stop=False)
                    x = pe.matmul(o, vT0[:, p, 2 * b + 1, :], AT0[:, p, 2 * b + 1, :], start=False, stop=True)
                x.then_inc(m["fp"], 1)

            def projections1(p, i):
                pe.wait_ge(m["x1"], i + 1)
                for c in range(4):
                    x = pe.matmul(bank(p, c)[:, 0:272], x1[:, p, c * P:(c + 1) * P], wc("W1"), start=True, stop=True)
                x.then_inc(m["prp"], 1)

            def keys1(p, i):
                pe.wait_ge(m["pr"], i + 1)
                pe.matmul(bank(p, 0)[0:KD], wc("We1"), x1[:, p, :], start=True, stop=True).then_inc(m["kep"], 1)

            def energies1(p, i):
                pe.wait_ge(m["vd"], i + 1)
                for b in range(2):
                    for c in range(2):
                        x = pe.matmul(bank(p, 1)[:, b * KD:(b + 1) * KD], vd1[:, p, 2 * b + c, :], pr1[:, p, 2 * b + c, 256:272],
                                      start=c == 0, stop=c == 1)
                x.then_inc(m["e1p"], 1)

            def transposes1(p, i):
                pe.wait_ge(m["a1"], i + 1)
                for b in range(2):
                    x = pe.transpose(bank(p, 2)[0:KD, b * P:(b + 1) * P], a1[:, p, b, :], ident)
                x.then_inc(m["a1p"], 1)

            def tokens(p, i):
                pe.wait_ge(m["aT1"], i + 1)
                pe.wait_ge(m["ke"], i + 1)
                for c in range(4):
                    o = bank(p, 3)[:, c * P:(c + 1) * P]
                    pe.matmul(o, x1[:, p, c * P:(c + 1) * P], ident, start=True, stop=False)
                    x = pe.matmul(o, ke1[:, p, c * P:(c + 1) * P], aT1[:, p, c // 2, :], start=False, stop=True)
                x.then_inc(m["tp"], 1)

            with pe.Fori(0, 2) as j:
                in_step((projections, energies, transposes, fused, projections1, keys1, energies1, transposes1, tokens), j)

        @block.scalar
        def _(act):
            act.wait_ge(s_set_v, 3)
            act.preload_act_table(ACT.Exp)

            def values(p, i):
                act.wait_ge(m["vtp"], i + 1)
                act.activation(vT0[:, p], bank(p, 2).rearrange("p (a b) -> p a b", a=4), ACT.Copy).then_inc(m["vt0"], 1)

            def exponentials(p, i):
                act.wait_ge(m["nm"], i + 1)
                for c in range(4):
                    act.activation(A0[:, p, c, :], bank(p, c // 2)[:, (c % 2) * N:(c % 2 + 1) * N], ACT.Exp,
                                   bias=nm0[:, p, c:c + 1], accum_out=sm0[:, p, c:c + 1]).then_inc(m["ex"], 1)

            def copy(p, i):
                act.wait_ge(m["atp"], 2 * i + 1)
                act.activation(AT0[:, p, 0:2, :], bank(p, 2).rearrange("p (a b) -> p a b", a=2), ACT.Copy).then_inc(m["at0a"], 1)

            def norm_relu(p, i):
                act.wait_ge(m["fp"], i + 1)
                act.activation(x1[:, p, :], bank(p, 0), ACT.Relu, bias=bn_t[:], scale=bn_s[:]).then_inc(m["x1"], 1)

            def keys1(p, i):
                act.wait_ge(m["kep"], i + 1)
                act.activation(ke1[:, p, :], bank(p, 0)[0:KD], ACT.Identity, bias=wc("be1", rows=KD)).then_inc(m["ke"], 1)

            def gate_exp(p, i):
                act.wait_ge(m["z"], i + 1)
                act.activation(g1[:, p, :], g1[:, p, :], ACT.Exp, scale=-1.0 / QK1).then_inc(m["ez"], 1)

            def exponentials1(p, i):
                act.wait_ge(m["nm1"], i + 1)
                for b in range(2):
                    act.activation(a1[:, p, b, :], bank(p, 1)[:, b * KD:(b + 1) * KD], ACT.Exp, bias=nm1[:, p, b:b + 1],
                                   accum_out=sm1[:, p, b:b + 1]).then_inc(m["ex1"], 1)

            with act.Fori(0, 2) as j:
                in_step((values, exponentials, copy, norm_relu, gate_exp, keys1, exponentials1), j)

        @block.vector
        def _(dve):
            chv.engine = dve
            dve.wait_ge(s_w, 16)
            dve.tensor_copy(identb[:], ident)
            dve.wait_ge(s_set_pe, 1)
            dve.tensor_scalar(gM[:], ps[:, 0, 0:P], wc("gamma"), None, ALU.mult).then_inc(s_set_v, 1)
            dve.tensor_scalar(bn_t[:], ps[:, 0, P:P + 1], wc("gamma"), wc("bn_mean"), ALU.mult, ALU.subtract).then_inc(s_set_v, 1)
            dve.wait_ge(s_set_p, 1)
            dve.wait_ge(s_set_v, 2)
            dve.tensor_scalar(bn_t[:], bn_t[:], bn_s[:], wc("bn_b"), ALU.mult, ALU.add).then_inc(s_set_v, 1)

            def queries_keys(p, i):
                dve.wait_ge(m["qkp"], i + 1)
                dve.tensor_scalar(q0[:, p, :], bank(p, 0)[0:KD], wc("bq0", rows=KD), None, ALU.add).then_inc(m["qk0"], 1)
                dve.tensor_scalar(k0[:, p, :], bank(p, 1)[0:KD], wc("bk0", rows=KD), None, ALU.add).then_inc(m["qk0"], 1)

            def maxima(p, i):
                dve.wait_ge(m["ep"], i + 1)
                dve.tensor_reduce(nm0[:, p, :], banks(p, 0, 2).rearrange("p a (i n) -> p (a i) n", i=2), AX.X, ALU.max,
                                  negate=True).then_inc(m["nm"], 1)

            def normalise(p, i):
                dve.wait_ge(m["ex"], 4 * i + 4)
                chv.done(dve.reciprocal(sm0[:, p, :], sm0[:, p, :]))
                chv.wait()
                dve.tensor_tensor(A0[:, p], A0[:, p], sm0[:, p, :, None].to_broadcast([P, 4, N]), ALU.mult).then_inc(m["an"], 1)

            def copy(p, i):
                dve.wait_ge(m["atp"], 2 * i + 2)
                dve.tensor_copy(AT0[:, p, 2:4, :], bank(p, 3).rearrange("p (a b) -> p a b", a=2)).then_inc(m["at0v"], 1)

            def projected1(p, i):
                dve.wait_ge(m["prp"], i + 1)
                dve.tensor_tensor(pr1[:, p], banks(p, 0, 4)[:, :, 0:272], wc("bias1")[:, None].to_broadcast([P, 4, 272]), ALU.add).then_inc(m["pr"], 1)
                dve.wait_ge(m["pr"], i + 1)
                chv.done(dve.tensor_tensor(qk1[:, p], pr1[:, p, :, 0:QK1], pr1[:, p, :, QK1:2 * QK1], ALU.mult))
                chv.wait()
                dve.tensor_reduce(g1[:, p, :], qk1[:, p], AX.X, ALU.add).then_inc(m["z"], 1)

            def gate(p, i):
                dve.wait_ge(m["ez"], i + 1)
                chv.done(dve.tensor_scalar(g1[:, p, :], g1[:, p, :], 1.0, None, ALU.add))
                chv.wait()
                chv.done(dve.reciprocal(g1[:, p, :], g1[:, p, :]))
                chv.wait()
                dve.tensor_tensor(vd1[:, p], pr1[:, p, :, 2 * QK1:2 * QK1 + P], g1[:, p, :, None].to_broadcast([P, 4, P]), ALU.mult).then_inc(m["vd"], 1)

            def maxima1(p, i):
                dve.wait_ge(m["e1p"], i + 1)
                dve.tensor_reduce(nm1[:, p, :], bank(p, 1)[:, 0:2 * KD].rearrange("p (b k) -> p b k", b=2), AX.X, ALU.max,
                                  negate=True).then_inc(m["nm1"], 1)

            def normalise1(p, i):
                dve.wait_ge(m["ex1"], 2 * i + 2)
                chv.done(dve.reciprocal(sm1[:, p, :], sm1[:, p, :]))
                chv.wait()
                dve.tensor_tensor(a1[:, p], a1[:, p], sm1[:, p, :, None].to_broadcast([P, 2, KD]), ALU.mult).then_inc(m["a1"], 1)

            def copy1(p, i):
                dve.wait_ge(m["a1p"], i + 1)
                dve.tensor_copy(aT1[:, p], bank(p, 2)[0:KD, 0:2 * P].rearrange("p (b c) -> p b c", b=2)).then_inc(m["aT1"], 1)

            def tokens(p, i):
                dve.wait_ge(m["tp"], i + 1)
                dve.tensor_copy(t[:, :, bass.ds(2 * i, 2), :].rearrange("p s b c -> p b s c"),
                                bank(p, 3).rearrange("p (b s c) -> p b s c", b=2, s=2)).then_inc(m["tdone"], 1)

            dve.sem_inc(m["tdone"], 2)
            with dve.Fori(0, 2) as j:
                chv.loop(j, 10)
                in_step((queries_keys, maxima, normalise, copy, projected1, gate, maxima1, normalise1, copy1, tokens), j)
            chv.end(2)

        room.close()
        qkv = own("qkv", [P, S, B, 3 * P])
        prd = own("prd", [P, 2, B, P])
        prp = own("prp", [P, 2, B, P])
        sc2 = own("sc2", [P, S, B, B, H])
        mx2 = own("mx2", [P, S, B, H])
        o2 = own("o2", [P, S, B, P])
        oT2 = own("oT2", [P, S, BLK])
        ln = {n: sem("ln_" + n) for n in "var rst nrm".split()}


        def ln_moments(dve, ch, halves, images=range(B)):
            for s in halves:
                for b in images:
                    k = dve.bn_stats(stats[:, s, b, :], t[:, s, b, :])
            ch.done(k)
            ch.wait()
            for s in halves:
                for b in images:
                    k = dve.bn_aggr(mv[:, s, b, :], stats[:, s, b, :])
            ch.done(k)

        def ln_variance(dve, ch, s):
            ch.wait()
            dve.tensor_scalar(var[:, s, :], mv[:, s, :, 1], LN_EPS, None, ALU.add).then_inc(ln["var"], 1)

        def ln_pool(pool, n, s):
            pool.wait_ge(ln["var"], S * n + s + 1)
            pool.tensor_tensor(rstd[:, s, :], var[:, s, :], halfs[:], ALU.pow).then_inc(ln["rst"], 1)

        def ln_apply(dve, n, s):
            dve.wait_ge(ln["rst"], S * n + s + 1)
            for b in range(B):
                k = dve.tensor_scalar(xc[:, s, b, :], t[:, s, b, :], mv[:, s, b, 0:1], rstd[:, s, b:b + 1], ALU.subtract, ALU.mult)
            k.then_inc(ln["nrm"], 1)

        def add_bias(pool, n, name, done):
            for s in range(S):
                pool.wait_ge(ln["nrm"], S * n + s + 1)
                ts = t[:, s]
                pool.tensor_tensor(ts, ts, wc(name)[:, None].to_broadcast([P, B, P]), ALU.add).then_inc(done, 1)

        def flat(banks):
            return banks.rearrange("p a b -> p (a b)")

        def ln_transposes(pe, n, done, s):
            pe.wait_ge(ln["nrm"], S * n + s + 1)
            for b in range(B):
                x = pe.transpose(ps[:, 2 * s + b // 4, (b % 4) * P:(b % 4 + 1) * P], xc[:, s, b, :], ident)
            x.then_inc(done, 1)

        def ln_copies(act, n, transposed, done):
            for s in range(S):
                act.wait_ge(transposed, s + 1)
                act.activation(lnT[:, s, :], flat(ps[:, 2 * s:2 * s + 2, :]), ACT.Copy).then_inc(done, 1)

        m2 = {n: sem("at2_" + n) for n in "ltp lt qp qkv ep e pn pp pd red pred otp ot op done tbo".split()}
        block2 = room.enter_context(nc.Block())
        OTB2, FB2 = (0, 4), (2, 6)
        POOLS, PES = (1, 3, 4, 6, 7), (0, 2, 5)

        def weighted(engine, s, q, out):
            return engine.tensor_tensor(out.rearrange("p k (h d) -> p k h d", h=H),
                                        qkv[:, s, :, 2 * P:3 * P].rearrange("p k (h d) -> p k h d", h=H),
                                        sc2[:, s, q][:, :, :, None].to_broadcast([P, B, H, DH]), ALU.mult)

        def multiplied(engine, s, q, out):
            return engine.tensor_tensor(out, qkv[:, s, :, P:2 * P], qkv[:, s, q, 0:P][:, None].to_broadcast([P, B, P]), ALU.mult)

        def red_after(s, which, q):
            before = (2 * B - len(PES)) * s + B * which
            return before + len([x for x in range(q + 1) if not (which and x in PES)])

        @block2.gpsimd
        def _(pool):
            for s in range(S):
                ln_pool(pool, 0, s)
            used = []
            for s in range(S):
                for which, (product, ready, count) in enumerate(((multiplied, "qkv", 2), (weighted, "pn", 1))):
                    pool.wait_ge(m2[ready], count * (s + 1))
                    for q in POOLS:
                        if len(used) >= 2:
                            pool.wait_ge(m2["red"], red_after(*used[-2]))
                        product(pool, s, q, prp[:, len(used) % 2]).then_inc(m2["pp"], 1)
                        used.append((s, which, q))
                    if s == 0 and which == 0:
                        add_bias(pool, 0, "bo2", m2["tbo"])
            ln_pool(pool, 1, 0)

        @block2.scalar
        def _(act):
            act.preload_act_table(ACT.Exp)
            ln_copies(act, 0, m2["ltp"], m2["lt"])
            for s in range(S):
                act.wait_ge(m2["ep"], s + 1)
                act.activation(sc2[:, s], sc2[:, s], ACT.Exp).then_inc(m2["e"], 1)
                act.wait_ge(m2["otp"], s + 1)
                act.activation(oT2[:, s, :], flat(ps[:, OTB2[s]:OTB2[s] + 2, :]), ACT.Copy).then_inc(m2["ot"], 1)

        @block2.tensor
        def _(pe):
            for s in range(S):
                ln_transposes(pe, 0, m2["ltp"], s)
            pe.wait_ge(s_rot, 1)
            for s in range(S):
                for g in range(2):
                    if s == 0:
                        pe.wait_ge(m2["lt"], 2 if g else 1)
                    else:
                        pe.wait_ge(m2["qkv"], g + 1)
                    for b in range(4):
                        i = 4 * g + b
                        lhsT, o = lnT[:, s, i * P:(i + 1) * P], ps[:, 4 * (1 - g) + b, :]
                        pe.matmul(o[:, 0:2 * P], lhsT, wb2[:, i, :], start=True, stop=True)
                        x = pe.matmul(o[:, 2 * P:3 * P], lhsT, wc("Wqkv2", 2 * P, 3 * P), start=True, stop=True)
                    x.then_inc(m2["qp"], 1)
            pe.wait_ge(m2["qkv"], 4)
            for s in range(S):
                for i, q in enumerate(PES):
                    pe.wait_ge(m2["pd"], len(PES) * s + i + 1)
                    o = ps[:, OTB2[s] + q // 4, (q % 4) * P:(q % 4 + 1) * P]
                    for k in range(B):
                        x = pe.matmul(o, prd[:, i % 2, k, :], ident, start=k == 0, stop=k == B - 1)
                    x.then_inc(m2["pred"], 1)
                pe.wait_ge(m2["red"], red_after(s, 1, B - 1))
                for q in range(B):
                    if q not in PES:
                        x = pe.transpose(ps[:, OTB2[s] + q // 4, (q % 4) * P:(q % 4 + 1) * P], o2[:, s, q, :], ident)
                x.then_inc(m2["otp"], 1)
                pe.wait_ge(m2["ot"], s + 1)
                for b in range(B):
                    x = pe.matmul(ps[:, FB2[s] + b // 4, (b % 4) * P:(b % 4 + 1) * P], oT2[:, s, b * P:(b + 1) * P], wc("Wo2"),
                                  start=True, stop=True)
                x.then_inc(m2["op"], 1)

        @block2.vector
        def _(dve):
            chv.engine = dve

            def projected(s, g):
                dve.wait_ge(m2["qp"], 2 * s + g + 1)
                at = 4 * (1 - g)
                dve.tensor_tensor(qkv[:, s, 4 * g:4 * g + 4, :], ps[:, at:at + 4, 0:3 * P], bb2[:, 4 * g:4 * g + 4, :],
                                  ALU.add).then_inc(m2["qkv"], 1)

            pooled, own_sums = [], []

            def rounds2(s, which, product, total):
                for q in range(B):
                    if q in POOLS:
                        dve.wait_ge(m2["pp"], len(pooled) + 1)
                        total(s, q, prp[:, len(pooled) % 2]).then_inc(m2["red"], 1)
                        pooled.append(q)
                    elif which and q in PES:
                        i = PES.index(q)
                        if i >= 2:
                            dve.wait_ge(m2["pred"], len(PES) * s + i - 1)
                        elif s:
                            dve.wait_ge(m2["pred"], len(PES))
                        product(dve, s, q, prd[:, i % 2]).then_inc(m2["pd"], 1)
                    else:
                        if own_sums:
                            dve.wait_ge(m2["red"], own_sums[-1])
                        if which == 0 and s:
                            dve.wait_ge(m2["pred"], len(PES))
                        chv.done(product(dve, s, q, prd[:, 0]))
                        chv.wait()
                        total(s, q, prd[:, 0]).then_inc(m2["red"], 1)
                        own_sums.append(red_after(s, which, q))

            def over_width(s, q, src):
                return dve.tensor_reduce(sc2[:, s, q], src.rearrange("p k (h d) -> p k h d", h=H), AX.X, ALU.add)

            def over_images(s, q, src):
                return dve.tensor_reduce(o2[:, s, q], src.rearrange("p k e -> p e k"), AX.X, ALU.add)

            def centre(s):
                dve.wait_ge(m2["red"], red_after(s, 0, B - 1))
                sc = sc2[:, s]
                chv.done(dve.tensor_reduce(mx2[:, s], sc.rearrange("p q k h -> p q h k"), AX.X, ALU.max))
                chv.wait()
                dve.tensor_tensor(sc, sc, mx2[:, s][:, :, None].to_broadcast([P, B, B, H]), ALU.subtract).then_inc(m2["ep"], 1)

            def normalise(s):
                dve.wait_ge(m2["e"], s + 1)
                chv.done(dve.tensor_reduce(mx2[:, s], sc2[:, s].rearrange("p q k h -> p q h k"), AX.X, ALU.add))
                chv.wait()
                chv.done(dve.reciprocal(mx2[:, s], mx2[:, s]))
                chv.wait()
                dve.tensor_tensor(sc2[:, s], sc2[:, s], mx2[:, s][:, :, None].to_broadcast([P, B, B, H]), ALU.mult).then_inc(m2["pn"], 1)
                dve.wait_ge(m2["pn"], s + 1)

            def add(s):
                dve.wait_ge(m2["op"], s + 1)
                dve.wait_ge(m2["tbo"], s + 1)
                ts = t[:, s]
                dve.tensor_tensor(ts, ts, ps[:, FB2[s]:FB2[s] + 2, :].rearrange("p a (b c) -> p (a b) c", c=P), ALU.add).then_inc(m2["done"], 1)

            for s in range(S):
                ln_moments(dve, chv, [s])
                ln_variance(dve, chv, s)
            for s in range(S):
                ln_apply(dve, 0, s)
            projected(0, 0)
            projected(0, 1)
            dve.wait_ge(m2["qkv"], 2)
            rounds2(0, 0, multiplied, over_width)
            centre(0)
            projected(1, 0)
            projected(1, 1)
            normalise(0)
            rounds2(0, 1, weighted, over_images)
            rounds2(1, 0, multiplied, over_width)
            centre(1)
            add(0)
            normalise(1)
            rounds2(1, 1, weighted, over_images)
            dve.wait_ge(m2["done"], 1)
            ln_moments(dve, chv, [0])
            ln_variance(dve, chv, 0)
            ln_apply(dve, 1, 0)
            add(1)

        gs = {n: sem("gate_" + n) for n in "ltp lt xl lgp ep e g gp gT st".split()}

        def gate_feature_major(xT, s):
            return xT[:].rearrange("p (b s n) -> p b s n", b=B, s=S)[:, :, s, :]

        def experts(layer, w_in, n_up, hid, gate_w, gate_b):
            hc = hid // P
            wcols = (n_up + 1) * hid
            n_bias = hc + 1 if layer == 0 else 0
            room.close()
            R = S * B
            lg = own(f"lg_{layer}", [P, R, E])
            pg = own(f"pg_{layer}", [P, R, E])
            gmx = own(f"gmx_{layer}", [P, R])
            cmp = own(f"cmp_{layer}", [P, R, E, E])
            gT = own(f"gT_{layer}", [E, S, BLK])
            wraw = own(f"wraw_{layer}", [P, 2, wcols + n_bias])
            wH = own(f"wH_{layer}", [P, 2, wcols], F32R)
            wL = own(f"wL_{layer}", [P, 2, wcols], F32R)
            bias = own(f"bias_{layer}", [P, 2, hc + 1])
            G = own(f"G_{layer}", [P, 2, T])
            hraw = own(f"hraw_{layer}", [P, 2, hc, CH])
            hH = own(f"hH_{layer}", [P, 2, hc, CH], F32R)
            hL = own(f"hL_{layer}", [P, 2, hc, CH], F32R)
            yg = own(f"yg_{layer}", [P, 2, CH])

            def rounds(engine):
                for k in range(2 * NCH):
                    yield 0, k, False
                with engine.Fori(1, E // 2 - 1) as j:
                    for k in range(2 * NCH):
                        yield j, k, False
                for k in range(2 * NCH):
                    yield E // 2 - 1, k, True

            z = {n: sem(f"ex{layer}_" + n) for n in "split wH hp act hm hH hl yp yg acc".split()}
            zw = [[sem(f"ex{layer}_{n}{p}") for n in ("w", "ga", "gb")] for p in range(2)]
            fin = {n: sem(f"fin{layer}_" + n) for n in "tp done st".split()}
            nn = 1 + 2 * layer
            blk = room.enter_context(nc.Block())

            @blk.sync
            def _(sp):
                def weights(j, p):
                    sp.wait_ge(z["split"], 2 * j + p + 1)
                    sp.dma_start(wraw[:, p, :], w_in[bass.ds(2 * j + p, 1)].rearrange("e p n -> p (e n)")).then_inc(zw[p][0], 16)

                def gates(j, p):
                    e = 2 * j + p
                    sp.wait_ge(z["yg"], NCH * e + 1)
                    for a_half in range(2):
                        c = slice(a_half * T // 2, (a_half + 1) * T // 2)
                        sp.dma_start(G[:, p, c], gd[layer][bass.ds(e, 1), c].to_broadcast([P, T // 2])).then_inc(zw[p][1 + a_half], 16)

                weights(0, 0)
                weights(0, 1)
                for s in range(S):
                    sp.wait_ge(gs["gT"], S * layer + s + 1)
                    sp.dma_start(gd[layer].rearrange("e (b s n) -> e b s n", b=B, s=S)[:, :, s, :],
                                 gT[:, s, :].rearrange("e (b n) -> e b n", b=B)).then_inc(gs["st"], 16)
                sp.wait_ge(gs["st"], 16 * S * (layer + 1))
                gates(0, 0)
                gates(0, 1)
                with sp.Fori(1, E // 2) as j:
                    for p in range(2):
                        weights(j, p)
                        gates(j, p)
                if layer == 1:
                    for c in range(NCH):
                        sp.wait_ge(z["acc"], (E - 1) * NCH + c + 1 + FREE_ACC)
                        sp.dma_start(out.rearrange("b c n -> c b n")[:, 2 * c:2 * c + 2, :],
                                     acc[:, c * CH:(c + 1) * CH].rearrange("c (b n) -> c b n", b=2)).then_inc(fin["st"], 16)
                    sp.wait_ge(fin["st"], 16 * NCH)

            @blk.gpsimd
            def _(pool):
                pool.sem_inc(z["split"], FREE_W)
                chp.engine = pool
                chp.done(pool.memset(cmp[:], 0.0))
                for s in range(S):
                    if layer == 1 or s == 1:
                        ln_pool(pool, nn, s)
                pool.sem_inc(z["acc"], FREE_ACC)

                def lower(j, p):
                    pool.wait_ge(z["wH"], 2 * j + p + 1)
                    pool.tensor_tensor(wL[:, p, 0:wcols], wraw[:, p, 0:wcols], wH[:, p, 0:wcols].bitcast(F32), ALU.subtract).then_inc(z["split"], 1)

                lower(0, 0)
                if layer == 1:
                    pool.wait_ge(fin["done"], NCH)
                for j, k, last in rounds(pool):
                    if k == 1:
                        lower(j, 1)
                    if k == NCH + 1 and not last:
                        lower(j + 1, 0)
                    c = k % NCH
                    pool.wait_ge(z["yg"], 2 * NCH * j + k + 1 + FREE_Y)
                    pool.tensor_tensor(acc[:, c * CH:(c + 1) * CH], acc[:, c * CH:(c + 1) * CH], yg[:, k % 2, :], ALU.add).then_inc(z["acc"], 1)

            @blk.scalar
            def _(act):
                act.preload_act_table(ACT.Exp)
                if layer == 1:
                    for c in range(NCH):
                        act.wait_ge(fin["tp"], c + 1)
                        act.activation(acc[:, c * CH:(c + 1) * CH], ps[:, 4 + c, :], ACT.Copy).then_inc(fin["done"], 1)
                for s in range(S):
                    act.wait_ge(gs["ltp"], S * layer + s + 1)
                    act.activation(lnT[:, s, :], flat(ps[:, 2 * s:2 * s + 2, :]), ACT.Copy).then_inc(gs["lt"], 1)
                act.wait_ge(gs["ep"], layer + 1)
                act.activation(pg[:], lg[:], ACT.Exp).then_inc(gs["e"], 1)
                act.preload_act_table(ACT.Gelu if layer == 0 else ACT.Silu)
                for j, k, last in rounds(act):
                    item = 2 * NCH * j + k
                    act.wait_ge(z["hl"], 2 * (item - 1) + FREE_H)
                    for h in range(hc):
                        act.wait_ge(z["hp"], item * hc + h + 1)
                        if layer == 0:
                            act.activation(hraw[:, k % 2, h, :], ps[:, h, :], ACT.Gelu,
                                           bias=bias[:, k // NCH, h:h + 1]).then_inc(z["act"], 1)
                        else:
                            act.activation(hraw[:, k % 2, h, :], ps[:, 2 * h, :], ACT.Silu).then_inc(z["act"], 1)
                    if layer == 1:
                        act.wait_ge(z["yp"], item - 1 + FREE_Y)
                        for h in range(hc):
                            act.wait_ge(z["hm"], item * hc + h + 1)
                            act.activation(hH[:, k % 2, h, :], hraw[:, k % 2, h, :], ACT.Copy).then_inc(z["hH"], 1)
                    if isinstance(j, int) and item == 0:
                        for s in range(S):
                            act.wait_ge(gs["gp"], S * layer + s + 1)
                            act.activation(gT[:, s, :].rearrange("p (a b) -> p a b", a=2), ps[0:E, 4 + 2 * s:6 + 2 * s, :], ACT.Copy).then_inc(gs["gT"], 1)

            @blk.tensor
            def _(pe):
                if layer == 1:
                    for c in range(NCH):
                        for i in range(4):
                            x = pe.transpose(ps[:, 4 + c, i * P:(i + 1) * P], t[:, i % 2, 2 * c + i // 2, :], ident)
                        x.then_inc(fin["tp"], 1)
                LGB = 6
                for s in range(S):
                    ln_transposes(pe, nn, gs["ltp"], s)
                    if layer == 1 and s == 0:
                        pe.wait_ge(fin["done"], NCH)
                    if layer == 0 or s == 1:
                        for g in ((s,) if layer == 0 else range(S)):
                            pe.wait_ge(gs["lt"], S * layer + g + 1)
                            for b in range(B):
                                r = g * B + b
                                x = pe.matmul(ps[:, LGB, r * E:(r + 1) * E], lnT[:, g, b * P:(b + 1) * P], wc(gate_w), start=True, stop=True)
                x.then_inc(gs["lgp"], 1)

                def gates_transposed():
                    pe.wait_ge(gs["g"], layer + 1)
                    for s in range(S):
                        for b in range(B):
                            x = pe.transpose(ps[0:E, 4 + 2 * s + b // 4, (b % 4) * P:(b % 4 + 1) * P], lg[:, s * B + b, :], ident)
                        x.then_inc(gs["gp"], 1)

                pe.wait_ge(gs["xl"], S * (layer + 1))
                pe.sem_inc(z["yp"], FREE_Y)

                def up(j, k):
                    item, p = 2 * NCH * j + k, k // NCH % 2
                    xa, xb = xH[:, (k % NCH) * CH:(k % NCH + 1) * CH], xL[:, (k % NCH) * CH:(k % NCH + 1) * CH]
                    if k % NCH == 0:
                        pe.wait_ge(z["split"], 2 * j + k // NCH + 1 + FREE_W)
                    for h in range(hc):
                        if not (isinstance(item, int) and item == 0):
                            pe.wait_ge(z["act"] if layer == 0 else z["hm"], (item - 1) * hc + h + 1)
                        for u in range(n_up):
                            at = u * hid + h * P
                            o = ps[:, n_up * h + u, :]
                            pe.matmul(o, wH[:, p, at:at + P], xa, start=True, stop=False)
                            pe.matmul(o, wH[:, p, at:at + P], xb, start=False, stop=False)
                            x = pe.matmul(o, wL[:, p, at:at + P], xa, start=False, stop=True)
                        x.then_inc(z["hp"], 1)

                def down(j, k):
                    item, p = 2 * NCH * j + k, k // NCH
                    if isinstance(j, int) and item == 0:
                        pe.wait_ge(gs["gT"], S * (layer + 1))
                    pe.wait_ge(z["yg"], item - 1 + FREE_Y)
                    pe.wait_ge(z["hl"], 2 * (item + 1) + FREE_H)
                    for h in range(hc):
                        at = n_up * hid + h * P
                        o = ps[:, 4 + k % 2, :]
                        pe.matmul(o, wH[:, p, at:at + P], hH[:, k % 2, h, :], start=h == 0, stop=False)
                        pe.matmul(o, wH[:, p, at:at + P], hL[:, k % 2, h, :], start=False, stop=False)
                        x = pe.matmul(o, wL[:, p, at:at + P], hH[:, k % 2, h, :], start=False, stop=h == hc - 1)
                    x.then_inc(z["yp"], 1)

                def sums_transposed(c):
                    pe.wait_ge(z["acc"], (E - 1) * NCH + c + 1 + FREE_ACC)
                    if c >= 2:
                        pe.wait_ge(fin["done"], c - 1)
                    for i in range(4):
                        x = pe.transpose(ps[:, 6 + c % 2, i * P:(i + 1) * P], acc[:, c * CH + i * P:c * CH + (i + 1) * P], ident)
                    x.then_inc(fin["tp"], 1)

                up(0, 0)
                gates_transposed()
                for j, k, last in rounds(pe):
                    if not (last and k == 2 * NCH - 1):
                        up(j, k + 1)
                    down(j, k)
                    if layer == 0 and last and k >= NCH + 2:
                        sums_transposed(k - NCH - 2)
                if layer == 0:
                    sums_transposed(NCH - 2)
                    sums_transposed(NCH - 1)

            @blk.vector
            def _(dve):
                chv.engine = dve
                half = hc // 2

                def upper(j, p):
                    dve.wait_ge(zw[p][0], 16 * (j + 1))
                    if not isinstance(j, int) or j > 0:
                        dve.wait_ge(z["yp"], NCH * (2 * j + p - 1) + FREE_Y)
                    if layer == 0:
                        dve.tensor_copy(bias[:, p, :], wraw[:, p, wcols:])
                    dve.tensor_copy(wH[:, p, 0:wcols], wraw[:, p, 0:wcols]).then_inc(z["wH"], 1)

                dve.sem_inc(z["hl"], FREE_H)
                dve.sem_inc(z["yg"], FREE_Y)
                halves = (0, 1) if layer == 1 else (1,)
                for s in halves:
                    ln_moments(dve, chv, [s])
                    ln_variance(dve, chv, s)
                for s in halves:
                    ln_apply(dve, nn, s)
                upper(0, 0)
                for s in range(S):
                    dve.wait_ge(gs["lt"], S * layer + s + 1)
                    lnv = lnT[:, s, :].rearrange("p (b n) -> p b n", b=B)
                    chv.done(dve.tensor_copy(gate_feature_major(xH, s), lnv))
                    chv.wait()
                    dve.tensor_tensor(gate_feature_major(xL, s), lnv, gate_feature_major(xH, s).bitcast(F32), ALU.subtract).then_inc(gs["xl"], 1)
                dve.wait_ge(gs["lgp"], layer + 1)
                lgb = ps[:, 6, 0:R * E].rearrange("p (r e) -> p r e", r=R)
                if gate_b is None:
                    chv.done(dve.tensor_copy(lg[:], lgb))
                else:
                    chv.done(dve.tensor_tensor(lg[:], lgb, wc(gate_b)[:, None].to_broadcast([P, R, E]), ALU.add))
                chv.wait()
                chv.done(dve.tensor_reduce(gmx[:], lg[:], AX.X, ALU.max))
                chv.wait()
                dve.tensor_tensor(lg[:], lg[:], gmx[:, :, None].to_broadcast([P, R, E]), ALU.subtract).then_inc(gs["ep"], 1)
                dve.wait_ge(gs["e"], layer + 1)
                chv.done(dve.tensor_reduce(gmx[:], pg[:], AX.X, ALU.add))
                chv.wait()
                chv.done(dve.reciprocal(gmx[:], gmx[:]))
                chv.wait()
                chv.done(dve.tensor_tensor(pg[:], pg[:], gmx[:, :, None].to_broadcast([P, R, E]), ALU.mult))
                chv.wait()
                for i in range(E):
                    def expert_i(n):
                        return pg[:, :, i:i + 1].to_broadcast([P, R, n])
                    if i > 0:
                        k = dve.tensor_tensor(cmp[:, :, i, 0:i], pg[:, :, 0:i], expert_i(i), ALU.is_ge)
                    if i + 1 < E:
                        k = dve.tensor_tensor(cmp[:, :, i, i + 1:E], pg[:, :, i + 1:E], expert_i(E - 1 - i), ALU.is_gt)
                chv.done(k)
                chv.wait()
                chv.done(dve.tensor_reduce(lg[:], cmp[:], AX.X, ALU.add))
                chv.wait()
                k = dve.scalar_tensor_tensor(lg[:], lg[:], TOPK - 0.5, pg[:], ALU.is_lt, ALU.mult)
                if layer == 0:
                    k.then_inc(gs["g"], 1)
                else:
                    chv.done(k)
                    chv.wait()
                    chv.done(dve.tensor_reduce(gmx[:], lg[:], AX.X, ALU.add))
                    chv.wait()
                    chv.done(dve.reciprocal(gmx[:], gmx[:]))
                    chv.wait()
                    dve.tensor_tensor(lg[:], lg[:], gmx[:, :, None].to_broadcast([P, R, E]), ALU.mult).then_inc(gs["g"], 1)

                def add_sums(c):
                    dve.wait_ge(fin["tp"], c + 1)
                    tc = t[:, :, 2 * c:2 * c + 2, :].rearrange("p s b c -> p b s c")
                    dve.tensor_tensor(tc, tc, ps[:, 6 + c % 2, :].rearrange("p (b s c) -> p b s c", b=2, s=2), ALU.add).then_inc(fin["done"], 1)

                def moments_of_sums(c):
                    dve.wait_ge(fin["done"], c + 1)
                    ln_moments(dve, chv, range(S), (2 * c, 2 * c + 1))

                def gated(j, k):
                    item, p, c = 2 * NCH * j + k, k // NCH, k % NCH
                    dve.wait_ge(z["yp"], item + 1 + FREE_Y)
                    if c % 2 == 0:
                        dve.wait_ge(zw[p][1 + c // 2], 16 * (j + 1))
                    dve.wait_ge(z["acc"], item - 1 + FREE_ACC)
                    gsl = G[:, p, c * CH:(c + 1) * CH]
                    if layer == 0:
                        dve.scalar_tensor_tensor(yg[:, k % 2, :], ps[:, 4 + k % 2, :], bias[:, p, hc:hc + 1],
                                                 gsl, ALU.add, ALU.mult).then_inc(z["yg"], 1)
                    else:
                        dve.tensor_tensor(yg[:, k % 2, :], ps[:, 4 + k % 2, :], gsl, ALU.mult).then_inc(z["yg"], 1)

                def gated_before(j, k):
                    if k > 0:
                        gated(j, k - 1)
                    elif not (isinstance(j, int) and j == 0):
                        gated(j - 1, 2 * NCH - 1)

                for j, k, last in rounds(dve):
                    item = 2 * NCH * j + k
                    if layer == 1:
                        for h in range(hc):
                            dve.wait_ge(z["act"], item * hc + h + 1)
                            dve.tensor_tensor(hraw[:, k % 2, h, :], hraw[:, k % 2, h, :], ps[:, 2 * h + 1, :], ALU.mult).then_inc(z["hm"], 1)
                    if layer == 1:
                        gated_before(j, k)
                    for g in range(2):
                        src, hi = hraw[:, k % 2, g * half:(g + 1) * half, :], hH[:, k % 2, g * half:(g + 1) * half, :]
                        if layer == 0:
                            dve.wait_ge(z["act"], item * hc + (g + 1) * half)
                            if g == 0:
                                dve.wait_ge(z["yp"], item - 1 + FREE_Y)
                            dve.tensor_copy(hi, src).then_inc(z["hH"], 1)
                        dve.wait_ge(z["hH"], 2 * item + g + 1)
                        dve.tensor_tensor(hL[:, k % 2, g * half:(g + 1) * half, :], src, hi.bitcast(F32), ALU.subtract).then_inc(z["hl"], 1)
                    if layer == 0:
                        gated_before(j, k)
                    if k == 1:
                        upper(j, 1)
                    if k == NCH + 1 and not last:
                        upper(j + 1, 0)
                    if layer == 0 and last and k == 2 * NCH - 1:
                        add_sums(0)
                        moments_of_sums(0)
                gated(E // 2 - 1, 2 * NCH - 1)
                if layer == 0:
                    for c in range(1, NCH):
                        add_sums(c)
                        moments_of_sums(c)
                    for s in range(S):
                        ln_variance(dve, chv, s)

        experts(0, a["ex2"], 1, F2, "gate2", "gateb2")

        room.close()
        wq3H, wq3L = own("wq3H", [P, 2 * P], F32R), own("wq3L", [P, 2 * P], F32R)
        wk3H, wk3L = own("wk3H", [P, 2 * P], F32R), own("wk3L", [P, 2 * P], F32R)
        wv3H, wv3L = own("wv3H", [P, P], F32R), own("wv3L", [P, P], F32R)
        wo3 = own("wo3", [P, 3, P], BF16)
        wtmp = own("wtmp", [P, P])
        q3H, q3L = own("q3H", [P, 2, N], F32R), own("q3L", [P, 2, N], F32R)
        k3H, k3S = own("k3H", [P, 2, N], F32R), own("k3S", [P, 2, N], F32R)
        v3r = own("v3r", [P, 2, S, P])
        vp3 = own("vp3", [P, B, S, H, 3, DH], BF16)
        mx3 = own("mx3", [P, H // 2, 2 * S])
        sm3 = own("sm3", [P, H // 2, 2 * S])
        smb3 = own("smb3", [P, H // 2, 2 * S], BF16)
        s3 = own("s3", [P, 2, 2 * S, N], BF16)
        p3 = own("p3", [P, 2, 2 * S, N], BF16)
        pT3 = own("pT3", [P, 2, 2, S, N], BF16)
        o3b = own("o3b", [P, S, P], BF16)
        oT3 = own("oT3", [P, N], BF16)
        m3 = {n: sem("at3_" + n) for n in
              "wh wl wr wo ltp lt xl vp vb vr v2 v prj pru prl sp sb sub ex p tp pt op o otp ot fp done tbo".split()}
        block4 = room.enter_context(nc.Block())
        QKB, TB, SB, OB = 0, 1, 2, 6

        def images(engine, step, around=None):
            for g in range(4):
                step(0, g, True)
            with engine.Fori(1, B - 2) as b:
                if around:
                    around(b)
                for g in range(4):
                    step(b, g, False)
            if around:
                around(None)
            for b in (B - 2, B - 1):
                for g in range(4):
                    step(b, g, False)

        def there(b, g):
            return not isinstance(b, int) or b < B

        def fragment(b, g, n):
            return b + (g + n) // 4, (g + n) % 4 // 2, (g + n) % 2

        def ahead(b, g, n):
            return (b, g + n) if g + n < 4 else (b + 1, g + n - 4)

        def by_head(x):
            return x.rearrange("p s (h d) -> p s h d", h=H)

        @block4.gpsimd
        def _(pool):
            for s in range(S):
                ln_pool(pool, 2, s)
            for i, (name, wh, wl) in enumerate((("Wq3", wq3H, wq3L), ("Wk3", wk3H, wk3L), ("Wv3", wv3H, wv3L))):
                pool.wait_ge(m3["wh"], i + 1)
                pool.tensor_tensor(wl[:], wc(name), wh[:].bitcast(F32), ALU.subtract).then_inc(m3["wl"], 1)
            pool.wait_ge(m3["wh"], 4)
            pool.tensor_tensor(wtmp[:], wc("Wo3"), wo3[:, 0], ALU.subtract).then_inc(m3["wr"], 1)
            pool.wait_ge(m3["wr"], 1)
            pool.wait_ge(m3["wh"], 5)
            pool.tensor_tensor(wo3[:, 2], wtmp[:], wo3[:, 1], ALU.subtract).then_inc(m3["wo"], 1)
            add_bias(pool, 2, "bo3", m3["tbo"])
            for b in range(B):
                pool.wait_ge(m3["v2"], b + 1)
                pool.tensor_tensor(vp3[:, b, :, :, 2, :], by_head(v3r[:, b % 2]), vp3[:, b, :, :, 1, :], ALU.subtract).then_inc(m3["v"], 1)

        @block4.scalar
        def _(act):
            act.preload_act_table(ACT.Exp)
            for name, wh in (("Wq3", wq3H[:]), ("Wk3", wk3H[:]), ("Wv3", wv3H[:]), ("Wo3", wo3[:, 0])):
                act.activation(wh, wc(name), ACT.Copy).then_inc(m3["wh"], 1)
            ln_copies(act, 2, m3["ltp"], m3["lt"])
            act.wait_ge(m3["wr"], 1)
            act.activation(wo3[:, 1], wtmp[:], ACT.Copy).then_inc(m3["wh"], 1)

            def upper(b, g, part, bank=QKB):
                act.wait_ge(m3["prj"], 4 * b + 2 * g + part + 1)
                dst, scale = ((q3H, DH ** -0.5), (k3H, 1.0))[part]
                act.activation(dst[:, g, :], ps[:, bank, part * N:(part + 1) * N], ACT.Copy, scale=scale).then_inc(m3["pru"], 1)

            def rounded(b, g):
                i = 4 * b + g
                act.wait_ge(m3["sp"], i + 1)
                if not (isinstance(b, int) and i < 2):
                    act.wait_ge(m3["ex"], 4 * (i - 1))
                act.activation(s3[:, g % 2], ps[:, SB + 2 * (g % 2):SB + 2 * (g % 2) + 2, :].rearrange("p a (s n) -> p (a s) n", s=2), ACT.Copy).then_inc(m3["sb"], 1)

            def exponentials(b, g):
                i = 4 * b + g
                act.wait_ge(m3["sub"], 4 * i + 4)
                if not (isinstance(b, int) and i < 2):
                    act.wait_ge(m3["tp"], i - 1)
                for r in range(4):
                    act.activation(p3[:, g % 2, r, :], s3[:, g % 2, r, :], ACT.Exp, accum_out=sm3[:, g, r:r + 1]).then_inc(m3["ex"], 1)

            def evacuate(b, g):
                i = 4 * b + g
                act.wait_ge(m3["tp"], i + 1)
                if not (isinstance(b, int) and i < 2):
                    act.wait_ge(m3["op"], i - 1)
                act.activation(pT3[:, g % 2].rearrange("p h k n -> p (h k n)"), psb(TB), ACT.Copy).then_inc(m3["pt"], 1)

            for n in range(4):
                upper(*fragment(0, 0, n), bank=n)
            for b in range(B):
                act.wait_ge(m3["vp"], b + 1)
                act.activation(vp3[:, b, :, :, 0, :], by_head(ps[:, 4 + b % 4, 0:N].rearrange("p (s c) -> p s c", s=S)),
                               ACT.Copy).then_inc(m3["vb"], 1)
            rounded(0, 0)
            rounded(0, 1)
            upper(*fragment(0, 0, 4))
            exponentials(0, 0)

            def step(b, g, first):
                if there(*ahead(b, g, 2)):
                    rounded(*ahead(b, g, 2))
                if not (first and g == 0):
                    evacuate(*((b, g - 1) if g else (b - 1, 3)))
                if there(*fragment(b, g, 5)[:2]):
                    upper(*fragment(b, g, 5))
                if there(*ahead(b, g, 1)):
                    exponentials(*ahead(b, g, 1))
            images(act, step)
            evacuate(B - 1, 3)

        @block4.tensor
        def _(pe):
            for s in range(S):
                ln_transposes(pe, 2, m3["ltp"], s)
            pe.wait_ge(m3["wl"], 3)
            pe.wait_ge(m3["wo"], 1)
            pe.wait_ge(m3["xl"], S)

            def project(b, g, part, bank=QKB):
                n = 4 * b + 2 * g + part
                if not (isinstance(b, int) and n < 4):
                    pe.wait_ge(m3["prl"], n)
                xa, xb = xH[:, bass.ds(b * N, N)], xL[:, bass.ds(b * N, N)]
                wh, wl = ((wq3H, wq3L), (wk3H, wk3L))[part]
                o, c = ps[:, bank, part * N:(part + 1) * N], slice(g * P, (g + 1) * P)
                pe.matmul(o, wh[:, c], xa, start=True, stop=False)
                pe.matmul(o, wh[:, c], xb, start=False, stop=False)
                pe.matmul(o, wl[:, c], xa, start=False, stop=True).then_inc(m3["prj"], 1)

            def scores(b, g):
                i = 4 * b + g
                if g % 2 == 0:
                    pe.wait_ge(m3["prl"], 4 * b + g + 2)
                if not (isinstance(b, int) and i < 2):
                    pe.wait_ge(m3["sb"], i - 1)
                for h in (2 * g, 2 * g + 1):
                    r, q = 32 * (h % 4), h // 4
                    for s in range(S):
                        o = ps[:, SB + 2 * (g % 2) + h % 2, s * N:(s + 1) * N]
                        pe.matmul(o, q3H[r:r + 32, q, s * P:(s + 1) * P], k3S[r:r + 32, q, :], start=True, stop=False)
                        x = pe.matmul(o, q3L[r:r + 32, q, s * P:(s + 1) * P], k3S[r:r + 32, q, :], start=False, stop=True)
                x.then_inc(m3["sp"], 1)

            def transposed(b, g):
                i = 4 * b + g
                pe.wait_ge(m3["p"], 4 * i + 4)
                if not (isinstance(b, int) and i == 0):
                    pe.wait_ge(m3["pt"], i)
                if g in (1, 2) and not (isinstance(b, int) and b == 0):
                    pe.wait_ge(m3["ot" if g == 1 else "done"], b)
                for h in range(2):
                    for kt in range(S):
                        for s in range(S):
                            x = pe.transpose(psb(TB)[:, ((h * S + kt) * S + s) * P:((h * S + kt) * S + s + 1) * P],
                                             p3[:, g % 2, h * S + s, kt * P:(kt + 1) * P], identb[:])
                x.then_inc(m3["tp"], 1)

            def values(b, g):
                i = 4 * b + g
                pe.wait_ge(m3["pt"], i + 1)
                if g == 0 and not (isinstance(b, int) and b == 0):
                    pe.wait_ge(m3["o"], b)
                for h in (2 * g, 2 * g + 1):
                    for s in range(S):
                        for kt in range(S):
                            v = vp3[:, bass.ds(b, 1), kt, h].rearrange("p b a d -> p (b a d)")
                            x = pe.matmul(ps[:, OB + s, h * 48:(h + 1) * 48], pT3[:, g % 2, h % 2, kt, s * P:(s + 1) * P], v,
                                          start=kt == 0, stop=kt == 1)
                x.then_inc(m3["op"], 1)

            def out_transposed(b):
                pe.wait_ge(m3["o"], b + 1)
                for s in range(S):
                    x = pe.transpose(psb(TB)[:, s * P:(s + 1) * P], o3b[:, s, :], identb[:])
                x.then_inc(m3["otp"], 1)

            def final(b):
                pe.wait_ge(m3["ot"], b + 1)
                for s in range(S):
                    for i in range(3):
                        x = pe.matmul(ps[:, TB, s * P:(s + 1) * P], oT3[:, s * P:(s + 1) * P], wo3[:, i, :], start=i == 0, stop=i == 2)
                x.then_inc(m3["fp"], 1)

            for n in range(4):
                project(*fragment(0, 0, n), bank=n)
            for b in range(B):
                if b >= 4:
                    pe.wait_ge(m3["vr"], b - 3)
                for s in range(S):
                    o, c = ps[:, 4 + b % 4, s * P:(s + 1) * P], slice(b * N + s * P, b * N + (s + 1) * P)
                    pe.matmul(o, xH[:, c], wv3H[:], start=True, stop=False)
                    pe.matmul(o, xL[:, c], wv3H[:], start=False, stop=False)
                    x = pe.matmul(o, xH[:, c], wv3L[:], start=False, stop=True)
                x.then_inc(m3["vp"], 1)
            pe.wait_ge(m3["prl"], 4)
            scores(0, 0)
            pe.wait_ge(m3["vr"], B)
            scores(0, 1)
            project(*fragment(0, 0, 4))
            scores(0, 2)
            project(*fragment(0, 0, 5))
            pe.wait_ge(m3["v"], B)

            def step(b, g, first):
                if there(*ahead(b, g, 3)):
                    scores(*ahead(b, g, 3))
                if not (first and g == 0):
                    values(*((b, g - 1) if g else (b - 1, 3)))
                if g == 1 and not first:
                    out_transposed(b - 1)
                if g == 2 and not first:
                    final(b - 1)
                transposed(b, g)
                if there(*fragment(b, g, 6)[:2]):
                    project(*fragment(b, g, 6))
            images(pe, step)
            values(B - 1, 3)
            out_transposed(B - 1)
            final(B - 1)

        @block4.vector
        def _(dve):
            chv.engine = dve
            for s in range(S):
                ln_apply(dve, 2, s)
            for s in range(S):
                dve.wait_ge(m3["lt"], s + 1)
                lnv = lnT[:, s, :].rearrange("p (b n) -> p b n", b=B)
                chv.done(dve.tensor_copy(gate_feature_major(xH, s), lnv))
                chv.wait()
                dve.tensor_tensor(gate_feature_major(xL, s), lnv, gate_feature_major(xH, s).bitcast(F32), ALU.subtract).then_inc(m3["xl"], 1)

            def lower(b, g, part, bank=QKB):
                dve.wait_ge(m3["pru"], 4 * b + 2 * g + part + 1)
                src = ps[:, bank, part * N:(part + 1) * N]
                if part == 0:
                    x = dve.scalar_tensor_tensor(q3L[:, g, :], src, DH ** -0.5, q3H[:, g, :].bitcast(F32), ALU.mult, ALU.subtract)
                else:
                    x = dve.scalar_tensor_tensor(k3S[:, g, :], k3H[:, g, :].bitcast(F32), wc("kmask"), src, ALU.mult, ALU.add)
                x.then_inc(m3["prl"], 1)

            def centre(b, g):
                dve.wait_ge(m3["sb"], 4 * b + g + 1)
                chv.done(dve.tensor_reduce(mx3[:, g, :], s3[:, g % 2], AX.X, ALU.max))
                chv.wait()
                for r in range(4):
                    dve.tensor_scalar(s3[:, g % 2, r, :], s3[:, g % 2, r, :], mx3[:, g, r:r + 1], None, ALU.subtract).then_inc(m3["sub"], 1)

            def normalise(b, g):
                dve.wait_ge(m3["ex"], 4 * (4 * b + g) + 4)
                chv.done(dve.tensor_copy(smb3[:, g, :], sm3[:, g, :]))
                chv.wait()
                chv.done(dve.reciprocal(sm3[:, g, :], smb3[:, g, :]))
                chv.wait()
                for r in range(4):
                    dve.tensor_scalar(p3[:, g % 2, r, :], p3[:, g % 2, r, :], sm3[:, g, r:r + 1], None, ALU.mult).then_inc(m3["p"], 1)

            def gather(b):
                dve.wait_ge(m3["op"], 4 * b + 4)
                if not isinstance(b, int) or b > 0:
                    dve.wait_ge(m3["otp"], b)
                with nc.allow_low_precision(reason="the reference's output here is bfloat16; the sum itself is float32"):
                    dve.tensor_reduce(by_head(o3b[:]), ps[:, OB:OB + 2, 0:384].rearrange("p s (h a d) -> p s h d a", h=H, a=3),
                                      AX.X, ALU.add).then_inc(m3["o"], 1)

            def copy_out(b):
                dve.wait_ge(m3["otp"], b + 1)
                if not isinstance(b, int) or b > 0:
                    dve.wait_ge(m3["fp"], b)
                dve.tensor_copy(oT3[:], psb(TB)[:, 0:N]).then_inc(m3["ot"], 1)

            def add(b):
                dve.wait_ge(m3["fp"], b + 1)
                tb = t[:, :, bass.ds(b, 1), :].rearrange("p s b c -> p s (b c)")
                dve.tensor_tensor(tb, tb, ps[:, TB, 0:N].rearrange("p (s c) -> p s c", s=S), ALU.add).then_inc(m3["done"], 1)

            def split_values(b):
                dve.wait_ge(m3["vb"], b + 1)
                if b >= 2:
                    dve.wait_ge(m3["v"], b - 1)
                dve.tensor_tensor(by_head(v3r[:, b % 2]), by_head(ps[:, 4 + b % 4, 0:N].rearrange("p (s c) -> p s c", s=S)),
                                  vp3[:, b, :, :, 0, :], ALU.subtract).then_inc(m3["vr"], 1)
                dve.wait_ge(m3["vr"], b + 1)
                dve.tensor_copy(vp3[:, b, :, :, 1, :], by_head(v3r[:, b % 2])).then_inc(m3["v2"], 1)

            for n in range(4):
                lower(*fragment(0, 0, n), bank=n)
            for b in range(B):
                split_values(b)
            centre(0, 0)
            lower(*fragment(0, 0, 4))

            def step(b, g, first):
                if there(*ahead(b, g, 1)):
                    centre(*ahead(b, g, 1))
                normalise(b, g)
                if there(*fragment(b, g, 5)[:2]):
                    lower(*fragment(b, g, 5))
                if g == 0 and not first:
                    gather(b - 1)
                if g == 1 and not first:
                    copy_out(b - 1)
                if g == 2 and not first:
                    add(b - 1)

            def count(b):
                if b is None:
                    chv.end(B - 3)
                else:
                    chv.loop(b - 1, 12)
            dve.wait_ge(m3["tbo"], S)
            images(dve, step, count)
            gather(B - 1)
            copy_out(B - 1)
            add(B - 1)

        experts(1, a["ex3"], 2, F3, "router3", None)
        room.close()


def _layout(inp):
    def rows(v):
        return np.tile(np.asarray(v).reshape(1, -1), (P, 1))

    def col(v):
        v = np.asarray(v).reshape(-1, 1)
        return np.concatenate([v, np.zeros((P - len(v), 1), np.float32)])

    def swap(x):
        y = x.reshape(*x.shape[:-1], -1, 2, DH // 2)[..., ::-1, :]
        return y.reshape(x.shape)

    def slots(x):
        return np.repeat(x.reshape(P, H, 1, DH), 2, axis=2).reshape(P, 2 * H * DH)

    f = (np.arange(B, dtype=np.float64)[:, None] / 10000.0 ** (np.arange(0, DH, 2) / DH)[None, :]).astype(np.float32)
    cos = np.cos(np.concatenate([f, f], 1))
    sin = np.sin(np.concatenate([-f, f], 1))
    wq, wk, wv = (inp[f"L2_attn_W{n}"].T for n in "qkv")
    bq, bk, bv = (inp[f"L2_attn_b{n}"] for n in "qkv")
    parts = {
        "Wq0": inp["L0_conv_Wq"].T, "Wk0": inp["L0_conv_Wk"].T, "Wv0": inp["L0_conv_Wv"], "Wf0": inp["L0_conv_Wf"].T,
        "W1": np.concatenate([inp[f"L1_conv_W{n}"].T for n in "qkvs"], 1), "We1": inp["L1_conv_We"].T,
        "Wqkv2": np.concatenate([wq, wk, wv], 1), "Wqk2r": np.concatenate([swap(wq), swap(wk)], 1),
        "Wo2": inp["L2_attn_Wo"].T, "gate2": inp["L2_ffn_gate_w"],
        "Wq3": slots(inp["L3_attn_Wq"]), "Wk3": slots(inp["L3_attn_Wkv"][:, :P]), "Wv3": inp["L3_attn_Wkv"][:, P:],
        "Wo3": inp["L3_attn_Wo"], "router3": inp["L3_ffn_router_w"], "ident": np.eye(P),
        "bv0": col(inp["L0_conv_bv"]), "bn_w": col(inp["L0_conv_bn_w"]), "bn_b": col(inp["L0_conv_bn_b"]),
        "bn_mean": col(inp["L0_conv_bn_mean"]), "bn_var": col(inp["L0_conv_bn_var"]),
        "bq0": col(inp["L0_conv_bq"]), "bk0": col(inp["L0_conv_bk"]), "be1": col(inp["L1_conv_be"]),
        "gamma": rows(inp["L0_conv_gamma"]),
        "kmask": np.where(np.arange(P) % (2 * DH) < DH, 0.0, -1.0)[:, None],
        "bias1": rows(np.concatenate([inp[f"L1_conv_b{n}"] for n in "qkvs"])),
        "bqkv2": rows(np.concatenate([bq, bk, bv])), "bqk2r": rows(np.concatenate([swap(bq), swap(bk)])),
        "bo2": rows(inp["L2_attn_bo"]), "gateb2": rows(inp["L2_ffn_gate_b"]), "bo3": rows(inp["L3_attn_bo"]),
        "cosq": rows(cos * DH ** -0.5), "sinq": rows(sin * DH ** -0.5), "cosk": rows(cos), "sink": rows(sin),
    }
    pack = np.concatenate([np.asarray(parts[n], np.float32) for n, _ in PACK], 1)

    def down(x, hid):
        return x.reshape(E, hid // P, P, P).transpose(0, 2, 1, 3).reshape(E, P, hid)
    ex2 = np.concatenate([inp["L2_ffn_w1"], down(inp["L2_ffn_w2"], F2), inp["L2_ffn_b1"].reshape(E, F2 // P, P).transpose(0, 2, 1),
                          inp["L2_ffn_b2"][:, :, None]], 2)
    ex3 = np.concatenate([inp["L3_ffn_w1"], inp["L3_ffn_w3"], down(inp["L3_ffn_w2"], F3)], 2)
    return {"pack": pack, "x": inp["x"].reshape(B, P, N), "ex2": ex2, "ex3": ex3}


def kernel(**inputs):
    from concourse import bacc
    from concourse.bass_utils import run_bass_kernel_spmd

    arrays = {k: np.ascontiguousarray(v) for k, v in _layout({k: np.asarray(v) for k, v in inputs.items()}).items()}
    nc = bacc.Bacc("TRN2", target_bir_lowering=False, num_devices=1)
    args = {k: nc.dram_tensor(f"in_{k}", v.shape, mybir.dt.from_np(v.dtype), kind="ExternalInput").ap() for k, v in arrays.items()}
    out = nc.dram_tensor("out", (B, P, N), F32, kind="ExternalOutput").ap()
    build(nc, args, out)
    r = run_bass_kernel_spmd(nc, [{f"in_{k}": v for k, v in arrays.items()}], core_ids=[0])
    return r.results[0]["out"].reshape(B, P, 16, 16)
```
